# Optimizing a Trainium2 kernel written in Bass

```python
import numpy as np
import jax
import jax.numpy as jnp

def _softmax(x, axis=-1):
    return jax.nn.softmax(x, axis=axis)

def _gelu(x):
    return jax.nn.gelu(x, approximate=True)

def _silu(x):
    return jax.nn.silu(x)

def _sigmoid(x):
    return jax.nn.sigmoid(x)

def _layernorm(x, axis=-1, eps=1e-05):
    m = jnp.mean(x, axis=axis, keepdims=True)
    v = jnp.var(x, axis=axis, keepdims=True)
    return (x - m) / jnp.sqrt(v + eps)

def _scatter_add(tgt, idx, src, axis=0):
    return tgt.at[idx].add(src)

def _segment_sum(src, seg, n):
    return jax.ops.segment_sum(src, seg, n)
kernel_name = 'mk_early_fusion_embed_d1_tok_img512_r4_b72857'

def setup_inputs(seed: int=0):
    np.random.seed(seed)
    _w = jnp.asarray

    def _rec_inputs():
        import jax
        import jax.numpy as jnp
        _rk = jax.random.key(seed)
        x = 7.57192e-06 + 1.00007 * jax.random.normal(jax.random.fold_in(_rk, 1), (32, 3, 224, 224), jnp.float32)
        x_txt = jax.random.randint(jax.random.fold_in(_rk, 51), (32, 77), 0, 50, jnp.int32)
        return (x, x_txt)
    x, x_txt = _rec_inputs()

    def _L0_tok_setup():
        import jax, jax.numpy as jnp
        import numpy as np
        DEPTH = 4
        HEADS = 8
        DIM = 128
        HID = 256
        P = 16
        IMG = 224
        GRID = IMG // P
        NPATCH = GRID * GRID
        NTOK = NPATCH + 1
        BATCH = 64
        EPS = 1e-05

        def layernorm(x, w, b):
            mu = jnp.mean(x, axis=-1, keepdims=True)
            var = jnp.mean(jnp.square(x - mu), axis=-1, keepdims=True)
            return (x - mu) * jax.lax.rsqrt(var + EPS) * w + b
        key = jax.random.key(seed)
        ks = jax.random.split(key, 12)
        s = 0.02
        inp = {'x': jax.random.normal(ks[0], (BATCH, 3, IMG, IMG), jnp.float32), 'conv_w': jax.random.normal(ks[1], (3 * P * P, DIM), jnp.float32) * s, 'conv_b': jnp.zeros((DIM,), jnp.float32), 'cls_token': jax.random.normal(ks[2], (1, 1, DIM), jnp.float32) * s, 'pos_embed': jax.random.normal(ks[3], (1, NTOK, DIM), jnp.float32) * s, 'ln1_w': jnp.ones((DEPTH, DIM), jnp.float32), 'ln1_b': jnp.zeros((DEPTH, DIM), jnp.float32), 'qkv_w': jax.random.normal(ks[4], (DEPTH, DIM, 3 * DIM), jnp.float32) * s, 'qkv_b': jnp.zeros((DEPTH, 3 * DIM), jnp.float32), 'proj_w': jax.random.normal(ks[5], (DEPTH, DIM, DIM), jnp.float32) * s, 'proj_b': jnp.zeros((DEPTH, DIM), jnp.float32), 'ln2_w': jnp.ones((DEPTH, DIM), jnp.float32), 'ln2_b': jnp.zeros((DEPTH, DIM), jnp.float32), 'fc1_w': jax.random.normal(ks[6], (DEPTH, DIM, HID), jnp.float32) * s, 'fc1_b': jnp.zeros((DEPTH, HID), jnp.float32), 'fc2_w': jax.random.normal(ks[7], (DEPTH, HID, DIM), jnp.float32) * s, 'fc2_b': jnp.zeros((DEPTH, DIM), jnp.float32), 'norm_w': jnp.ones((DIM,), jnp.float32), 'norm_b': jnp.zeros((DIM,), jnp.float32)}
        return inp
    _L0_tok_all = _L0_tok_setup()
    _L0_tok_in = {k: v for k, v in _L0_tok_all.items() if k in ('conv_w', 'conv_b', 'cls_token', 'pos_embed', 'ln1_w', 'ln1_b', 'qkv_w', 'qkv_b', 'proj_w', 'proj_b', 'ln2_w', 'ln2_b', 'fc1_w', 'fc1_b', 'fc2_w', 'fc2_b', 'norm_w', 'norm_b')}
    del _L0_tok_all

    def _L0_txt_setup():
        import jax, jax.numpy as jnp
        import numpy as np
        D_MODEL = 128
        END_IDX = 2

        def _build_tree(tokens):
            B, T = tokens.shape
            cap = 2 * T + 2
            left2 = jnp.array([1.0, 0.0], jnp.float32)
            right2 = jnp.array([0.0, 1.0], jnp.float32)
            bidx = jnp.arange(B)
            X0 = jnp.zeros((B, T, D_MODEL), jnp.float32)
            par0 = jnp.zeros((B, cap), jnp.int32)
            lr0 = jnp.zeros((B, cap), jnp.int32)
            head0 = jnp.zeros((B,), jnp.int32)
            tail0 = jnp.zeros((B,), jnp.int32)

            def body(carry, t):
                X, par, lr, head, tail = carry
                parent = par[bidx, head]
                plr = lr[bidx, head]
                x_parent = X[bidx, parent]
                lrvec = jnp.where(plr[:, None] == 0, left2, right2)
                x_it = jnp.concatenate([lrvec, x_parent[:, :-2]], axis=1)
                x_it = jnp.where(t == 0, 0.0, x_it)
                X = X.at[bidx, t].set(x_it)
                tok = tokens[bidx, t]
                push = jnp.where(t == 0, True, tok != END_IDX)
                tval = jnp.full((B,), 0, jnp.int32) + jnp.int32(t)
                par = par.at[bidx, tail].set(tval).at[bidx, tail + 1].set(tval)
                lr = lr.at[bidx, tail].set(0).at[bidx, tail + 1].set(1)
                tail = tail + 2 * push.astype(jnp.int32)
                pop = (t > 0) & (tail - head > 1)
                head = head + pop.astype(jnp.int32)
                return ((X, par, lr, head, tail), None)
            (X, _, _, _, _), _ = jax.lax.scan(body, (X0, par0, lr0, head0, tail0), jnp.arange(T))
            return X
        key = jax.random.key(seed)
        tokens = jax.random.randint(key, (64, 256), 0, 50, dtype=jnp.int32)
        p = jnp.ones((1,), dtype=jnp.float32)
        return {'tokens': tokens, 'p': p}
    _L0_txt_all = _L0_txt_setup()
    _L0_txt_in = {k: v for k, v in _L0_txt_all.items() if k in ('p',)}
    del _L0_txt_all

    def _L0_attn_setup():
        import jax, jax.numpy as jnp
        import numpy as np
        B, S, D, DI = (8, 1024, 128, 512)
        EPS = 1e-12

        def _l2norm(x):
            n = jnp.sqrt(jnp.sum(x * x, axis=-1, keepdims=True))
            return x / jnp.maximum(n, EPS)
        key = jax.random.key(seed)
        ks = jax.random.split(key, 10)
        sd = 1.0 / np.sqrt(D)
        si = 1.0 / np.sqrt(DI)
        return {'x': jax.random.normal(ks[0], (B, S, D), jnp.float32), 'wq': jax.random.uniform(ks[1], (D, DI), jnp.float32, -sd, sd), 'wk': jax.random.uniform(ks[2], (D, DI), jnp.float32, -sd, sd), 'wv': jax.random.uniform(ks[3], (D, DI), jnp.float32, -sd, sd), 'wo': jax.random.uniform(ks[4], (DI, D), jnp.float32, -si, si), 'w1': jax.random.uniform(ks[5], (D, DI), jnp.float32, -sd, sd), 'b1': jax.random.uniform(ks[6], (DI,), jnp.float32, -sd, sd), 'w2': jax.random.uniform(ks[7], (DI, D), jnp.float32, -si, si), 'b2': jax.random.uniform(ks[8], (D,), jnp.float32, -si, si)}
    _L0_attn_all = _L0_attn_setup()
    _L0_attn_in = {k: v for k, v in _L0_attn_all.items() if k in ('wq', 'wk', 'wv', 'wo', 'w1', 'b1', 'w2', 'b2')}
    del _L0_attn_all

    def _L0_ffn_setup():
        import jax, jax.numpy as jnp
        import numpy as np
        B, S, H, E, K = (8, 1024, 128, 8, 2)
        key = jax.random.key(seed)
        ks = jax.random.split(key, 7)
        s_h = 1.0 / np.sqrt(H)
        s_2h = 1.0 / np.sqrt(2 * H)
        return {'x': jax.random.normal(ks[0], (B, S, H), dtype=jnp.float32), 'gate_w': jax.random.uniform(ks[1], (H, E), minval=-s_h, maxval=s_h, dtype=jnp.float32), 'gate_b': jax.random.uniform(ks[2], (E,), minval=-s_h, maxval=s_h, dtype=jnp.float32), 'w1': jax.random.uniform(ks[3], (E, H, 2 * H), minval=-s_h, maxval=s_h, dtype=jnp.float32), 'b1': jax.random.uniform(ks[4], (E, 2 * H), minval=-s_h, maxval=s_h, dtype=jnp.float32), 'w2': jax.random.uniform(ks[5], (E, 2 * H, H), minval=-s_2h, maxval=s_2h, dtype=jnp.float32), 'b2': jax.random.uniform(ks[6], (E, H), minval=-s_2h, maxval=s_2h, dtype=jnp.float32)}
    _L0_ffn_all = _L0_ffn_setup()
    _L0_ffn_in = {k: v for k, v in _L0_ffn_all.items() if k in ('gate_w', 'gate_b', 'w1', 'b1', 'w2', 'b2')}
    del _L0_ffn_all
    return {'x': x, 'x_txt': x_txt, 'L0_tok_conv_w': _L0_tok_in['conv_w'], 'L0_tok_conv_b': _L0_tok_in['conv_b'], 'L0_tok_cls_token': _L0_tok_in['cls_token'], 'L0_tok_pos_embed': _L0_tok_in['pos_embed'], 'L0_tok_ln1_w': _L0_tok_in['ln1_w'], 'L0_tok_ln1_b': _L0_tok_in['ln1_b'], 'L0_tok_qkv_w': _L0_tok_in['qkv_w'], 'L0_tok_qkv_b': _L0_tok_in['qkv_b'], 'L0_tok_proj_w': _L0_tok_in['proj_w'], 'L0_tok_proj_b': _L0_tok_in['proj_b'], 'L0_tok_ln2_w': _L0_tok_in['ln2_w'], 'L0_tok_ln2_b': _L0_tok_in['ln2_b'], 'L0_tok_fc1_w': _L0_tok_in['fc1_w'], 'L0_tok_fc1_b': _L0_tok_in['fc1_b'], 'L0_tok_fc2_w': _L0_tok_in['fc2_w'], 'L0_tok_fc2_b': _L0_tok_in['fc2_b'], 'L0_tok_norm_w': _L0_tok_in['norm_w'], 'L0_tok_norm_b': _L0_tok_in['norm_b'], 'L0_txt_p': _L0_txt_in['p'], 'L0_attn_wq': _L0_attn_in['wq'], 'L0_attn_wk': _L0_attn_in['wk'], 'L0_attn_wv': _L0_attn_in['wv'], 'L0_attn_wo': _L0_attn_in['wo'], 'L0_attn_w1': _L0_attn_in['w1'], 'L0_attn_b1': _L0_attn_in['b1'], 'L0_attn_w2': _L0_attn_in['w2'], 'L0_attn_b2': _L0_attn_in['b2'], 'L0_ffn_gate_w': _L0_ffn_in['gate_w'], 'L0_ffn_gate_b': _L0_ffn_in['gate_b'], 'L0_ffn_w1': _L0_ffn_in['w1'], 'L0_ffn_b1': _L0_ffn_in['b1'], 'L0_ffn_w2': _L0_ffn_in['w2'], 'L0_ffn_b2': _L0_ffn_in['b2']}

def reference(x, x_txt, L0_tok_conv_w, L0_tok_conv_b, L0_tok_cls_token, L0_tok_pos_embed, L0_tok_ln1_w, L0_tok_ln1_b, L0_tok_qkv_w, L0_tok_qkv_b, L0_tok_proj_w, L0_tok_proj_b, L0_tok_ln2_w, L0_tok_ln2_b, L0_tok_fc1_w, L0_tok_fc1_b, L0_tok_fc2_w, L0_tok_fc2_b, L0_tok_norm_w, L0_tok_norm_b, L0_txt_p, L0_attn_wq, L0_attn_wk, L0_attn_wv, L0_attn_wo, L0_attn_w1, L0_attn_b1, L0_attn_w2, L0_attn_b2, L0_ffn_gate_w, L0_ffn_gate_b, L0_ffn_w1, L0_ffn_b1, L0_ffn_w2, L0_ffn_b2):
    import jax
    import jax.numpy as jnp

    def _L0_tok_ref(x, conv_w, conv_b, cls_token, pos_embed, ln1_w, ln1_b, qkv_w, qkv_b, proj_w, proj_b, ln2_w, ln2_b, fc1_w, fc1_b, fc2_w, fc2_b, norm_w, norm_b):
        import jax, jax.numpy as jnp
        import numpy as np
        DEPTH = 4
        HEADS = 8
        DIM = 128
        HID = 256
        P = 16
        IMG = 224
        GRID = IMG // P
        NPATCH = GRID * GRID
        NTOK = NPATCH + 1
        BATCH = 64
        EPS = 1e-05

        def layernorm(x, w, b):
            mu = jnp.mean(x, axis=-1, keepdims=True)
            var = jnp.mean(jnp.square(x - mu), axis=-1, keepdims=True)
            return (x - mu) * jax.lax.rsqrt(var + EPS) * w + b
        B = x.shape[0]
        hd = DIM // HEADS
        scale = hd ** (-0.5)
        patches = x.reshape(B, 3, GRID, P, GRID, P)
        patches = patches.transpose(0, 2, 4, 1, 3, 5).reshape(B, NPATCH, 3 * P * P)
        tok = patches @ conv_w + conv_b
        cls = jnp.broadcast_to(cls_token, (B, 1, DIM))
        h = jnp.concatenate([cls, tok], axis=1) + pos_embed
        for i in range(DEPTH):
            y = layernorm(h, ln1_w[i], ln1_b[i])
            qkv = (y @ qkv_w[i] + qkv_b[i]).reshape(B, NTOK, 3, HEADS, hd)
            qkv = qkv.transpose(2, 0, 3, 1, 4)
            q, k, v = (qkv[0], qkv[1], qkv[2])
            attn = jax.nn.softmax(jnp.einsum('bhnd,bhmd->bhnm', q, k) * scale, axis=-1)
            o = jnp.einsum('bhnm,bhmd->bhnd', attn, v)
            o = o.transpose(0, 2, 1, 3).reshape(B, NTOK, DIM)
            h = h + (o @ proj_w[i] + proj_b[i])
            y = layernorm(h, ln2_w[i], ln2_b[i])
            y = jax.nn.gelu(y @ fc1_w[i] + fc1_b[i], approximate=False)
            h = h + (y @ fc2_w[i] + fc2_b[i])
        return layernorm(h, norm_w, norm_b)

    def _L0_txt_ref(tokens, p):
        import jax, jax.numpy as jnp
        import numpy as np
        D_MODEL = 128
        END_IDX = 2

        def _build_tree(tokens):
            B, T = tokens.shape
            cap = 2 * T + 2
            left2 = jnp.array([1.0, 0.0], jnp.float32)
            right2 = jnp.array([0.0, 1.0], jnp.float32)
            bidx = jnp.arange(B)
            X0 = jnp.zeros((B, T, D_MODEL), jnp.float32)
            par0 = jnp.zeros((B, cap), jnp.int32)
            lr0 = jnp.zeros((B, cap), jnp.int32)
            head0 = jnp.zeros((B,), jnp.int32)
            tail0 = jnp.zeros((B,), jnp.int32)

            def body(carry, t):
                X, par, lr, head, tail = carry
                parent = par[bidx, head]
                plr = lr[bidx, head]
                x_parent = X[bidx, parent]
                lrvec = jnp.where(plr[:, None] == 0, left2, right2)
                x_it = jnp.concatenate([lrvec, x_parent[:, :-2]], axis=1)
                x_it = jnp.where(t == 0, 0.0, x_it)
                X = X.at[bidx, t].set(x_it)
                tok = tokens[bidx, t]
                push = jnp.where(t == 0, True, tok != END_IDX)
                tval = jnp.full((B,), 0, jnp.int32) + jnp.int32(t)
                par = par.at[bidx, tail].set(tval).at[bidx, tail + 1].set(tval)
                lr = lr.at[bidx, tail].set(0).at[bidx, tail + 1].set(1)
                tail = tail + 2 * push.astype(jnp.int32)
                pop = (t > 0) & (tail - head > 1)
                head = head + pop.astype(jnp.int32)
                return ((X, par, lr, head, tail), None)
            (X, _, _, _, _), _ = jax.lax.scan(body, (X0, par0, lr0, head0, tail0), jnp.arange(T))
            return X
        X = _build_tree(tokens)
        poly = p ** jnp.arange(D_MODEL, dtype=jnp.float32)
        return X * poly

    def _L0_attn_ref(x, wq, wk, wv, wo, w1, b1, w2, b2):
        import jax, jax.numpy as jnp
        import numpy as np
        B, S, D, DI = (8, 1024, 128, 512)
        EPS = 1e-12

        def _l2norm(x):
            n = jnp.sqrt(jnp.sum(x * x, axis=-1, keepdims=True))
            return x / jnp.maximum(n, EPS)
        q = _l2norm(jnp.einsum('bsd,de->bse', x, wq))
        k = _l2norm(jnp.einsum('bsd,de->bse', x, wk))
        v = jnp.einsum('bsd,de->bse', x, wv)
        kv = jnp.sum(k * v, axis=-2, keepdims=True)
        attn = jnp.einsum('bse,ed->bsd', q * kv, wo) + x
        h = jax.nn.relu(jnp.einsum('bsd,de->bse', attn, w1) + b1)
        out = jnp.einsum('bse,ed->bsd', h, w2) + b2 + attn
        return out

    def _L0_ffn_ref(x, gate_w, gate_b, w1, b1, w2, b2):
        import jax, jax.numpy as jnp
        import numpy as np
        B, S, H, E, K = (8, 1024, 128, 8, 2)
        logits = jnp.einsum('bsh,he->bse', x, gate_w) + gate_b
        topk_vals, topk_idx = jax.lax.top_k(logits, K)
        topk_weights = jax.nn.softmax(topk_vals, axis=-1)
        mask = jax.nn.one_hot(topk_idx, E, dtype=topk_weights.dtype)
        weights = jnp.einsum('bske,bsk->bse', mask, topk_weights)
        h = jax.nn.relu(jnp.einsum('bsh,ehf->bsef', x, w1) + b1)
        expert_out = jnp.einsum('bsef,efh->bseh', h, w2) + b2
        return jnp.einsum('bseh,bse->bsh', expert_out, weights)
    h = _L0_tok_ref(x, L0_tok_conv_w, L0_tok_conv_b, L0_tok_cls_token, L0_tok_pos_embed, L0_tok_ln1_w, L0_tok_ln1_b, L0_tok_qkv_w, L0_tok_qkv_b, L0_tok_proj_w, L0_tok_proj_b, L0_tok_ln2_w, L0_tok_ln2_b, L0_tok_fc1_w, L0_tok_fc1_b, L0_tok_fc2_w, L0_tok_fc2_b, L0_tok_norm_w, L0_tok_norm_b)
    h = jnp.concatenate([h, _L0_txt_ref(x_txt, L0_txt_p)], axis=1)
    h = h + _L0_attn_ref(_layernorm(h, axis=-1), L0_attn_wq, L0_attn_wk, L0_attn_wv, L0_attn_wo, L0_attn_w1, L0_attn_b1, L0_attn_w2, L0_attn_b2)
    h = h + _L0_ffn_ref(_layernorm(h, axis=-1), L0_ffn_gate_w, L0_ffn_gate_b, L0_ffn_w1, L0_ffn_b1, L0_ffn_w2, L0_ffn_b2)
    return h

_drawn_inputs = setup_inputs


def setup_inputs(seed=0):
    import zlib

    import numpy as np

    out = dict(_drawn_inputs(seed))
    spreads = {'L0_tok_conv_b': (0.0, 0.1),
     'L0_tok_ln1_w': (1.0, 0.6),
     'L0_tok_ln1_b': (0.0, 0.431),
     'L0_tok_qkv_b': (0.0, 0.1),
     'L0_tok_proj_b': (0.0, 0.1),
     'L0_tok_ln2_w': (1.0, 0.6),
     'L0_tok_ln2_b': (0.0, 0.569),
     'L0_tok_fc1_b': (0.0, 0.1),
     'L0_tok_fc2_b': (0.0, 0.1),
     'L0_tok_norm_w': (1.0, 0.2),
     'L0_tok_norm_b': (0.0, 0.1)}
    factors = {'L0_tok_cls_token': 8.0,
     'L0_attn_b1': 3.988,
     'L0_attn_b2': 3.391,
     'L0_ffn_gate_b': 2.701,
     'L0_ffn_b1': 7.19,
     'L0_ffn_b2': 4.031}
    for name, (base, spread) in spreads.items():
        noise = np.random.default_rng([zlib.crc32(name.encode()), seed]).standard_normal(out[name].shape)
        drawn = base * np.exp(spread * noise) if base else spread * noise
        out[name] = jnp.asarray(drawn.astype(out[name].dtype))
    for name, factor in factors.items():
        out[name] = (out[name] * factor).astype(out[name].dtype)
    return out
```

```python
from contextlib import ExitStack

import concourse.bass as bass
from concourse import mybir

F32 = mybir.dt.float32
F32R = mybir.dt.float32r
BF16 = mybir.dt.bfloat16
I32 = mybir.dt.int32
U32 = mybir.dt.uint32
ALU = mybir.AluOpType
ACT = mybir.ActivationFunctionType
AX = mybir.AxisListType

NB = 32
IMG, PT = 224, 16
GRID = IMG // PT
D = 128
HEADS, HD = 8, 16
PAIRS = HEADS // 2
DEPTH = 4
HID = 256
NT = GRID * GRID + 1
T = 77
S = NT + T
DI = 512
NE = 8
EF = 256
EPS = 1e-5
END_TOKEN = 2

CP = (NT + 1) // 2
NTP = 2 * CP
KROWS = (CP, NT - CP)

PARTS = 3 * 2 * HD
GUARD = 112
STACK_DMAS = 16 * 7
STACKS = 6

VROWS = NB * NT
VG = VROWS // 512
VREM = VROWS % 512 // 4
JROWS = NB * S
JG = JROWS // 512
JREM = JROWS % 512 // 4


def row(ap, parts):
    return ap.rearrange("(a n) -> a n", a=1).broadcast_to([parts, ap.shape[0]])


def image(hv, b):
    return hv[bass.ds(b * NT, NTP), :].rearrange("(p c) d -> p c d", c=2)


class Phase:

    def __init__(self, nc, name):
        self.nc, self.name, self.ctx, self.sems = nc, name, ExitStack(), []

    def sb(self, name, shape, dt=F32):
        return self.ctx.enter_context(self.nc.sbuf_tensor(f"{self.name}_{name}", shape, dt))

    def sem(self, name):
        s = self.ctx.enter_context(self.nc.semaphore(f"{self.name}_{name}"))
        self.sems.append(s)
        return s

    def close(self):
        with self.nc.Block() as block:
            @block.sync
            def _(sp):
                for s in self.sems:
                    sp.sem_clear(s)
        self.ctx.close()


def build_constants(nc, C, hv):
    ph = Phase(nc, "const")
    filled, selected, stored = ph.sem("filled"), ph.sem("selected"), ph.sem("stored")
    with nc.Block() as block:
        @block.gpsimd
        def _(pool):
            pool.memset(C.ident[:, :], 0.0).then_inc(filled, 1)
            pool.memset(C.ones[:, :], 1.0).then_inc(filled, 1)
            pool.memset(C.zeros[:, :], 0.0).then_inc(filled, 1)
            pool.memset(C.half[:, :], -0.5).then_inc(filled, 1)
            pool.memset(C.eps[:, :], EPS).then_inc(filled, 1)
            pool.wait_ge(filled, 5)
            pool.affine_select(out=C.ident[:, :], in_=C.ident[:, :], compare_op=ALU.not_equal, fill=1.0,
                               base=0, pattern=[[-1, 128]], channel_multiplier=1).then_inc(selected, 1)

        @block.sync
        def _(sp):
            sp.wait_ge(filled, 5)
            sp.dma_start(hv[VROWS:VROWS + 1, :], C.zeros[0:1, 0:D]).then_inc(stored, 16)
            sp.wait_ge(stored, 16)
            sp.wait_ge(selected, 1)
    ph.close()


def build_texts(nc, C, A, rows_dram, txt_dram):
    ph = Phase(nc, "txt")
    tok = ph.sb("tok", [NB, T], I32)
    tf = ph.sb("tf", [NB, 8, T])
    ti = ph.sb("ti", [NB, 2, T], I32)
    order_bc = ph.sb("order_bc", [T, NB, T])
    parent_bc = ph.sb("parent_bc", [T, NB, T])
    cols = ph.sb("cols", [T, 3, NB])
    P = ph.sb("P", [T, 2, NB, T], BF16)
    Q = ph.sb("Q", [T, 2, NB, T], BF16)
    X = ph.sb("X", [T, NB, D], BF16)
    res = ph.sb("res", [T, NB, D])
    poly = ph.sb("poly", [T, D])
    pw = ph.sb("pw", [T, 8])
    loaded, seq, rows_out, rows_in = ph.sem("loaded"), ph.sem("seq"), ph.sem("rows_out"), ph.sem("rows_in")
    built, zeroed, xmm, xcp, pmm, pcp = (ph.sem(n) for n in ("built", "zeroed", "xmm", "xcp", "pmm", "pcp"))
    poly_ready, pseq, res_ready, stored = ph.sem("poly_ready"), ph.sem("pseq"), ph.sem("res_ready"), ph.sem("stored")
    GT = 6
    groups = [(a, min(a + GT, NB)) for a in range(0, NB, GT)]
    STEPS = 6
    SEQ = 16

    with nc.Block() as block:
        @block.sync
        def _(sp):
            sp.dma_start(tok[:, :], A["x_txt"]).then_inc(loaded, 16)
            sp.dma_start(pw[:, 0:1], row(A["L0_txt_p"], T)).then_inc(loaded, 16)
            sp.wait_ge(seq, SEQ)
            for r in range(3):
                sp.dma_start(rows_dram[r], tf[:, 5 + r, :]).then_inc(rows_out, 16)
            sp.wait_ge(rows_out, 48)
            for r, dst in ((0, order_bc), (1, parent_bc)):
                sp.dma_start(dst[:, :, :], rows_dram[r:r + 1].broadcast_to([T, NB, T])).then_inc(rows_in, 16)
            for r in range(3):
                sp.dma_start(cols[:, r, :], rows_dram[r].rearrange("b t -> t b"), allow_slow_non_contiguous=True).then_inc(rows_in, 16)
            sp.wait_ge(res_ready, 1)
            sp.dma_start(txt_dram.rearrange("b t d -> t b d"), res[:, :, :]).then_inc(stored, 16)
            sp.wait_ge(stored, 16)

        @block.gpsimd
        def _(pool):
            pool.memset(X[:, :, :], 0.0).then_inc(zeroed, 1)

        @block.vector
        def _(dve):
            done = [0]

            def step(ins):
                done[0] += 1
                ins.then_inc(seq, 1)
                dve.wait_ge(seq, done[0])

            tokf, push, gain, length, pushes, order, parent, side = (tf[:, r, :] for r in range(8))
            dve.wait_ge(loaded, 32)
            step(dve.tensor_copy(tokf, tok[:, :]))
            step(dve.tensor_scalar(push, tokf, float(END_TOKEN), None, ALU.not_equal))
            step(dve.memset(push[:, 0:1], 1.0))
            step(dve.tensor_scalar(gain, push, 2.0, -1.0, ALU.mult, ALU.add))
            step(dve.memset(tokf, 1.0))
            step(dve.tensor_tensor_scan(length, gain, tokf, 1.0, ALU.add, ALU.max))
            step(dve.memset(tokf, 0.0))
            step(dve.tensor_tensor_scan(pushes, push, tokf, 0.0, ALU.add, ALU.add))
            step(dve.tensor_tensor(order, pushes, push, ALU.mult))
            step(dve.scalar_tensor_tensor(out=ti[:, 0, 1:T], in0=pushes[:, 0:T - 1], scalar=2.0,
                                          in1=length[:, 0:T - 1], op0=ALU.mult, op1=ALU.subtract))
            step(dve.tensor_scalar(ti[:, 1, 1:T], ti[:, 0, 1:T], 1, None, ALU.bitwise_and))
            step(dve.tensor_copy(side[:, 1:T], ti[:, 1, 1:T]))
            step(dve.tensor_scalar(ti[:, 1, 1:T], ti[:, 0, 1:T], 1, None, ALU.arith_shift_right))
            step(dve.tensor_scalar(parent[:, 1:T], ti[:, 1, 1:T], 1.0, None, ALU.add))
            step(dve.memset(parent[:, 0:1], -1.0))
            step(dve.memset(side[:, 0:1], 2.0))
            assert done[0] == SEQ

            dve.wait_ge(rows_in, 80)
            dve.tensor_tensor(P[:, 0, :, :], order_bc[:, :, :], cols[:, 1, :].unsqueeze(2).broadcast_to([T, NB, T]),
                              ALU.is_equal).then_inc(built, 1)
            dve.tensor_tensor(Q[:, 0, :, :], parent_bc[:, :, :], cols[:, 0, :].unsqueeze(2).broadcast_to([T, NB, T]),
                              ALU.is_equal).then_inc(built, 1)
            dve.wait_ge(zeroed, 1)
            for k in range(2):
                dve.tensor_scalar(X[:, :, k:k + 1], cols[:, 2, :].unsqueeze(2), float(k), None,
                                  ALU.is_equal).then_inc(built, 1)
            dve.memset(poly[:, 0:1], 1.0).then_inc(pseq, 1)
            for k in range(7):
                n = 1 << k
                dve.wait_ge(pseq, 2 * k + 1)
                dve.tensor_scalar(poly[:, n:2 * n], poly[:, 0:n], pw[:, k:k + 1], None, ALU.mult).then_inc(pseq, 1)
                dve.tensor_tensor(pw[:, k + 1:k + 2], pw[:, k:k + 1], pw[:, k:k + 1], ALU.mult).then_inc(pseq, 1)

            px = 0
            for s in range(STEPS):
                w = 2 << s
                for a in range(0, NB, 8):
                    px += 1
                    dve.wait_ge(xmm, px)
                    bank = C.bank[(px - 1) % 2]
                    dve.tensor_copy(X[:, a:a + 8, w:2 * w], bank[0:T, 0:8 * w].rearrange("p (b w) -> p b w", b=8))\
                       .then_inc(xcp, 1)
            dve.wait_ge(xcp, px)
            dve.wait_ge(pseq, 15)
            dve.tensor_tensor(res[:, :, :], X[:, :, :], poly[:, :].unsqueeze(1).broadcast_to([T, NB, D]),
                              ALU.mult).then_inc(res_ready, 1)

        @block.scalar
        def _(act):
            n = 0
            for s in range(STEPS - 1):
                for a, z in groups:
                    for M in (P, Q):
                        act.wait_ge(pmm, n + 1)
                        act.activation(M[:, (s + 1) % 2, a:z, :],
                                       C.bank[2 + n % 6][0:T, 0:(z - a) * T].rearrange("p (b t) -> p b t", t=T),
                                       ACT.Copy).then_inc(pcp, 1)
                        n += 1

        @block.tensor
        def _(pe):
            pe.wait_ge(built, 4)
            px = n = 0
            for s in range(STEPS):
                w = 2 << s
                if s:
                    pe.wait_ge(pcp, n)
                    pe.wait_ge(xcp, px)
                for a in range(0, NB, 8):
                    if px >= 2:
                        pe.wait_ge(xcp, px - 1)
                    for b in range(8):
                        mm = pe.matmul(C.bank[px % 2][0:T, b * w:(b + 1) * w], Q[:, s % 2, a + b, :],
                                       X[:, a + b, 0:w], start=True, stop=True)
                    mm.then_inc(xmm, 1)
                    px += 1
                if s == STEPS - 1:
                    break
                for a, z in groups:
                    for L, R in ((Q, P), (P, Q)):
                        if n >= 6:
                            pe.wait_ge(pcp, n - 5)
                        for b in range(a, z):
                            mm = pe.matmul(C.bank[2 + n % 6][0:T, (b - a) * T:(b - a + 1) * T], L[:, s % 2, b, :],
                                           R[:, s % 2, b, :], start=True, stop=True)
                        mm.then_inc(pmm, 1)
                        n += 1
    ph.close()


def build_patches(nc, C, A, hv):
    ph = Phase(nc, "px")
    HP = PT // 2
    RW = 3 * PT
    TP = GRID * GRID // 2
    img = [ph.sb(f"img{p}", [2 * RW, GRID, IMG]) for p in range(2)]
    w = ph.sb("w", [2 * RW, HP, D])
    pos = ph.sb("pos", [TP, 2, D])
    bias = ph.sb("bias", [TP, D])
    first = ph.sb("first", [NB, 2, D])
    emb = [ph.sb(f"emb{p}", [TP, 2, D]) for p in range(2)]
    weights = ph.sem("weights")
    loaded = [ph.sem(f"loaded{p}") for p in range(2)]
    stored = [ph.sem(f"stored{p}") for p in range(2)]
    summed, pos_ready, added, cls_ready, cls_out = (ph.sem(n) for n in ("summed", "pos_ready", "added", "cls_ready", "cls_out"))

    def load_image(eng, b, p, half):
        wd = IMG - HP * half
        for c in range(3):
            r = RW * half + PT * c
            eng.dma_start(img[p][r:r + PT, :, 0:wd],
                          A["x"][bass.ds(b, 1), c, :, HP * half:IMG].rearrange("o (g r) w -> r (o g) w", r=PT))\
               .then_inc(loaded[p], 16)

    def store(eng, b, p):
        eng.wait_ge(added, b + 1)
        eng.dma_start(hv[bass.ds(b * NT + 1, NT - 1), :].rearrange("(c p) d -> p c d", c=2),
                      emb[p][:, :, :]).then_inc(stored[p], 16)

    with nc.Block() as block:
        @block.sync
        def _(sp):
            cw = A["L0_tok_conv_w"].rearrange("(r x) d -> r x d", x=PT)
            for half in range(2):
                sp.dma_start(w[RW * half:RW * half + RW, :, :], cw[:, HP * half:HP * half + HP, :]).then_inc(weights, 16)
            position = A["L0_tok_pos_embed"][0]
            sp.dma_start(pos[:, :, :], position[1:NT, :].rearrange("(c p) d -> p c d", c=2)).then_inc(weights, 16)
            sp.dma_start(bias[:, :], row(A["L0_tok_conv_b"], TP)).then_inc(weights, 16)
            sp.dma_start(first[:, 0, :], A["L0_tok_cls_token"][0].broadcast_to([NB, D])).then_inc(weights, 16)
            sp.dma_start(first[:, 1, :], position[0:1, :].broadcast_to([NB, D])).then_inc(weights, 16)
            for p in range(2):
                load_image(sp, p, p, 0)
            with sp.Fori(1, NB // 2) as k:
                for p in range(2):
                    sp.wait_ge(summed, 2 * k + p - 1)
                    load_image(sp, 2 * k + p, p, 0)
                    store(sp, 2 * k + p - 2, p)
            for p in range(2):
                store(sp, NB - 2 + p, p)
            sp.wait_ge(cls_ready, 1)
            sp.dma_start(hv[0:VROWS, :].rearrange("(b t) d -> b t d", t=NT)[:, 0, :], first[:, 0, :]).then_inc(cls_out, 16)
            sp.wait_ge(cls_out, 16)
            for p in range(2):
                sp.wait_ge(stored[p], 16 * NB // 2)

        @block.scalar
        def _(act):
            for p in range(2):
                load_image(act, p, p, 1)
            with act.Fori(1, NB // 2) as k:
                for p in range(2):
                    act.wait_ge(summed, 2 * k + p - 1)
                    load_image(act, 2 * k + p, p, 1)

        @block.tensor
        def _(pe):
            pe.wait_ge(weights, 96)

            def embed(k, p, again):
                pe.wait_ge(loaded[p], 96 * k + 96)
                if again:
                    pe.wait_ge(added, 2 * k + p - 1)
                for c in range(2):
                    for x in range(HP):
                        mm = pe.matmul(C.bank[p][0:TP, c * D:(c + 1) * D],
                                       img[p][:, 7 * c:7 * c + 7, x:x + PT * (GRID - 1) + 1:PT], w[:, x, :],
                                       start=(x == 0), stop=(x == HP - 1))
                mm.then_inc(summed, 1)
            for p in range(2):
                embed(0, p, False)
            with pe.Fori(1, NB // 2) as k:
                for p in range(2):
                    embed(k, p, True)

        @block.vector
        def _(dve):
            dve.wait_ge(weights, 96)
            dve.tensor_tensor(pos[:, :, :], pos[:, :, :], bias[:, :].unsqueeze(1).broadcast_to([TP, 2, D]),
                              ALU.add).then_inc(pos_ready, 1)
            dve.tensor_tensor(first[:, 0, :], first[:, 0, :], first[:, 1, :], ALU.add).then_inc(cls_ready, 1)
            dve.wait_ge(pos_ready, 1)

            def add(k, p, again):
                dve.wait_ge(summed, 2 * k + p + 1)
                if again:
                    dve.wait_ge(stored[p], 16 * k)
                dve.tensor_tensor(emb[p][:, :, :], C.bank[p][0:TP, 0:2 * D].rearrange("p (c d) -> p c d", c=2),
                                  pos[:, :, :], ALU.add).then_inc(added, 1)
            for p in range(2):
                add(0, p, False)
            with dve.Fori(1, NB // 2) as k:
                for p in range(2):
                    add(k, p, True)

    ph.close()


def build_attention(nc, C, A, hv, bounce, layer):
    ph = Phase(nc, "att")
    w_qkv = ph.sb("w_qkv", [D, 3 * D])
    w_turned = ph.sb("w_turned", [D, 2, 2, HD, PAIRS])
    w_proj = ph.sb("w_proj", [D, D])
    ln = ph.sb("ln", [D, 2])
    b_qk = ph.sb("b_qk", [D, 2])
    b_v = ph.sb("b_v", [128, D])
    b_proj = ph.sb("b_proj", [128, D])
    ha = [ph.sb(f"ha{p}", [CP, 2, D]) for p in range(2)]
    hr = [ph.sb(f"hr{p}", [CP, 2, D]) for p in range(3)]
    xn = [ph.sb(f"xn{p}", [CP, 2, D]) for p in range(2)]
    st = ph.sb("st", [CP, 2, 6])
    mv = [ph.sb(f"mv{p}", [CP, 2, 2]) for p in range(2)]
    ve = ph.sb("ve", [CP, 2])
    rs = [ph.sb(f"rs{p}", [CP, 2]) for p in range(2)]
    yT = [ph.sb(f"yT{p}", [D, NTP]) for p in range(2)]
    Q_LO, Q_HI, K_LO, K_HI = range(4)
    parts = [ph.sb(f"parts{p}", [D, 4, NTP], F32R) for p in range(2)]
    vblk = [ph.sb(f"vblk{q}", [CP, 2, HEADS, 2 * HD]) for q in range(STACKS)]
    oblk = ph.sb("oblk", [CP, 2, 2 * HD])
    qst = [ph.sb(f"qst{q}", [128, PAIRS, NTP], F32R) for q in range(STACKS)]
    kst = [[ph.sb(f"kst{q}{j}", [128, PAIRS, NTP], F32R) for j in range(2)] for q in range(STACKS)]
    negm = [ph.sb(f"negm{p}", [CP, 2, HEADS]) for p in range(2)]
    gmax = ph.sb("gmax", [HEADS, NTP], F32R)
    E = [ph.sb(f"E{c}", [CP, PAIRS, 2, NTP]) for c in range(2)]
    rden = ph.sb("rden", [D, NTP])
    oT = [ph.sb(f"oT{p}", [D, NTP]) for p in range(2)]

    weights, init, ones_in, v_zero, turned = (ph.sem(n) for n in ("weights", "init", "ones_in", "v_zero", "turned"))
    ha_in = [ph.sem(f"ha_in{p}") for p in range(2)]
    hr_in = [ph.sem(f"hr_in{p}") for p in range(2)]
    bounced = [ph.sem(f"bounced{p}") for p in range(2)]
    stacked = [ph.sem(f"stacked{p}") for p in range(2)]
    guarded = [ph.sem(f"guarded{p}") for p in range(2)]
    stored = [ph.sem(f"stored{p}") for p in range(2)]
    (stats, var, eps_added, rstd, normed, xT, y_ready, qk, v_sum, hi, lo, v_ready, max_sum, maxed, gT, g_ready,
     s_sum, exped, pv, rden_ready, o_ready, projected, biased, summed) = (ph.sem(n) for n in (
        "stats", "var", "eps_added", "rstd", "normed", "xT", "y_ready", "qk", "v_sum", "hi", "lo", "v_ready",
        "max_sum", "maxed", "gT", "g_ready", "s_sum", "exped", "pv", "rden_ready", "o_ready", "projected",
        "biased", "summed"))

    FIRST, LAST = 3, 20

    def steps(eng, step):
        def peeled(i):
            def at(d):
                return (i + d) // 2, (i + d) % 2, i + d, (i + d) % STACKS
            step(at, lambda d: 0 <= i + d < NB, lambda d, n: i + d >= n)

        def looped(m, r):
            def at(d):
                c = FIRST + r + d
                return STACKS // 2 * m + c // 2, c % 2, STACKS * m + c, c % STACKS
            step(at, lambda d: True, lambda d, n: True)
        for i in range(-5, FIRST):
            peeled(i)
        with eng.Fori(0, (LAST - FIRST + 1) // STACKS) as m:
            for r in range(STACKS):
                looped(m, r)
        for i in range(LAST + 1, NB + 2):
            peeled(i)

    with nc.Block() as block:
        @block.sync
        def _(sp):
            def of(nm):
                return A["L0_tok_" + nm][bass.ds(layer, 1)]
            sp.dma_start(ha[0][:, :, :], image(hv, 0)).then_inc(ha_in[0], 16)
            sp.dma_start(w_qkv[:, :], of("qkv_w").rearrange("o p n -> (o p) n")).then_inc(weights, 16)
            sp.dma_start(w_proj[:, :], of("proj_w").rearrange("o p n -> (o p) n")).then_inc(weights, 16)
            for k, nm in enumerate(("ln1_w", "ln1_b")):
                sp.dma_start(ln[:, k:k + 1], of(nm).rearrange("o p -> p o"), allow_slow_non_contiguous=True)\
                  .then_inc(weights, 16)
            for k in range(2):
                by_side = of("qkv_b")[:, k * D:(k + 1) * D].rearrange("o (g j d) -> j d g o", j=2, d=HD)
                for j in range(2):
                    sp.dma_start(b_qk[64 * j:64 * j + 64, k:k + 1], by_side[j], allow_slow_non_contiguous=True)\
                      .then_inc(weights, 16)
            sp.dma_start(b_v[:, :], of("qkv_b")[:, 2 * D:3 * D].broadcast_to([128, D])).then_inc(weights, 16)
            sp.dma_start(b_proj[:, :], of("proj_b").broadcast_to([128, D])).then_inc(weights, 16)
            sp.wait_ge(init, 3 * STACKS + 1)
            for q4 in range(STACKS):
                for j in range(2):
                    sp.dma_start(kst[q4][j][GUARD + j:GUARD + j + 1, :, :].bitcast(F32),
                                 C.ones[0:1, :].rearrange("o (g t) -> o g t", g=PAIRS)).then_inc(ones_in, 16)

            def step(at, live, old):
                if live(-2):
                    k, p, n, q4 = at(-2)
                    sp.wait_ge(summed, 2 * k + p + 1)
                    sp.dma_start(hv[bass.ds(n * NT, NT - 1), :].rearrange("(p c) d -> p c d", c=2),
                                 hr[q4 % 3][0:CP - 1, :, :]).then_inc(stored[p], 16)
                    sp.dma_start(hv[bass.ds(n * NT + NT - 1, 1), :], hr[q4 % 3][CP - 1:CP, 0, :]).then_inc(stored[p], 16)
                if live(0):
                    k, p, n, q4 = at(0)
                    if old(0, 3):
                        sp.wait_ge(stored[1 - p], 32 * (k - 1 + p))
                    sp.dma_start(hr[q4 % 3][:, :, :], image(hv, n)).then_inc(hr_in[p], 16)
                if live(6):
                    k, p, n, q4 = at(6)
                    if old(6, 2):
                        sp.wait_ge(normed, 2 * (2 * k + p) - 2)
                    sp.dma_start(ha[p][:, :, :], image(hv, n)).then_inc(ha_in[p], 16)
                if live(1):
                    k, p, n, q4 = at(1)
                    sp.wait_ge(g_ready, 2 * k + p + 1)
                    sp.dma_start(qst[q4][GUARD:GUARD + 2, :, :].bitcast(F32), gmax[:, :].bitcast(F32))\
                      .then_inc(guarded[p], 16)
                if live(3):
                    k, p, n, q4 = at(3)
                    sp.wait_ge(bounced[p], 32 * k + 32)
                    if old(3, STACKS):
                        sp.wait_ge(s_sum, 8 * (2 * k + p) - 8 * STACKS + 8)
                    sp.dma_start(qst[q4][0:PARTS, :, :].bitcast(F32), bounce[p][0:3].rearrange("s j d g t -> (s j d) g t"))\
                      .then_inc(stacked[p], 16)
                    for j in range(2):
                        for s in range(3):
                            r = 32 * s + HD * j
                            sp.dma_start(kst[q4][j][r:r + HD, :, :].bitcast(F32), bounce[p][3 + s, j])\
                              .then_inc(stacked[p], 16)
            steps(sp, step)
            for p in range(2):
                sp.wait_ge(stored[p], 32 * NB // 2)

        @block.gpsimd
        def _(pool):
            for q4 in range(STACKS):
                pool.memset(qst[q4][:, :, :].bitcast(F32), 0.0).then_inc(init, 1)
                for j in range(2):
                    pool.memset(kst[q4][j][:, :, :].bitcast(F32), 0.0).then_inc(init, 1)
            pool.memset(oblk[:, :, :], 0.0).then_inc(init, 1)
            pool.wait_ge(init, 3 * STACKS + 1)
            for j in range(2):
                pool.memset(oblk[:, j, HD * j:HD * j + HD], 1.0).then_inc(init, 1)
            pool.wait_ge(weights, 160)

            def step(at, live, old):
                if live(5):
                    k, p, n, q4 = at(5)
                    pool.wait_ge(var, 2 * (2 * k + p) + 2)
                    pool.tensor_tensor(ve[:, :], mv[p][:, :, 1], C.eps[0:CP, 0:2], ALU.add).then_inc(eps_added, 1)
                    pool.wait_ge(eps_added, 2 * k + p + 1)
                    if old(5, 2):
                        pool.wait_ge(normed, 2 * (2 * k + p) - 2)
                    pool.tensor_tensor(rs[p][:, :], ve[:, :], C.half[0:CP, 0:2], ALU.pow).then_inc(rstd, 1)
                if live(-1):
                    k, p, n, q4 = at(-1)
                    pool.wait_ge(hr_in[p], 16 * k + 16)
                    pool.tensor_tensor(hr[q4 % 3][:, :, :], hr[q4 % 3][:, :, :],
                                       b_proj[0:CP, :].unsqueeze(1).broadcast_to([CP, 2, D]), ALU.add)\
                        .then_inc(biased, 1)
            steps(pool, step)

        @block.vector
        def _(dve):
            for q4 in range(STACKS):
                dve.memset(vblk[q4][:, :, :, :], 0.0).then_inc(v_zero, 1)
            dve.wait_ge(v_zero, STACKS)
            dve.wait_ge(weights, 160)
            for q in range(2):
                for j in range(2):
                    dve.tensor_copy(w_turned[:, q, j, :, :],
                                    w_qkv[:, q * D:(q + 1) * D].rearrange("p (g j d) -> p j d g", j=2, d=HD)[:, j, :, :])\
                       .then_inc(turned, 1)

            def step(at, live, old):
                def maximum(u):
                    k, p, n, q4 = at(2)
                    b = 2 * k + p
                    dve.wait_ge(max_sum, 8 * b + u + 1)
                    if u == 0 and old(2, 2):
                        dve.wait_ge(gT, b - 1)
                    c, g = u // PAIRS, u % PAIRS
                    src = C.bank[2 + u % 2][0:CP, 0:2 * NTP].rearrange("p (j t) -> p j t", j=2)[:, :, 0:NT]
                    dve.tensor_reduce(negm[p][:, c, g::PAIRS], src, AX.X, ALU.max, negate=True).then_inc(maxed, 1)
                if live(2):
                    maximum(0)
                if live(5):
                    k, p, n, q4 = at(5)
                    b = 2 * k + p
                    dve.wait_ge(ha_in[p], 16 * k + 16)
                    for c in range(2):
                        dve.bn_stats(st[:, c, :], ha[p][:, c, :]).then_inc(stats, 1)
                    dve.wait_ge(stats, 3 * b + 2)
                    dve.memset(C.mark[:, :], 0.0).then_inc(stats, 1)
                    for c in range(2):
                        dve.bn_aggr(mv[p][:, c, :], st[:, c, :]).then_inc(var, 1)
                if live(2):
                    for u in range(1, 4):
                        maximum(u)
                if live(-1):
                    k, p, n, q4 = at(-1)
                    b = 2 * k + p
                    dve.wait_ge(pv, 2 * b + 2)
                    dve.reciprocal(rden[:, :], C.bank[4][:, NTP:2 * NTP]).then_inc(rden_ready, 1)
                    dve.wait_ge(rden_ready, b + 1)
                    if old(-1, 2):
                        dve.wait_ge(projected, b - 1)
                    dve.tensor_tensor(oT[p][:, :], C.bank[4][:, 0:NTP], rden[:, :], ALU.mult).then_inc(o_ready, 1)
                if live(2):
                    for u in range(4, 6):
                        maximum(u)
                if live(5):
                    k, p, n, q4 = at(5)
                    b = 2 * k + p
                    dve.wait_ge(rstd, b + 1)
                    if old(5, 2):
                        dve.wait_ge(xT, b - 1)
                    for c in range(2):
                        dve.tensor_scalar(xn[p][:, c, :], ha[p][:, c, :], mv[p][:, c, 0:1], rs[p][:, c:c + 1],
                                          ALU.subtract, ALU.mult).then_inc(normed, 1)
                if live(4):
                    k, p, n, q4 = at(4)
                    b = 2 * k + p
                    dve.wait_ge(v_sum, b + 1)
                    if old(4, STACKS):
                        dve.wait_ge(pv, 2 * b - 2 * STACKS + 2)
                    for j in range(2):
                        out = vblk[q4][:, :, j::2, HD * j:HD * j + HD]
                        src = C.bank[5][0:CP, 2 * D:4 * D].rearrange("p (c g j d) -> p c g j d", c=2, j=2, d=HD)
                        bias = b_v[0:CP, :].rearrange("p (g j d) -> p g j d", j=2, d=HD)[:, :, j, :]
                        dve.tensor_tensor(out, src[:, :, :, j, :], bias.unsqueeze(1).broadcast_to([CP, 2, PAIRS, HD]),
                                          ALU.add).then_inc(v_ready, 1)
                if live(2):
                    maximum(6)
                if live(4):
                    k, p, n, q4 = at(4)
                    b = 2 * k + p
                    dve.wait_ge(hi, 2 * b + 2)
                    for q, (dl, dh) in enumerate(((Q_LO, Q_HI), (K_LO, K_HI))):
                        dve.scalar_tensor_tensor(out=parts[p][:, dl, :], in0=C.bank[6][:, q * NTP:(q + 1) * NTP],
                                                 scalar=b_qk[:, q:q + 1], in1=parts[p][:, dh, :].bitcast(F32),
                                                 op0=ALU.add, op1=ALU.subtract).then_inc(lo, 1)
                if live(2):
                    maximum(7)
                if live(-1):
                    k, p, n, q4 = at(-1)
                    b = 2 * k + p
                    dve.wait_ge(projected, b + 1)
                    dve.wait_ge(biased, b + 1)
                    dve.tensor_tensor(hr[q4 % 3][:, :, :], C.bank[7][0:CP, 0:2 * D].rearrange("p (c d) -> p c d", c=2),
                                      hr[q4 % 3][:, :, :], ALU.add).then_inc(summed, 1)
            steps(dve, step)

        @block.scalar
        def _(act):
            act.wait_ge(weights, 160)

            def step(at, live, old):
                def exponential(u):
                    k, p, n, q4 = at(0)
                    b = 2 * k + p
                    c, g = u // PAIRS, u % PAIRS
                    act.wait_ge(s_sum, 8 * b + u + 1)
                    if g == 0 and old(0, 1):
                        act.wait_ge(pv, 2 * b - 1 + c)
                    nk = KROWS[c]
                    act.activation(E[c][0:nk, g, :, :], C.bank[u % 2][0:nk, 0:2 * NTP].rearrange("p (j t) -> p j t", j=2),
                                   ACT.Exp, scale=HD ** -0.5).then_inc(exped, 1)
                if live(3):
                    k, p, n, q4 = at(3)
                    b = 2 * k + p
                    act.wait_ge(lo, 2 * b + 2)
                    if old(3, 2):
                        act.wait_ge(stacked[p], STACK_DMAS * k)
                    places = bounce[p].rearrange("s j d g t -> (j d g) s t")
                    act.dma_start(places[:, 1:5, :], parts[p][:, :, :].bitcast(F32)).then_inc(bounced[p], 16)
                    act.dma_start(places[:, 0:6:5, :], parts[p][:, Q_HI:K_HI + 1:K_HI - Q_HI, :].bitcast(F32))\
                       .then_inc(bounced[p], 16)
                if live(0):
                    for u in range(2):
                        exponential(u)
                if live(4):
                    k, p, n, q4 = at(4)
                    b = 2 * k + p
                    act.wait_ge(xT, b + 1)
                    if old(4, 2):
                        act.wait_ge(v_sum, b - 1)
                    act.activation(yT[p][:, :], C.bank[5][:, 0:NTP], ACT.Identity, scale=ln[:, 0:1], bias=ln[:, 1:2])\
                       .then_inc(y_ready, 1)
                if live(0):
                    exponential(2)
                if live(1):
                    k, p, n, q4 = at(1)
                    b = 2 * k + p
                    act.wait_ge(gT, b + 1)
                    if old(1, 1):
                        ko = k - 1 + p
                        act.wait_ge(guarded[1 - p], 16 * ko + 16)
                    act.activation(gmax[:, :], C.bank[7][0:HEADS, 2 * D:2 * D + NTP], ACT.Copy).then_inc(g_ready, 1)
                if live(0):
                    for u in range(3, 5):
                        exponential(u)
                if live(4):
                    k, p, n, q4 = at(4)
                    b = 2 * k + p
                    act.wait_ge(qk, b + 1)
                    if old(4, 2):
                        act.wait_ge(bounced[p], 32 * k)
                    for q, dh in enumerate((Q_HI, K_HI)):
                        act.activation(parts[p][:, dh, :], C.bank[6][:, q * NTP:(q + 1) * NTP], ACT.Identity,
                                       bias=b_qk[:, q:q + 1]).then_inc(hi, 1)
                if live(0):
                    for u in range(5, 8):
                        exponential(u)
            steps(act, step)

        @block.tensor
        def _(pe):
            pe.wait_ge(weights, 160)
            pe.wait_ge(init, 3 * STACKS + 3)
            pe.wait_ge(ones_in, 32 * STACKS)
            pe.wait_ge(turned, 4)

            def step(at, live, old):
                def scores(u):
                    k, p, n, q4 = at(0)
                    b = 2 * k + p
                    c, g = u // PAIRS, u % PAIRS
                    nk = KROWS[c]
                    if u == 0:
                        pe.wait_ge(guarded[p], 16 * k + 16)
                    if u >= 2 or old(0, 1):
                        pe.wait_ge(exped, 8 * b + u - 1)
                    for j in range(2):
                        mm = pe.matmul(C.bank[u % 2][0:nk, j * NTP:(j + 1) * NTP],
                                       kst[q4][j][0:GUARD + 2, g, c * CP:c * CP + nk], qst[q4][0:GUARD + 2, g, :],
                                       start=True, stop=True)
                    mm.then_inc(s_sum, 1)

                def scores_for_max(u):
                    k, p, n, q4 = at(2)
                    b = 2 * k + p
                    c, g = u // PAIRS, u % PAIRS
                    if u == 0:
                        pe.wait_ge(stacked[p], STACK_DMAS * k + STACK_DMAS)
                    if u >= 2 or old(2, 1):
                        pe.wait_ge(maxed, 8 * b + u - 1)
                    for j in range(2):
                        mm = pe.matmul(C.bank[2 + u % 2][0:CP, j * NTP:(j + 1) * NTP],
                                       qst[q4][0:GUARD, g, c * CP:(c + 1) * CP], kst[q4][j][0:GUARD, g, :],
                                       start=True, stop=True)
                    mm.then_inc(max_sum, 1)

                def values(d, c):
                    k, p, n, q4 = at(d)
                    b = 2 * k + p
                    pe.wait_ge(exped, 8 * b + 4 * c + 4)
                    if c == 0:
                        pe.wait_ge(v_ready, 2 * b + 2)
                        if old(0, 1):
                            pe.wait_ge(o_ready, b)
                    nk = KROWS[c]
                    for what in range(2):
                        for j in range(2):
                            for g in range(PAIRS):
                                lhs = vblk[q4][0:nk, c, 2 * g + j, :] if what == 0 else oblk[0:nk, j, :]
                                mm = pe.matmul(C.bank[4][32 * g:32 * g + 32, what * NTP:(what + 1) * NTP], lhs,
                                               E[c][0:nk, g, j, :], start=(c == 0 and what == 0 and j == 0),
                                               stop=(c == 1 and j == 1), skip_group_check=True)
                    mm.then_inc(pv, 1)

                for u in range(8):
                    if live(0):
                        scores(u)
                    if live(2):
                        scores_for_max(u)
                    if u == 0 and live(4):
                        k, p, n, q4 = at(4)
                        b = 2 * k + p
                        pe.wait_ge(normed, 2 * b + 2)
                        if old(4, 1):
                            pe.wait_ge(v_ready, 2 * b)
                        for c in range(2):
                            mm = pe.transpose(C.bank[5][:, c * CP:(c + 1) * CP], xn[p][:, c, :], C.ident[0:CP, 0:CP])
                        mm.then_inc(xT, 1)
                    if u == 1 and live(1):
                        k, p, n, q4 = at(1)
                        b = 2 * k + p
                        pe.wait_ge(maxed, 8 * b + 8)
                        if old(1, 1):
                            pe.wait_ge(g_ready, b)
                        if live(-2):
                            pe.wait_ge(summed, b - 2)
                        for c in range(2):
                            mm = pe.transpose(C.bank[7][0:HEADS, 2 * D + c * CP:2 * D + (c + 1) * CP], negm[p][:, c, :],
                                              C.ident[0:CP, 0:CP])
                        mm.then_inc(gT, 1)
                    if u == 1 and live(-1):
                        values(-1, 1)
                    if u == 3 and live(4):
                        k, p, n, q4 = at(4)
                        b = 2 * k + p
                        pe.wait_ge(y_ready, b + 1)
                        if old(4, 1):
                            pe.wait_ge(lo, 2 * b)
                        for q in range(2):
                            mm = pe.matmul(C.bank[6][:, q * NTP:(q + 1) * NTP],
                                           w_turned[:, q, :, :, :].rearrange("p j d g -> p (j d g)"),
                                           yT[p][:, :], start=True, stop=True)
                        mm.then_inc(qk, 1)
                        for c in range(2):
                            mm = pe.matmul(C.bank[5][0:CP, (2 + c) * D:(3 + c) * D], yT[p][:, c * CP:(c + 1) * CP],
                                           w_qkv[:, 2 * D:3 * D], start=True, stop=True)
                        mm.then_inc(v_sum, 1)
                    if u == 5 and live(0):
                        values(0, 0)
                    if u == 6 and live(-1):
                        k, p, n, q4 = at(-1)
                        b = 2 * k + p
                        pe.wait_ge(o_ready, b + 1)
                        if live(1):
                            pe.wait_ge(g_ready, b + 3)
                        for c in range(2):
                            mm = pe.matmul(C.bank[7][0:CP, c * D:(c + 1) * D], oT[p][:, c * CP:(c + 1) * CP],
                                           w_proj[:, :], start=True, stop=True)
                        mm.then_inc(projected, 1)
            steps(pe, step)
    ph.close()


def build_mlp(nc, C, A, hv, layer):
    ph = Phase(nc, "mlp")
    NG = VG + 1
    fc1 = ph.sb("fc1", [D, HID])
    fc2 = ph.sb("fc2", [128, 2, D])
    ln = ph.sb("ln", [D, 2])
    b_fc1 = ph.sb("b_fc1", [128, 2])
    b_fc2 = ph.sb("b_fc2", [128, D])
    ha = [ph.sb(f"ha{p}", [128, 4, D]) for p in range(2)]
    hr = [ph.sb(f"hr{p}", [128, 4, D]) for p in range(2)]
    ho = [ph.sb(f"ho{p}", [128, 4, D]) for p in range(2)]
    xn = [ph.sb(f"xn{p}", [128, 4, D]) for p in range(2)]
    st = ph.sb("st", [128, 4, 6])
    mv = [ph.sb(f"mv{p}", [128, 4, 2]) for p in range(2)]
    ve = ph.sb("ve", [128, 4])
    rs = [ph.sb(f"rs{p}", [128, 4]) for p in range(2)]
    yT = [ph.sb(f"yT{p}", [D, 512]) for p in range(2)]
    mid = [ph.sb(f"mid{p}", [128, 2, 512]) for p in range(2)]
    ha_in = [ph.sem(f"ha_in{p}") for p in range(2)]
    hr_in = [ph.sem(f"hr_in{p}") for p in range(2)]
    stored = [ph.sem(f"stored{p}") for p in range(2)]
    weights, stats, var, eps_added, rstd, normed, xT, y_ready, up, gelued, down, biased, summed = (ph.sem(n) for n in (
        "weights", "stats", "var", "eps_added", "rstd", "normed", "xT", "y_ready", "up", "gelued", "down", "biased",
        "summed"))
    LOOP = (4, 9)

    def steps(eng, step):
        def peeled(i):
            step(lambda d: ((i + d) // 2, (i + d) % 2, i + d), lambda d: 0 <= i + d < NG, lambda d, n: i + d >= n,
                 lambda d: VREM if i + d == NG - 1 else 128)
        for i in range(-2, LOOP[0]):
            peeled(i)
        with eng.Fori(0, (LOOP[1] - LOOP[0] + 1) // 2) as m:
            for r in range(2):
                c0 = LOOP[0] + r
                step(lambda d, c0=c0: (m + (c0 + d) // 2, (c0 + d) % 2, 2 * m + c0 + d), lambda d: True,
                     lambda d, n: True, lambda d: 128)
        for i in range(LOOP[1] + 1, NG + 2):
            peeled(i)

    def group(n, P):
        return hv[bass.ds(n * 512, 4 * P), :].rearrange("(p t) d -> p t d", t=4)

    with nc.Block() as block:
        @block.sync
        def _(sp):
            def of(nm):
                return A["L0_tok_" + nm][bass.ds(layer, 1)]
            sp.dma_start(ha[0][:, :, :], group(0, 128)).then_inc(ha_in[0], 16)
            sp.dma_start(fc1[:, :], of("fc1_w").rearrange("o p n -> (o p) n")).then_inc(weights, 16)
            sp.dma_start(fc2[:, :, :], of("fc2_w").rearrange("o (c p) n -> p (o c) n", c=2)).then_inc(weights, 16)
            for k, nm in enumerate(("ln2_w", "ln2_b")):
                sp.dma_start(ln[:, k:k + 1], of(nm).rearrange("o p -> p o"), allow_slow_non_contiguous=True)\
                  .then_inc(weights, 16)
            sp.dma_start(b_fc1[:, :], of("fc1_b").rearrange("o (c p) -> p (o c)", c=2), allow_slow_non_contiguous=True)\
              .then_inc(weights, 16)
            sp.dma_start(b_fc2[:, :], of("fc2_b").broadcast_to([128, D])).then_inc(weights, 16)

            def step(at, live, old, parts):
                if live(2) and old(2, 1):
                    k, p, n = at(2)
                    if old(2, 2):
                        sp.wait_ge(normed, 4 * (2 * k + p) - 4)
                    sp.dma_start(ha[p][0:parts(2), :, :], group(n, parts(2))).then_inc(ha_in[p], 16)
                if live(0):
                    k, p, n = at(0)
                    if old(0, 2):
                        sp.wait_ge(summed, 2 * k + p - 1)
                    sp.dma_start(hr[p][0:parts(0), :, :], group(n, parts(0))).then_inc(hr_in[p], 16)
                if live(-2):
                    k, p, n = at(-2)
                    sp.wait_ge(summed, 2 * k + p + 1)
                    sp.dma_start(group(n, parts(-2)), ho[p][0:parts(-2), :, :]).then_inc(stored[p], 16)
            steps(sp, step)
            for p in range(2):
                sp.wait_ge(stored[p], 16 * ((NG + 1 - p) // 2))

        @block.gpsimd
        def _(pool):
            pool.wait_ge(weights, 96)

            def step(at, live, old, parts):
                if live(1):
                    k, p, n = at(1)
                    b, P = 2 * k + p, parts(1)
                    pool.wait_ge(var, 4 * b + 4)
                    pool.tensor_tensor(ve[0:P, :], mv[p][0:P, :, 1], C.eps[0:P, 0:4], ALU.add).then_inc(eps_added, 1)
                    pool.wait_ge(eps_added, b + 1)
                    if old(1, 2):
                        pool.wait_ge(normed, 4 * b - 4)
                    pool.tensor_tensor(rs[p][0:P, :], ve[0:P, :], C.half[0:P, 0:4], ALU.pow).then_inc(rstd, 1)
                if live(-1):
                    k, p, n = at(-1)
                    b, P = 2 * k + p, parts(-1)
                    pool.wait_ge(hr_in[p], 16 * k + 16)
                    pool.tensor_tensor(hr[p][0:P, :, :], hr[p][0:P, :, :],
                                       b_fc2[0:P, :].unsqueeze(1).broadcast_to([P, 4, D]), ALU.add).then_inc(biased, 1)
            steps(pool, step)

        @block.vector
        def _(dve):
            def step(at, live, old, parts):
                if live(1):
                    k, p, n = at(1)
                    b, P = 2 * k + p, parts(1)
                    dve.wait_ge(ha_in[p], 16 * k + 16)
                    for t in range(4):
                        dve.bn_stats(st[0:P, t, :], ha[p][0:P, t, :]).then_inc(stats, 1)
                    dve.wait_ge(stats, 5 * b + 4)
                    dve.memset(C.mark[:, :], 0.0).then_inc(stats, 1)
                    for t in range(4):
                        dve.bn_aggr(mv[p][0:P, t, :], st[0:P, t, :]).then_inc(var, 1)
                if live(-2):
                    k, p, n = at(-2)
                    b, P = 2 * k + p, parts(-2)
                    dve.wait_ge(down, b + 1)
                    dve.wait_ge(biased, b + 1)
                    if old(-2, 2):
                        dve.wait_ge(stored[p], 16 * k)
                    dve.tensor_tensor(ho[p][0:P, :, :], C.bank[5 + p][0:P, :].rearrange("p (t d) -> p t d", t=4),
                                      hr[p][0:P, :, :], ALU.add).then_inc(summed, 1)
                if live(1):
                    k, p, n = at(1)
                    b, P = 2 * k + p, parts(1)
                    dve.wait_ge(rstd, b + 1)
                    if old(1, 2):
                        dve.wait_ge(xT, b - 1)
                    for t in range(4):
                        dve.tensor_scalar(xn[p][0:P, t, :], ha[p][0:P, t, :], mv[p][0:P, t, 0:1], rs[p][0:P, t:t + 1],
                                          ALU.subtract, ALU.mult).then_inc(normed, 1)
            steps(dve, step)

        @block.scalar
        def _(act):
            act.wait_ge(weights, 96)

            def step(at, live, old, parts):
                if live(0):
                    k, p, n = at(0)
                    b, P = 2 * k + p, parts(0)
                    for f in range(2):
                        act.wait_ge(up, 2 * b + f + 1)
                        if f == 0 and old(0, 2):
                            act.wait_ge(down, b - 1)
                        act.activation(mid[p][:, f, 0:4 * P], C.bank[1 + 2 * p + f][:, 0:4 * P], ACT.Gelu,
                                       bias=b_fc1[:, f:f + 1]).then_inc(gelued, 1)
                if live(1):
                    k, p, n = at(1)
                    b, P = 2 * k + p, parts(1)
                    act.wait_ge(xT, b + 1)
                    if old(1, 2):
                        act.wait_ge(up, 2 * b - 2)
                    act.activation(yT[p][:, 0:4 * P], C.bank[0][:, 0:4 * P], ACT.Identity, scale=ln[:, 0:1],
                                   bias=ln[:, 1:2]).then_inc(y_ready, 1)
            steps(act, step)

        @block.tensor
        def _(pe):
            pe.wait_ge(weights, 96)

            def step(at, live, old, parts):
                def second_layer(tiles):
                    k, p, n = at(-1)
                    b, P = 2 * k + p, parts(-1)
                    for t in tiles:
                        for f in range(2):
                            mm = pe.matmul(C.bank[5 + p][0:P, t * D:(t + 1) * D], mid[p][:, f, t * P:(t + 1) * P],
                                           fc2[:, f, :], start=(f == 0), stop=(f == 1))
                    return mm
                if live(0):
                    k, p, n = at(0)
                    b, P = 2 * k + p, parts(0)
                    pe.wait_ge(y_ready, b + 1)
                    if old(0, 2):
                        pe.wait_ge(gelued, 2 * b - 2)
                    for f in range(2):
                        pe.matmul(C.bank[1 + 2 * p + f][:, 0:4 * P], fc1[:, f * 128:(f + 1) * 128], yT[p][:, 0:4 * P],
                                  start=True, stop=True).then_inc(up, 1)
                if live(-1):
                    k, p, n = at(-1)
                    b, P = 2 * k + p, parts(-1)
                    pe.wait_ge(gelued, 2 * b + 2)
                    if old(-1, 2):
                        pe.wait_ge(summed, b - 1)
                    second_layer(range(3))
                if live(1):
                    k, p, n = at(1)
                    b, P = 2 * k + p, parts(1)
                    pe.wait_ge(normed, 4 * b + 4)
                    if old(1, 1):
                        pe.wait_ge(y_ready, b)
                    for t in range(4):
                        mm = pe.transpose(C.bank[0][:, t * P:(t + 1) * P], xn[p][0:P, t, :], C.ident[0:P, 0:P])
                    mm.then_inc(xT, 1)
                if live(-1):
                    second_layer([3]).then_inc(down, 1)
            steps(pe, step)
    ph.close()


def build_joint(nc, C, A, hv, txt_dram, hj):
    ph = Phase(nc, "joint")
    LS = 4
    NC = 3
    ROWS = (*KROWS, T)
    COL = (0, KROWS[0], NT, S)
    wq, wk, wv, w1 = (ph.sb(n, [D, DI]) for n in ("wq", "wk", "wv", "w1"))
    wo, w2 = (ph.sb(n, [128, 4, D]) for n in ("wo", "w2"))
    b1 = ph.sb("b1", [128, 4])
    b2, nw, nb = (ph.sb(n, [128, D]) for n in ("b2", "nw", "nb"))
    wT = ph.sb("wT", [128, 2, 4, D])
    gram = ph.sb("gram", [D, 2, D])
    h, z, a = ([ph.sb(f"{n}{s}", [CP, NC, D]) for s in range(LS)] for n in ("h", "z", "a"))
    st = ph.sb("st", [CP, LS, NC, 6])
    mv = ph.sb("mv", [CP, LS, NC, 2])
    ve = ph.sb("ve", [CP, LS, NC])
    rs = ph.sb("rs", [CP, LS, NC])
    nsq = ph.sb("nsq", [CP, LS, 2 * NC])
    rn = ph.sb("rn", [CP, LS, 2 * NC])
    junk = ph.sb("junk", [CP, 2 * NC, D])
    zT = [ph.sb(f"zT{s}", [D, S]) for s in range(LS)]
    M = ph.sb("M", [D, LS, D])
    prod = ph.sb("prod", [D, LS, DI])
    kv = ph.sb("kv", [128, LS, 4])
    wos = ph.sb("wos", [128, LS, 4, D])
    W = ph.sb("W", [D, LS, D])
    hid = ph.sb("hid", [128, LS, 4, S])
    loaded = [ph.sem(f"loaded{s}") for s in range(LS)]
    stored = [ph.sem(f"stored{s}") for s in range(LS)]
    names = ("weights turnedT turned grammed gram_ready zeroed stats var eps rstd finaled scaled shifted stats2 var2 "
             "eps2 rstd2 z_ready z_turned zT_ready products norms clipped unit zk_ready m_sum m_ready mv_sum prod_ready "
             "kv_sum kv_ready wo_scaled w_sum w_ready a_sum a_ready a_turned aT_ready up relued down biased summed").split()
    sm = {n: ph.sem(n) for n in names}
    SLOT = range(LS)

    def both(s):
        return C.bank[s], C.bank[LS + s]

    with nc.Block() as block:
        @block.sync
        def _(sp):
            for dst, nm in ((wq, "wq"), (wk, "wk"), (wv, "wv"), (w1, "w1")):
                sp.dma_start(dst[:, :], A["L0_attn_" + nm]).then_inc(sm["weights"], 16)
            for dst, nm in ((wo, "wo"), (w2, "w2")):
                sp.dma_start(dst[:, :, :], A["L0_attn_" + nm].rearrange("(c p) d -> p c d", c=4)).then_inc(sm["weights"], 16)
            sp.dma_start(b1[:, :], A["L0_attn_b1"].rearrange("(c p) -> p c", c=4), allow_slow_non_contiguous=True)\
              .then_inc(sm["weights"], 16)
            for dst, nm in ((b2, "L0_attn_b2"), (nw, "L0_tok_norm_w"), (nb, "L0_tok_norm_b")):
                sp.dma_start(dst[:, :], row(A[nm], 128)).then_inc(sm["weights"], 16)
            sp.wait_ge(sm["zeroed"], LS + 1)

            def load(it, s):
                n = LS * it + s
                sp.dma_start(h[s][:, 0:2, :], image(hv, n)).then_inc(loaded[s], 16)
                sp.dma_start(h[s][0:T, 2, :], txt_dram[bass.ds(n, 1)].rearrange("o t d -> (o t) d")).then_inc(loaded[s], 16)

            def store(it, s):
                n = LS * it + s
                sp.wait_ge(sm["summed"], n * NC + NC)
                sp.dma_start(hj[bass.ds(n * S, NT - 1), :].rearrange("(p c) d -> p c d", c=2), h[s][0:CP - 1, 0:2, :])\
                  .then_inc(stored[s], 16)
                sp.dma_start(hj[bass.ds(n * S + NT - 1, 1), :], h[s][CP - 1:CP, 0, :]).then_inc(stored[s], 16)
                sp.dma_start(hj[bass.ds(n * S + NT, T), :], h[s][0:T, 2, :]).then_inc(stored[s], 16)
            for s in SLOT:
                load(0, s)
            with sp.Fori(0, NB // LS - 1) as it:
                for s in SLOT:
                    store(it, s)
                    sp.wait_ge(stored[s], 48 * it + 48)
                    load(it + 1, s)
            for s in SLOT:
                store(NB // LS - 1, s)
            for s in SLOT:
                sp.wait_ge(stored[s], 48 * NB // LS)

        @block.gpsimd
        def _(pool):
            for s in SLOT:
                pool.memset(h[s][:, :, :], 0.0).then_inc(sm["zeroed"], 1)
            pool.memset(nsq[:, :, :], 1.0).then_inc(sm["zeroed"], 1)
            pool.wait_ge(sm["weights"], 160)
            with pool.Fori(0, NB // LS) as it:
                for s in SLOT:
                    n = LS * it + s
                    pool.wait_ge(sm["var"], 2 * n + 2)
                    pool.tensor_tensor(ve[:, s, 0:2], mv[:, s, 0:2, 1], C.eps[0:CP, 0:2], ALU.add).then_inc(sm["eps"], 1)
                    pool.wait_ge(sm["eps"], n + 1)
                    pool.tensor_tensor(rs[:, s, 0:2], ve[:, s, 0:2], C.half[0:CP, 0:2], ALU.pow).then_inc(sm["rstd"], 1)
                for s in SLOT:
                    n = LS * it + s
                    pool.wait_ge(sm["finaled"], 2 * n + 2)
                    pool.tensor_tensor(h[s][:, 0:2, :], h[s][:, 0:2, :], nw[0:CP, :].unsqueeze(1).broadcast_to([CP, 2, D]),
                                       ALU.mult).then_inc(sm["scaled"], 1)
                    pool.wait_ge(sm["scaled"], n + 1)
                    pool.tensor_tensor(h[s][:, 0:2, :], h[s][:, 0:2, :], nb[0:CP, :].unsqueeze(1).broadcast_to([CP, 2, D]),
                                       ALU.add).then_inc(sm["shifted"], 1)
                for s in SLOT:
                    n = LS * it + s
                    pool.wait_ge(sm["var2"], NC * n + NC)
                    pool.tensor_tensor(ve[:, s, :], mv[:, s, :, 1], C.eps[0:CP, 0:NC], ALU.add).then_inc(sm["eps2"], 1)
                    pool.wait_ge(sm["eps2"], n + 1)
                    pool.tensor_tensor(rs[:, s, :], ve[:, s, :], C.half[0:CP, 0:NC], ALU.pow).then_inc(sm["rstd2"], 1)
                for s in SLOT:
                    n = LS * it + s
                    pool.wait_ge(sm["clipped"], n + 1)
                    pool.tensor_tensor(rn[:, s, :], nsq[:, s, :], C.half[0:CP, 0:2 * NC], ALU.pow).then_inc(sm["unit"], 1)
                for s in SLOT:
                    n = LS * it + s
                    pool.wait_ge(sm["a_ready"], NC * n + NC)
                    pool.tensor_tensor(h[s][:, :, :], h[s][:, :, :], a[s][:, :, :], ALU.add).then_inc(sm["biased"], 1)
                    pool.wait_ge(sm["biased"], 2 * n + 1)
                    pool.tensor_tensor(h[s][:, :, :], h[s][:, :, :], b2[0:CP, :].unsqueeze(1).broadcast_to([CP, NC, D]),
                                       ALU.add).then_inc(sm["biased"], 1)

        @block.vector
        def _(dve):
            dve.wait_ge(sm["weights"], 160)
            for q in range(2):
                dve.wait_ge(sm["turnedT"], q + 1)
                dve.tensor_copy(wT[:, q, :, :], C.bank[q][:, :].rearrange("p (c i) -> p c i", c=4)).then_inc(sm["turned"], 1)
            dve.wait_ge(sm["grammed"], 1)
            dve.tensor_copy(gram[:, :, :], C.bank[2][:, 0:2 * D].rearrange("p (q i) -> p q i", q=2)).then_inc(sm["gram_ready"], 1)
            with dve.Fori(0, NB // LS) as it:
                for s in SLOT:
                    n = LS * it + s
                    dve.wait_ge(loaded[s], 32 * it + 32)
                    for c in range(2):
                        dve.bn_stats(st[:, s, c, :], h[s][:, c, :]).then_inc(sm["stats"], 1)
                    dve.wait_ge(sm["stats"], 3 * n + 2)
                    dve.memset(C.mark[:, :], 0.0).then_inc(sm["stats"], 1)
                    for c in range(2):
                        dve.bn_aggr(mv[:, s, c, :], st[:, s, c, :]).then_inc(sm["var"], 1)
                for s in SLOT:
                    n = LS * it + s
                    dve.wait_ge(sm["rstd"], n + 1)
                    for c in range(2):
                        dve.tensor_scalar(h[s][:, c, :], h[s][:, c, :], mv[:, s, c, 0:1], rs[:, s, c:c + 1],
                                          ALU.subtract, ALU.mult).then_inc(sm["finaled"], 1)
                for s in SLOT:
                    n = LS * it + s
                    dve.wait_ge(sm["shifted"], n + 1)
                    for c in range(NC):
                        dve.bn_stats(st[:, s, c, :], h[s][:, c, :]).then_inc(sm["stats2"], 1)
                    dve.wait_ge(sm["stats2"], (NC + 1) * n + NC)
                    dve.memset(C.mark2[:, :], 0.0).then_inc(sm["stats2"], 1)
                    for c in range(NC):
                        dve.bn_aggr(mv[:, s, c, :], st[:, s, c, :]).then_inc(sm["var2"], 1)
                for s in SLOT:
                    n = LS * it + s
                    dve.wait_ge(sm["rstd2"], n + 1)
                    for c in range(NC):
                        dve.tensor_scalar(z[s][:, c, :], h[s][:, c, :], mv[:, s, c, 0:1], rs[:, s, c:c + 1],
                                          ALU.subtract, ALU.mult).then_inc(sm["z_ready"], 1)
                for s in SLOT:
                    n = LS * it + s
                    b0, b1_ = both(s)
                    dve.wait_ge(sm["products"], n + 1)
                    for c in range(NC):
                        r = ROWS[c]
                        for q in range(2):
                            src = (b0 if c < 2 else b1_)[0:r, (c % 2) * 2 * D + q * D:(c % 2) * 2 * D + (q + 1) * D]
                            dve.tensor_tensor_reduce(junk[0:r, 2 * c + q, :], src, z[s][0:r, c, :], 1.0, 0.0, ALU.mult, ALU.add,
                                                     nsq[0:r, s, 2 * c + q:2 * c + q + 1]).then_inc(sm["norms"], 1)
                    dve.wait_ge(sm["norms"], 2 * NC * n + 2 * NC)
                    dve.tensor_scalar(nsq[:, s, :], nsq[:, s, :], 1e-24, None, ALU.max).then_inc(sm["clipped"], 1)
                for s in SLOT:
                    n = LS * it + s
                    dve.wait_ge(sm["unit"], n + 1)
                    for c in range(NC):
                        dve.tensor_scalar(a[s][:, c, :], z[s][:, c, :], rn[:, s, 2 * c + 1:2 * c + 2], None, ALU.mult)\
                           .then_inc(sm["zk_ready"], 1)
                for s in SLOT:
                    n = LS * it + s
                    dve.wait_ge(sm["mv_sum"], n + 1)
                    dve.tensor_tensor(prod[:, s, :], both(s)[0][:, :], wk[:, :], ALU.mult).then_inc(sm["prod_ready"], 1)
                for s in SLOT:
                    n = LS * it + s
                    dve.wait_ge(sm["a_sum"], n + 1)
                    for c in range(NC):
                        r = ROWS[c]
                        dve.scalar_tensor_tensor(out=a[s][0:r, c, :], in0=both(s)[0][0:r, c * D:(c + 1) * D],
                                                 scalar=rn[0:r, s, 2 * c:2 * c + 1], in1=z[s][0:r, c, :],
                                                 op0=ALU.mult, op1=ALU.add).then_inc(sm["a_ready"], 1)
                for s in SLOT:
                    n = LS * it + s
                    dve.wait_ge(sm["down"], n + 1)
                    dve.wait_ge(sm["biased"], 2 * n + 2)
                    for c in range(NC):
                        r = ROWS[c]
                        dve.tensor_tensor(h[s][0:r, c, :], both(s)[0][0:r, c * D:(c + 1) * D], h[s][0:r, c, :], ALU.add)\
                           .then_inc(sm["summed"], 1)

        @block.scalar
        def _(act):
            act.wait_ge(sm["weights"], 160)
            with act.Fori(0, NB // LS) as it:
                def copy(wait, dst, src, done):
                    for s in SLOT:
                        act.wait_ge(sm[wait], LS * it + s + 1)
                        act.activation(dst(s), src(s), ACT.Copy).then_inc(sm[done], 1)
                copy("z_turned", lambda s: zT[s][:, :], lambda s: both(s)[0][:, 0:S], "zT_ready")
                copy("m_sum", lambda s: M[:, s, :], lambda s: both(s)[1][:, 256:256 + D], "m_ready")
                copy("kv_sum", lambda s: kv[:, s, :], lambda s: both(s)[1][:, 0:4], "kv_ready")
                for s in SLOT:
                    act.wait_ge(sm["kv_ready"], LS * it + s + 1)
                    for c in range(4):
                        act.activation(wos[:, s, c, :], wo[:, c, :], ACT.Copy, scale=kv[:, s, c:c + 1])\
                           .then_inc(sm["wo_scaled"], 1)
                copy("w_sum", lambda s: W[:, s, :], lambda s: both(s)[1][:, 256:256 + D], "w_ready")
                copy("a_turned", lambda s: zT[s][:, :], lambda s: both(s)[1][:, 0:S], "aT_ready")
                for f2 in range(2):
                    for s in SLOT:
                        n = LS * it + s
                        for f in (2 * f2, 2 * f2 + 1):
                            act.wait_ge(sm["up"], 16 * it + 8 * f2 + 2 * s + f % 2 + 1)
                            act.activation(hid[:, s, f, :], both(s)[f % 2][:, 0:S], ACT.Relu, bias=b1[:, f:f + 1])\
                               .then_inc(sm["relued"], 1)

        @block.tensor
        def _(pe):
            pe.wait_ge(sm["weights"], 160)
            for q, w in enumerate((wq, wk)):
                for c in range(4):
                    mm = pe.transpose(C.bank[q][:, c * D:(c + 1) * D], w[:, c * D:(c + 1) * D], C.ident[:, :])
                mm.then_inc(sm["turnedT"], 1)
            pe.wait_ge(sm["turned"], 2)
            for q in range(2):
                for c in range(4):
                    mm = pe.matmul(C.bank[2][:, q * D:(q + 1) * D], wT[:, q, c, :], wT[:, q, c, :],
                                   start=(c == 0), stop=(c == 3))
            mm.then_inc(sm["grammed"], 1)
            pe.wait_ge(sm["gram_ready"], 1)
            with pe.Fori(0, NB // LS) as it:
                def turn(s, src, dst):
                    for c in range(NC):
                        mm = pe.transpose(dst[:, COL[c]:COL[c + 1]], src[0:ROWS[c], c, :], C.ident[0:ROWS[c], 0:ROWS[c]])
                    return mm
                for s in SLOT:
                    n = LS * it + s
                    pe.wait_ge(sm["z_ready"], NC * n + NC)
                    turn(s, z[s], both(s)[0]).then_inc(sm["z_turned"], 1)
                for s in SLOT:
                    n = LS * it + s
                    b0, b1_ = both(s)
                    pe.wait_ge(sm["zT_ready"], n + 1)
                    for c in range(NC):
                        mm = pe.matmul((b0 if c < 2 else b1_)[0:ROWS[c], (c % 2) * 256:(c % 2) * 256 + 256],
                                       zT[s][:, COL[c]:COL[c + 1]], gram[:, :, :].rearrange("p q i -> p (q i)"),
                                       start=True, stop=True)
                    mm.then_inc(sm["products"], 1)
                for s in SLOT:
                    n = LS * it + s
                    pe.wait_ge(sm["zk_ready"], NC * n + NC)
                    for c in range(NC):
                        mm = pe.matmul(both(s)[1][:, 256:256 + D], a[s][0:ROWS[c], c, :], z[s][0:ROWS[c], c, :],
                                       start=(c == 0), stop=(c == NC - 1))
                    mm.then_inc(sm["m_sum"], 1)
                for s in SLOT:
                    n = LS * it + s
                    pe.wait_ge(sm["m_ready"], n + 1)
                    pe.matmul(both(s)[0][:, :], M[:, s, :], wv[:, :], start=True, stop=True).then_inc(sm["mv_sum"], 1)
                for s in SLOT:
                    n = LS * it + s
                    pe.wait_ge(sm["prod_ready"], n + 1)
                    for c in range(4):
                        mm = pe.matmul(both(s)[1][:, c:c + 1], prod[:, s, c * 128:(c + 1) * 128], C.ones[:, 0:1],
                                       start=True, stop=True)
                    mm.then_inc(sm["kv_sum"], 1)
                for s in SLOT:
                    n = LS * it + s
                    pe.wait_ge(sm["wo_scaled"], 4 * n + 4)
                    for c in range(4):
                        mm = pe.matmul(both(s)[1][:, 256:256 + D], wT[:, 0, c, :], wos[:, s, c, :],
                                       start=(c == 0), stop=(c == 3))
                    mm.then_inc(sm["w_sum"], 1)
                for s in SLOT:
                    n = LS * it + s
                    pe.wait_ge(sm["w_ready"], n + 1)
                    for c in range(NC):
                        mm = pe.matmul(both(s)[0][0:ROWS[c], c * D:(c + 1) * D], zT[s][:, COL[c]:COL[c + 1]], W[:, s, :],
                                       start=True, stop=True)
                    mm.then_inc(sm["a_sum"], 1)
                for s in SLOT:
                    n = LS * it + s
                    pe.wait_ge(sm["a_ready"], NC * n + NC)
                    turn(s, a[s], both(s)[1]).then_inc(sm["a_turned"], 1)
                for f2 in range(2):
                    for s in SLOT:
                        n = LS * it + s
                        if f2 == 0:
                            pe.wait_ge(sm["aT_ready"], n + 1)
                        else:
                            pe.wait_ge(sm["relued"], 16 * it + 2 * s + 2)
                        for f in (2 * f2, 2 * f2 + 1):
                            pe.matmul(both(s)[f % 2][:, 0:S], w1[:, f * 128:(f + 1) * 128], zT[s][:, :],
                                      start=True, stop=True).then_inc(sm["up"], 1)
                for s in SLOT:
                    n = LS * it + s
                    pe.wait_ge(sm["relued"], 16 * it + 8 + 2 * s + 2)
                    for c in range(NC):
                        for f in range(4):
                            mm = pe.matmul(both(s)[0][0:ROWS[c], c * D:(c + 1) * D], hid[:, s, f, COL[c]:COL[c + 1]],
                                           w2[:, f, :], start=(f == 0), stop=(f == 3))
                    mm.then_inc(sm["down"], 1)
                pe.wait_ge(sm["summed"], LS * NC * it + LS * NC)
    ph.close()


def build_experts(nc, C, A, hj, out):
    ph = Phase(nc, "moe")
    NG = JG + 1
    LOOP = (1, 14)
    K2 = 2
    w1 = ph.sb("w1", [D, NE, EF])
    w2 = ph.sb("w2", [128, NE, 2, D])
    b1 = ph.sb("b1", [128, NE, 2])
    b2 = ph.sb("b2", [NE, D])
    wg = ph.sb("wg", [D, NE])
    bg = ph.sb("bg", [128, NE])
    number = ph.sb("number", [128, NE])
    h, xn = ([ph.sb(f"{n}{p}", [128, 4, D]) for p in range(2)] for n in ("h", "xn"))
    st = ph.sb("st", [128, 4, 6])
    mv = [ph.sb(f"mv{p}", [128, 4, 2]) for p in range(2)]
    ve = ph.sb("ve", [128, 4])
    rs = [ph.sb(f"rs{p}", [128, 4]) for p in range(2)]
    uT = [ph.sb(f"uT{p}", [D, 512]) for p in range(2)]
    logits = ph.sb("logits", [128, 4, NE])
    top = ph.sb("top", [128, 4, 8])
    where = ph.sb("where", [128, 4, 8], U32)
    wheref = ph.sb("wheref", [128, 4, K2])
    diff = ph.sb("diff", [128, 4])
    share = ph.sb("share", [128, 3, 4])
    first = ph.sb("first", [128, 4])
    sel = ph.sb("sel", [128, K2, 4, NE])
    wt = [ph.sb(f"wt{p}", [128, 4, NE]) for p in range(2)]
    wtT = [ph.sb(f"wtT{p}", [NE, 512]) for p in range(2)]
    mid = [ph.sb(f"mid{q}", [128, 2, 512]) for q in range(2)]
    loaded = [ph.sem(f"loaded{p}") for p in range(2)]
    stored = [ph.sem(f"stored{p}") for p in range(2)]
    (weights, numbered, stats, var, eps_added, rstd, normed, xT, u_ready, gated, logits_ready, topped, placed, converted,
     differed, exped, chain, wt_ready, wtT_sum, wtT_ready, up, relued, down, added) = (ph.sem(n) for n in (
        "weights", "numbered", "stats", "var", "eps_added", "rstd", "normed", "xT", "u_ready", "gated", "logits_ready",
        "topped", "placed", "converted", "differed", "exped", "chain", "wt_ready", "wtT_sum", "wtT_ready", "up",
        "relued", "down", "added"))
    CHAIN = 8
    UNITS = NE + 1

    def steps(eng, step):
        def peeled(i):
            step(lambda d: ((i + d) // 2, (i + d) % 2, i + d), lambda d: 0 <= i + d < NG, lambda d, n: i + d >= n,
                 lambda d: JREM if i + d == NG - 1 else 128)
        for i in range(-1, LOOP[0]):
            peeled(i)
        with eng.Fori(0, (LOOP[1] - LOOP[0] + 1) // 2) as m:
            for r in range(2):
                c0 = LOOP[0] + r
                step(lambda d, c0=c0: (m + (c0 + d) // 2, (c0 + d) % 2, 2 * m + c0 + d), lambda d: True,
                     lambda d, n: True, lambda d: 128)
        for i in range(LOOP[1] + 1, NG):
            peeled(i)

    def group(t, n, P):
        return t[bass.ds(n * 512, 4 * P), :].rearrange("(p t) d -> p t d", t=4)
    out_rows = out.rearrange("b s d -> (b s) d")

    with nc.Block() as block:
        @block.sync
        def _(sp):
            sp.dma_start(h[0][:, :, :], group(hj, 0, 128)).then_inc(loaded[0], 16)
            sp.dma_start(wg[:, :], A["L0_ffn_gate_w"]).then_inc(weights, 16)
            sp.dma_start(bg[:, :], row(A["L0_ffn_gate_b"], 128)).then_inc(weights, 16)
            sp.dma_start(w1[:, :, :], A["L0_ffn_w1"].rearrange("e p f -> p e f")).then_inc(weights, 16)
            for c in range(2):
                sp.dma_start(w2[:, :, c, :], A["L0_ffn_w2"][:, c * 128:(c + 1) * 128, :].rearrange("e p d -> p e d"))\
                  .then_inc(weights, 16)
                sp.dma_start(b1[:, :, c], A["L0_ffn_b1"][:, c * 128:(c + 1) * 128].rearrange("e p -> p e"),
                             allow_slow_non_contiguous=True).then_inc(weights, 16)
            sp.dma_start(b2[:, :], A["L0_ffn_b2"]).then_inc(weights, 16)

            def step(at, live, old, parts):
                if live(0):
                    k, p, n = at(0)
                    sp.wait_ge(added, UNITS * (2 * k + p) + UNITS)
                    sp.dma_start(group(out_rows, n, parts(0)), h[p][0:parts(0), :, :]).then_inc(stored[p], 16)
                if live(2):
                    k, p, n = at(2)
                    if old(2, 2):
                        sp.wait_ge(stored[p], 16 * k)
                    sp.dma_start(h[p][0:parts(2), :, :], group(hj, n, parts(2))).then_inc(loaded[p], 16)
            steps(sp, step)
            for p in range(2):
                sp.wait_ge(stored[p], 16 * ((NG + 1 - p) // 2))

        @block.gpsimd
        def _(pool):
            pool.iota(number[:, :], pattern=[[1, NE]], base=0, channel_multiplier=0,
                      allow_small_or_imprecise_dtypes=True).then_inc(numbered, 1)

            def step(at, live, old, parts):
                if live(1):
                    k, p, n = at(1)
                    b, P = 2 * k + p, parts(1)
                    pool.wait_ge(var, 4 * b + 4)
                    pool.tensor_tensor(ve[0:P, :], mv[p][0:P, :, 1], C.eps[0:P, 0:4], ALU.add).then_inc(eps_added, 1)
                    pool.wait_ge(eps_added, b + 1)
                    if old(1, 2):
                        pool.wait_ge(normed, 4 * b - 4)
                    pool.tensor_tensor(rs[p][0:P, :], ve[0:P, :], C.half[0:P, 0:4], ALU.pow).then_inc(rstd, 1)
            steps(pool, step)

        @block.vector
        def _(dve):
            dve.wait_ge(weights, 128)
            dve.wait_ge(numbered, 1)

            def step(at, live, old, parts):
                def add(u):
                    k, p, n = at(0)
                    b, P = 2 * k + p, parts(0)
                    dve.wait_ge(down, UNITS * b + u + 1)
                    bank = C.bank[6 + u % 2]
                    if u == 0:
                        dve.wait_ge(normed, 4 * b + 4)
                        dve.tensor_tensor(h[p][0:P, :, :], bank[0:P, :].rearrange("p (t d) -> p t d", t=4), h[p][0:P, :, :],
                                          ALU.add).then_inc(added, 1)
                        return
                    dve.wait_ge(added, UNITS * b + u)
                    for t in range(4):
                        ins = dve.scalar_tensor_tensor(out=h[p][0:P, t, :], in0=bank[0:P, t * D:(t + 1) * D],
                                                       scalar=wt[p][0:P, t, u - 1:u], in1=h[p][0:P, t, :],
                                                       op0=ALU.mult, op1=ALU.add)
                    ins.then_inc(added, 1)
                if live(1):
                    k, p, n = at(1)
                    b, P = 2 * k + p, parts(1)
                    dve.wait_ge(loaded[p], 16 * k + 16)
                    for t in range(4):
                        dve.bn_stats(st[0:P, t, :], h[p][0:P, t, :]).then_inc(stats, 1)
                    dve.wait_ge(stats, 5 * b + 4)
                    dve.memset(C.mark[:, :], 0.0).then_inc(stats, 1)
                    for t in range(4):
                        dve.bn_aggr(mv[p][0:P, t, :], st[0:P, t, :]).then_inc(var, 1)
                if live(0):
                    for u in range(2):
                        add(u)
                if live(1):
                    dve.wait_ge(rstd, b + 1)
                    if old(1, 2):
                        dve.wait_ge(xT, b - 1)
                    for t in range(4):
                        dve.tensor_scalar(xn[p][0:P, t, :], h[p][0:P, t, :], mv[p][0:P, t, 0:1], rs[p][0:P, t:t + 1],
                                          ALU.subtract, ALU.mult).then_inc(normed, 1)
                if live(0):
                    for u in range(2, 6):
                        add(u)
                if live(1):
                    dve.wait_ge(gated, b + 1)
                    dve.tensor_tensor(logits[0:P, :, :], C.bank[1][0:P, 0:4 * NE].rearrange("p (t e) -> p t e", t=4),
                                      bg[0:P, :].unsqueeze(1).broadcast_to([P, 4, NE]), ALU.add).then_inc(logits_ready, 1)
                    dve.wait_ge(logits_ready, 2 * b + 1)
                    dve.memset(C.mark3[:, :], 0.0).then_inc(logits_ready, 1)
                    for t in range(4):
                        dve.max(top[0:P, t, :], logits[0:P, t, :]).then_inc(topped, 1)
                    dve.wait_ge(topped, 5 * b + 4)
                    dve.memset(C.mark2[:, :], 0.0).then_inc(topped, 1)
                    for t in range(4):
                        dve.max_index(where[0:P, t, :], top[0:P, t, :], logits[0:P, t, :]).then_inc(placed, 1)
                    if old(1, 1):
                        dve.wait_ge(exped, b)
                    dve.tensor_tensor(diff[0:P, :], top[0:P, :, 1], top[0:P, :, 0], ALU.subtract).then_inc(differed, 1)
                    dve.wait_ge(placed, 4 * b + 4)
                    dve.tensor_copy(wheref[0:P, :, :], where[0:P, :, 0:K2]).then_inc(converted, 1)
                if live(0):
                    add(6)
                if live(1):
                    if old(1, 2):
                        dve.wait_ge(wtT_sum, b - 1)
                    dve.wait_ge(converted, b + 1)
                    for q in range(K2):
                        dve.tensor_tensor(sel[0:P, q, :, :], number[0:P, :].unsqueeze(1).broadcast_to([P, 4, NE]),
                                          wheref[0:P, :, q:q + 1].broadcast_to([P, 4, NE]), ALU.is_equal).then_inc(chain, 1)
                    dve.wait_ge(exped, b + 1)
                    dve.tensor_scalar(share[0:P, 1, :], share[0:P, 0, :], 1.0, None, ALU.add).then_inc(chain, 1)
                    dve.wait_ge(chain, CHAIN * b + 3)
                    dve.reciprocal(first[0:P, :], share[0:P, 1, :]).then_inc(chain, 1)
                    dve.wait_ge(chain, CHAIN * b + 4)
                    dve.tensor_tensor(share[0:P, 2, :], share[0:P, 0, :], first[0:P, :], ALU.mult).then_inc(chain, 1)
                    dve.wait_ge(chain, CHAIN * b + 5)
                    for q, weight in enumerate((first[0:P, :], share[0:P, 2, :])):
                        dve.tensor_tensor(sel[0:P, q, :, :], sel[0:P, q, :, :],
                                          weight.unsqueeze(2).broadcast_to([P, 4, NE]), ALU.mult).then_inc(chain, 1)
                    dve.wait_ge(chain, CHAIN * b + 7)
                    dve.tensor_tensor(wt[p][0:P, :, :], sel[0:P, 0, :, :], sel[0:P, 1, :, :], ALU.add).then_inc(chain, 1)
                if live(0):
                    for u in range(7, UNITS):
                        add(u)
            steps(dve, step)

        @block.scalar
        def _(act):
            act.wait_ge(weights, 128)

            def step(at, live, old, parts):
                def relu(e):
                    k, p, n = at(0)
                    b, P = 2 * k + p, parts(0)
                    for f in range(2):
                        act.wait_ge(up, 2 * (NE * b + e) + f + 1)
                        if f == 0 and (e >= 2 or old(0, 1)):
                            act.wait_ge(down, UNITS * b + e)
                        act.activation(mid[e % 2][:, f, 0:4 * P], C.bank[2 + 2 * (e % 2) + f][:, 0:4 * P], ACT.Relu,
                                       bias=b1[:, e, f:f + 1]).then_inc(relued, 1)
                if live(0):
                    for e in range(3):
                        relu(e)
                if live(1):
                    k, p, n = at(1)
                    b, P = 2 * k + p, parts(1)
                    act.wait_ge(xT, b + 1)
                    act.activation(uT[p][:, 0:4 * P], C.bank[0][:, 0:4 * P], ACT.Copy).then_inc(u_ready, 1)
                if live(0):
                    for e in range(3, 6):
                        relu(e)
                if live(1):
                    act.wait_ge(differed, b + 1)
                    if old(1, 1):
                        act.wait_ge(chain, CHAIN * b)
                    act.activation(share[0:P, 0, :], diff[0:P, :], ACT.Exp).then_inc(exped, 1)
                if live(0):
                    for e in range(6, 8):
                        relu(e)
                if live(1):
                    act.wait_ge(wtT_sum, b + 1)
                    act.activation(wtT[p][:, 0:4 * P], C.bank[0][0:NE, 0:4 * P], ACT.Copy).then_inc(wtT_ready, 1)
            steps(act, step)

        @block.tensor
        def _(pe):
            pe.wait_ge(weights, 128)

            def step(at, live, old, parts):
                def first_layer(e):
                    k, p, n = at(0)
                    b, P = 2 * k + p, parts(0)
                    if e >= 2 or old(0, 1):
                        pe.wait_ge(relued, 2 * (NE * b + e) - 2)
                    for f in range(2):
                        pe.matmul(C.bank[2 + 2 * (e % 2) + f][:, 0:4 * P], w1[:, e, f * 128:(f + 1) * 128],
                                  uT[p][:, 0:4 * P], start=True, stop=True).then_inc(up, 1)

                def second_layer(e):
                    k, p, n = at(0)
                    b, P = 2 * k + p, parts(0)
                    u = e + 1
                    pe.wait_ge(relued, 2 * (NE * b + e) + 2)
                    if u >= 2 or old(0, 1):
                        pe.wait_ge(added, UNITS * b + u - 1)
                    for t in range(4):
                        for f in range(2):
                            mm = pe.matmul(C.bank[6 + u % 2][0:P, t * D:(t + 1) * D], mid[e % 2][:, f, t * P:(t + 1) * P],
                                           w2[:, e, f, :], start=(f == 0), stop=(f == 1))
                    mm.then_inc(down, 1)
                if live(0):
                    k, p, n = at(0)
                    b, P = 2 * k + p, parts(0)
                    first_layer(0)
                    pe.wait_ge(wtT_ready, b + 1)
                    if old(0, 1):
                        pe.wait_ge(added, UNITS * b)
                    for t in range(4):
                        mm = pe.matmul(C.bank[6][0:P, t * D:(t + 1) * D], wtT[p][:, t * P:(t + 1) * P], b2[:, :],
                                       start=True, stop=True)
                    mm.then_inc(down, 1)
                    for e in range(3):
                        first_layer(e + 1)
                        second_layer(e)
                if live(1):
                    k, p, n = at(1)
                    b, P = 2 * k + p, parts(1)
                    pe.wait_ge(normed, 4 * b + 4)
                    if old(1, 1):
                        pe.wait_ge(wtT_ready, b)
                    for t in range(4):
                        mm = pe.transpose(C.bank[0][:, t * P:(t + 1) * P], xn[p][0:P, t, :], C.ident[0:P, 0:P])
                    mm.then_inc(xT, 1)
                if live(0):
                    first_layer(4)
                    second_layer(3)
                if live(1):
                    pe.wait_ge(u_ready, b + 1)
                    if old(1, 1):
                        pe.wait_ge(logits_ready, 2 * b)
                    for t in range(4):
                        mm = pe.matmul(C.bank[1][0:P, t * NE:(t + 1) * NE], uT[p][:, t * P:(t + 1) * P], wg[:, :],
                                       start=True, stop=True)
                    mm.then_inc(gated, 1)
                if live(0):
                    for e in range(4, 7):
                        first_layer(e + 1)
                        second_layer(e)
                    second_layer(7)
                if live(1):
                    pe.wait_ge(chain, CHAIN * b + 8)
                    for t in range(4):
                        mm = pe.transpose(C.bank[0][0:NE, t * P:(t + 1) * P], wt[p][0:P, t, :], C.ident[0:P, 0:P])
                    mm.then_inc(wtT_sum, 1)
            steps(pe, step)
    ph.close()


class Consts:
    pass


def make_consts(nc, ctx):
    C = Consts()
    C.bank = [ctx.enter_context(nc.psum_tensor(f"bank{i}", [128, 512], F32)) for i in range(8)]
    C.ident = ctx.enter_context(nc.sbuf_tensor("ident", [128, 128], F32))
    C.ones = ctx.enter_context(nc.sbuf_tensor("ones", [128, NTP * PAIRS], F32))
    C.zeros = ctx.enter_context(nc.sbuf_tensor("zeros", [1, NTP * PAIRS], F32))
    C.eps = ctx.enter_context(nc.sbuf_tensor("eps", [128, 8], F32))
    C.mark = ctx.enter_context(nc.sbuf_tensor("mark", [1, 1], F32))
    C.mark2 = ctx.enter_context(nc.sbuf_tensor("mark2", [1, 1], F32))
    C.mark3 = ctx.enter_context(nc.sbuf_tensor("mark3", [1, 1], F32))
    C.half = ctx.enter_context(nc.sbuf_tensor("half", [128, 8], F32))
    return C


def build_program(nc, A, out):
    hv = nc.dram_tensor("hv", (VROWS + 2, D), F32, kind="Internal").ap()
    txt_dram = nc.dram_tensor("txt_dram", (NB, T, D), F32, kind="Internal").ap()
    hj = nc.dram_tensor("hj", (JROWS, D), F32, kind="Internal").ap()
    rows_dram = nc.dram_tensor("rows_dram", (3, NB, T), F32, kind="Internal").ap()
    bounce = [nc.dram_tensor(f"bounce{p}", (6, 2, HD, PAIRS, NTP), F32, kind="Internal").ap() for p in range(2)]
    with ExitStack() as ctx:
        C = make_consts(nc, ctx)
        build_constants(nc, C, hv)
        build_texts(nc, C, A, rows_dram, txt_dram)
        build_patches(nc, C, A, hv)
        with nc.Fori(0, DEPTH) as layer:
            build_attention(nc, C, A, hv, bounce, layer)
            build_mlp(nc, C, A, hv, layer)
        build_joint(nc, C, A, hv, txt_dram, hj)
        build_experts(nc, C, A, hj, out)


_INS = ["x", "x_txt", "L0_tok_conv_w", "L0_tok_conv_b", "L0_tok_cls_token", "L0_tok_pos_embed", "L0_tok_ln1_w",
        "L0_tok_ln1_b", "L0_tok_qkv_w", "L0_tok_qkv_b", "L0_tok_proj_w", "L0_tok_proj_b", "L0_tok_ln2_w",
        "L0_tok_ln2_b", "L0_tok_fc1_w", "L0_tok_fc1_b", "L0_tok_fc2_w", "L0_tok_fc2_b", "L0_tok_norm_w",
        "L0_tok_norm_b", "L0_txt_p", "L0_attn_wq", "L0_attn_wk", "L0_attn_wv", "L0_attn_wo", "L0_attn_w1",
        "L0_attn_b1", "L0_attn_w2", "L0_attn_b2", "L0_ffn_gate_w", "L0_ffn_gate_b", "L0_ffn_w1", "L0_ffn_b1",
        "L0_ffn_w2", "L0_ffn_b2"]


def kernel(**inputs):
    import numpy as _np
    import concourse.bacc as _bacc
    from concourse import mybir as _mybir
    from concourse.bass_utils import run_bass_kernel_spmd as _run

    nc = _bacc.Bacc("TRN2", target_bir_lowering=False, num_devices=1)
    arrays, A = {}, {}
    for name in _INS:
        a = _np.ascontiguousarray(inputs[name])
        arrays[f"in_{name}_dram"] = a
        A[name] = nc.dram_tensor(f"in_{name}_dram", a.shape, _mybir.dt.from_np(a.dtype), kind="ExternalInput").ap()
    out = nc.dram_tensor("out_0_dram", (NB, S, D), _mybir.dt.float32, kind="ExternalOutput").ap()
    build_program(nc, A, out)
    r = _run(nc, [arrays], core_ids=[0])
    return r.results[0]["out_0_dram"]
```

```python
from contextlib import ExitStack

import concourse.bass as bass
from concourse import mybir

F32 = mybir.dt.float32
F32R = mybir.dt.float32r
BF16 = mybir.dt.bfloat16
I32 = mybir.dt.int32
U32 = mybir.dt.uint32
ALU = mybir.AluOpType
ACT = mybir.ActivationFunctionType
AX = mybir.AxisListType

NB = 32
IMG, PT = 224, 16
GRID = IMG // PT
D = 128
HEADS, HD = 8, 16
PAIRS = HEADS // 2
DEPTH = 4
HID = 256
NT = GRID * GRID + 1
T = 77
S = NT + T
DI = 512
NE = 8
EF = 256
EPS = 1e-5
END_TOKEN = 2

CP = (NT + 1) // 2
NTP = 2 * CP
KROWS = (CP, NT - CP)

PARTS = 3 * 2 * HD
GUARD = 112
STACK_DMAS = 16 * 7
STACKS = 6

VROWS = NB * NT
VG = VROWS // 512
VREM = VROWS % 512 // 4
JROWS = NB * S
JG = JROWS // 512
JREM = JROWS % 512 // 4


def row(ap, parts):
    return ap.rearrange("(a n) -> a n", a=1).broadcast_to([parts, ap.shape[0]])


def image(hv, b):
    return hv[bass.ds(b * NT, NTP), :].rearrange("(p c) d -> p c d", c=2)


class Phase:

    def __init__(self, nc, name):
        self.nc, self.name, self.ctx, self.sems = nc, name, ExitStack(), []

    def sb(self, name, shape, dt=F32):
        return self.ctx.enter_context(self.nc.sbuf_tensor(f"{self.name}_{name}", shape, dt))

    def sem(self, name):
        s = self.ctx.enter_context(self.nc.semaphore(f"{self.name}_{name}"))
        self.sems.append(s)
        return s

    def close(self):
        with self.nc.Block() as block:
            @block.sync
            def _(sp):
                for s in self.sems:
                    sp.sem_clear(s)
        self.ctx.close()


def build_constants(nc, C, hv):
    ph = Phase(nc, "const")
    filled, selected, stored = ph.sem("filled"), ph.sem("selected"), ph.sem("stored")
    with nc.Block() as block:
        @block.gpsimd
        def _(pool):
            pool.memset(C.ident[:, :], 0.0).then_inc(filled, 1)
            pool.memset(C.ones[:, :], 1.0).then_inc(filled, 1)
            pool.memset(C.zeros[:, :], 0.0).then_inc(filled, 1)
            pool.memset(C.half[:, :], -0.5).then_inc(filled, 1)
            pool.memset(C.eps[:, :], EPS).then_inc(filled, 1)
            pool.wait_ge(filled, 5)
            pool.affine_select(out=C.ident[:, :], in_=C.ident[:, :], compare_op=ALU.not_equal, fill=1.0,
                               base=0, pattern=[[-1, 128]], channel_multiplier=1).then_inc(selected, 1)

        @block.sync
        def _(sp):
            sp.wait_ge(filled, 5)
            sp.dma_start(hv[VROWS:VROWS + 1, :], C.zeros[0:1, 0:D]).then_inc(stored, 16)
            sp.wait_ge(stored, 16)
            sp.wait_ge(selected, 1)
    ph.close()


def build_texts(nc, C, A, rows_dram, txt_dram):
    ph = Phase(nc, "txt")
    tok = ph.sb("tok", [NB, T], I32)
    tf = ph.sb("tf", [NB, 8, T])
    ti = ph.sb("ti", [NB, 2, T], I32)
    order_bc = ph.sb("order_bc", [T, NB, T])
    parent_bc = ph.sb("parent_bc", [T, NB, T])
    cols = ph.sb("cols", [T, 3, NB])
    P = ph.sb("P", [T, 2, NB, T], BF16)
    Q = ph.sb("Q", [T, 2, NB, T], BF16)
    X = ph.sb("X", [T, NB, D], BF16)
    res = ph.sb("res", [T, NB, D])
    poly = ph.sb("poly", [T, D])
    pw = ph.sb("pw", [T, 8])
    loaded, seq, rows_out, rows_in = ph.sem("loaded"), ph.sem("seq"), ph.sem("rows_out"), ph.sem("rows_in")
    built, zeroed, xmm, xcp, pmm, pcp = (ph.sem(n) for n in ("built", "zeroed", "xmm", "xcp", "pmm", "pcp"))
    poly_ready, pseq, res_ready, stored = ph.sem("poly_ready"), ph.sem("pseq"), ph.sem("res_ready"), ph.sem("stored")
    GT = 6
    groups = [(a, min(a + GT, NB)) for a in range(0, NB, GT)]
    STEPS = 6
    SEQ = 16

    with nc.Block() as block:
        @block.sync
        def _(sp):
            sp.dma_start(tok[:, :], A["x_txt"]).then_inc(loaded, 16)
            sp.dma_start(pw[:, 0:1], row(A["L0_txt_p"], T)).then_inc(loaded, 16)
            sp.wait_ge(seq, SEQ)
            for r in range(3):
                sp.dma_start(rows_dram[r], tf[:, 5 + r, :]).then_inc(rows_out, 16)
            sp.wait_ge(rows_out, 48)
            for r, dst in ((0, order_bc), (1, parent_bc)):
                sp.dma_start(dst[:, :, :], rows_dram[r:r + 1].broadcast_to([T, NB, T])).then_inc(rows_in, 16)
            for r in range(3):
                sp.dma_start(cols[:, r, :], rows_dram[r].rearrange("b t -> t b"), allow_slow_non_contiguous=True).then_inc(rows_in, 16)
            sp.wait_ge(res_ready, 1)
            sp.dma_start(txt_dram.rearrange("b t d -> t b d"), res[:, :, :]).then_inc(stored, 16)
            sp.wait_ge(stored, 16)

        @block.gpsimd
        def _(pool):
            pool.memset(X[:, :, :], 0.0).then_inc(zeroed, 1)

        @block.vector
        def _(dve):
            done = [0]

            def step(ins):
                done[0] += 1
                ins.then_inc(seq, 1)
                dve.wait_ge(seq, done[0])

            tokf, push, gain, length, pushes, order, parent, side = (tf[:, r, :] for r in range(8))
            dve.wait_ge(loaded, 32)
            step(dve.tensor_copy(tokf, tok[:, :]))
            step(dve.tensor_scalar(push, tokf, float(END_TOKEN), None, ALU.not_equal))
            step(dve.memset(push[:, 0:1], 1.0))
            step(dve.tensor_scalar(gain, push, 2.0, -1.0, ALU.mult, ALU.add))
            step(dve.memset(tokf, 1.0))
            step(dve.tensor_tensor_scan(length, gain, tokf, 1.0, ALU.add, ALU.max))
            step(dve.memset(tokf, 0.0))
            step(dve.tensor_tensor_scan(pushes, push, tokf, 0.0, ALU.add, ALU.add))
            step(dve.tensor_tensor(order, pushes, push, ALU.mult))
            step(dve.scalar_tensor_tensor(out=ti[:, 0, 1:T], in0=pushes[:, 0:T - 1], scalar=2.0,
                                          in1=length[:, 0:T - 1], op0=ALU.mult, op1=ALU.subtract))
            step(dve.tensor_scalar(ti[:, 1, 1:T], ti[:, 0, 1:T], 1, None, ALU.bitwise_and))
            step(dve.tensor_copy(side[:, 1:T], ti[:, 1, 1:T]))
            step(dve.tensor_scalar(ti[:, 1, 1:T], ti[:, 0, 1:T], 1, None, ALU.arith_shift_right))
            step(dve.tensor_scalar(parent[:, 1:T], ti[:, 1, 1:T], 1.0, None, ALU.add))
            step(dve.memset(parent[:, 0:1], -1.0))
            step(dve.memset(side[:, 0:1], 2.0))
            assert done[0] == SEQ

            dve.wait_ge(rows_in, 80)
            dve.tensor_tensor(P[:, 0, :, :], order_bc[:, :, :], cols[:, 1, :].unsqueeze(2).broadcast_to([T, NB, T]),
                              ALU.is_equal).then_inc(built, 1)
            dve.tensor_tensor(Q[:, 0, :, :], parent_bc[:, :, :], cols[:, 0, :].unsqueeze(2).broadcast_to([T, NB, T]),
                              ALU.is_equal).then_inc(built, 1)
            dve.wait_ge(zeroed, 1)
            for k in range(2):
                dve.tensor_scalar(X[:, :, k:k + 1], cols[:, 2, :].unsqueeze(2), float(k), None,
                                  ALU.is_equal).then_inc(built, 1)
            dve.memset(poly[:, 0:1], 1.0).then_inc(pseq, 1)
            for k in range(7):
                n = 1 << k
                dve.wait_ge(pseq, 2 * k + 1)
                dve.tensor_scalar(poly[:, n:2 * n], poly[:, 0:n], pw[:, k:k + 1], None, ALU.mult).then_inc(pseq, 1)
                dve.tensor_tensor(pw[:, k + 1:k + 2], pw[:, k:k + 1], pw[:, k:k + 1], ALU.mult).then_inc(pseq, 1)

            px = 0
            for s in range(STEPS):
                w = 2 << s
                for a in range(0, NB, 8):
                    px += 1
                    dve.wait_ge(xmm, px)
                    bank = C.bank[(px - 1) % 2]
                    dve.tensor_copy(X[:, a:a + 8, w:2 * w], bank[0:T, 0:8 * w].rearrange("p (b w) -> p b w", b=8))\
                       .then_inc(xcp, 1)
            dve.wait_ge(xcp, px)
            dve.wait_ge(pseq, 15)
            dve.tensor_tensor(res[:, :, :], X[:, :, :], poly[:, :].unsqueeze(1).broadcast_to([T, NB, D]),
                              ALU.mult).then_inc(res_ready, 1)

        @block.scalar
        def _(act):
            n = 0
            for s in range(STEPS - 1):
                for a, z in groups:
                    for M in (P, Q):
                        act.wait_ge(pmm, n + 1)
                        act.activation(M[:, (s + 1) % 2, a:z, :],
                                       C.bank[2 + n % 6][0:T, 0:(z - a) * T].rearrange("p (b t) -> p b t", t=T),
                                       ACT.Copy).then_inc(pcp, 1)
                        n += 1

        @block.tensor
        def _(pe):
            pe.wait_ge(built, 4)
            px = n = 0
            for s in range(STEPS):
                w = 2 << s
                if s:
                    pe.wait_ge(pcp, n)
                    pe.wait_ge(xcp, px)
                for a in range(0, NB, 8):
                    if px >= 2:
                        pe.wait_ge(xcp, px - 1)
                    for b in range(8):
                        mm = pe.matmul(C.bank[px % 2][0:T, b * w:(b + 1) * w], Q[:, s % 2, a + b, :],
                                       X[:, a + b, 0:w], start=True, stop=True)
                    mm.then_inc(xmm, 1)
                    px += 1
                if s == STEPS - 1:
                    break
                for a, z in groups:
                    for L, R in ((Q, P), (P, Q)):
                        if n >= 6:
                            pe.wait_ge(pcp, n - 5)
                        for b in range(a, z):
                            mm = pe.matmul(C.bank[2 + n % 6][0:T, (b - a) * T:(b - a + 1) * T], L[:, s % 2, b, :],
                                           R[:, s % 2, b, :], start=True, stop=True)
                        mm.then_inc(pmm, 1)
                        n += 1
    ph.close()


def build_patches(nc, C, A, hv):
    ph = Phase(nc, "px")
    HP = PT // 2
    RW = 3 * PT
    RIGHT = 64
    ROWS = RIGHT + RW
    TP = GRID * GRID // 2
    BUFS = 4
    img = [ph.sb(f"img{q}", [ROWS, GRID, IMG]) for q in range(BUFS)]
    w = ph.sb("w", [ROWS, HP, D])
    pos = ph.sb("pos", [TP, 2, D])
    bias = ph.sb("bias", [TP, D])
    first = ph.sb("first", [NB, 2, D])
    emb = [ph.sb(f"emb{q}", [TP, 2, D]) for q in range(BUFS)]
    weights = ph.sem("weights")
    loaded = [ph.sem(f"loaded{q}") for q in range(BUFS)]
    stored = [ph.sem(f"stored{q}") for q in range(BUFS)]
    w_zero, img_zero, copied, summed, pos_ready, added, cls_ready, cls_out = (ph.sem(n) for n in (
        "w_zero", "img_zero", "copied", "summed", "pos_ready", "added", "cls_ready", "cls_out"))

    with nc.Block() as block:
        @block.sync
        def _(sp):
            def load_image(b, q):
                for c in range(3):
                    sp.dma_start(img[q][PT * c:PT * c + PT, :, :],
                                 A["x"][bass.ds(b, 1), c, :, :].rearrange("o (g r) w -> r (o g) w", r=PT))\
                      .then_inc(loaded[q], 16)

            def store(b, q):
                sp.wait_ge(added, b + 1)
                sp.dma_start(hv[bass.ds(b * NT + 1, NT - 1), :].rearrange("(c p) d -> p c d", c=2),
                             emb[q][:, :, :]).then_inc(stored[q], 16)
            for q in range(BUFS):
                sp.wait_ge(img_zero, q + 1)
                load_image(q, q)
            sp.wait_ge(w_zero, 1)
            cw = A["L0_tok_conv_w"].rearrange("(r x) d -> r x d", x=PT)
            for half in range(2):
                sp.dma_start(w[RIGHT * half:RIGHT * half + RW, :, :], cw[:, HP * half:HP * half + HP, :]).then_inc(weights, 16)
            position = A["L0_tok_pos_embed"][0]
            sp.dma_start(pos[:, :, :], position[1:NT, :].rearrange("(c p) d -> p c d", c=2)).then_inc(weights, 16)
            sp.dma_start(bias[:, :], row(A["L0_tok_conv_b"], TP)).then_inc(weights, 16)
            sp.dma_start(first[:, 0, :], A["L0_tok_cls_token"][0].broadcast_to([NB, D])).then_inc(weights, 16)
            sp.dma_start(first[:, 1, :], position[0:1, :].broadcast_to([NB, D])).then_inc(weights, 16)
            with sp.Fori(1, NB // BUFS) as k:
                for q in range(BUFS):
                    sp.wait_ge(summed, BUFS * k + q - BUFS + 1)
                    load_image(BUFS * k + q, q)
                    store(BUFS * k + q - BUFS, q)
            for q in range(BUFS):
                store(NB - BUFS + q, q)
            sp.wait_ge(cls_ready, 1)
            sp.dma_start(hv[0:VROWS, :].rearrange("(b t) d -> b t d", t=NT)[:, 0, :], first[:, 0, :]).then_inc(cls_out, 16)
            sp.wait_ge(cls_out, 16)
            for q in range(BUFS):
                sp.wait_ge(stored[q], 16 * NB // BUFS)

        @block.gpsimd
        def _(pool):
            pool.memset(w[32:64, :, :], 0.0).then_inc(w_zero, 1)

        @block.scalar
        def _(act):
            def copy(k, q, again):
                act.wait_ge(loaded[q], 48 * k + 48)
                if again:
                    act.wait_ge(summed, BUFS * k + q - BUFS + 1)
                patches = img[q][:, :, :].rearrange("p g (q x) -> p (g q) x", x=PT)
                act.activation(patches[RIGHT:ROWS, :, 0:HP], patches[0:RW, :, HP:PT], ACT.Copy).then_inc(copied, 1)
            for q in range(BUFS):
                copy(0, q, False)
            with act.Fori(1, NB // BUFS) as k:
                for q in range(BUFS):
                    copy(k, q, True)

        @block.tensor
        def _(pe):
            pe.wait_ge(weights, 96)

            def embed(k, q, again):
                pe.wait_ge(copied, BUFS * k + q + 1)
                if again:
                    pe.wait_ge(added, BUFS * k + q - BUFS + 1)
                for c in range(2):
                    for x in range(HP):
                        mm = pe.matmul(C.bank[q][0:TP, c * D:(c + 1) * D],
                                       img[q][:, 7 * c:7 * c + 7, x:x + PT * (GRID - 1) + 1:PT], w[:, x, :],
                                       start=(x == 0), stop=(x == HP - 1))
                mm.then_inc(summed, 1)
            for q in range(BUFS):
                embed(0, q, False)
            with pe.Fori(1, NB // BUFS) as k:
                for q in range(BUFS):
                    embed(k, q, True)

        @block.vector
        def _(dve):
            for q in range(BUFS):
                dve.memset(img[q][32:64, :, :], 0.0).then_inc(img_zero, 1)
            dve.wait_ge(weights, 96)
            dve.tensor_tensor(pos[:, :, :], pos[:, :, :], bias[:, :].unsqueeze(1).broadcast_to([TP, 2, D]),
                              ALU.add).then_inc(pos_ready, 1)
            dve.tensor_tensor(first[:, 0, :], first[:, 0, :], first[:, 1, :], ALU.add).then_inc(cls_ready, 1)
            dve.wait_ge(pos_ready, 1)

            def add(k, q, again):
                dve.wait_ge(summed, BUFS * k + q + 1)
                if again:
                    dve.wait_ge(stored[q], 16 * k)
                dve.tensor_tensor(emb[q][:, :, :], C.bank[q][0:TP, 0:2 * D].rearrange("p (c d) -> p c d", c=2),
                                  pos[:, :, :], ALU.add).then_inc(added, 1)
            for q in range(BUFS):
                add(0, q, False)
            with dve.Fori(1, NB // BUFS) as k:
                for q in range(BUFS):
                    add(k, q, True)
    ph.close()


def build_stacks(nc, C, ctx):
    def sb(name, shape, dt=F32):
        return ctx.enter_context(nc.sbuf_tensor(name, shape, dt))
    C.vblk = [sb(f"vblk{q}", [CP, 2, HEADS, 2 * HD]) for q in range(STACKS)]
    C.oblk = sb("oblk", [CP, 2, 2 * HD])
    C.qst = [sb(f"qst{q}", [128, PAIRS, NTP], F32R) for q in range(STACKS)]
    C.kst = [[sb(f"kst{q}{j}", [128, PAIRS, NTP], F32R) for j in range(2)] for q in range(STACKS)]
    ph = Phase(nc, "stacks")
    k_zero, rest_zero, ones_in = ph.sem("k_zero"), ph.sem("rest_zero"), ph.sem("ones_in")
    with nc.Block() as block:
        @block.gpsimd
        def _(pool):
            for q in range(STACKS):
                pool.memset(C.qst[q][:, :, :].bitcast(F32), 0.0).then_inc(rest_zero, 1)
                pool.memset(C.vblk[q][:, :, :, :], 0.0).then_inc(rest_zero, 1)
            pool.memset(C.oblk[:, :, :], 0.0).then_inc(rest_zero, 1)
            pool.wait_ge(rest_zero, 2 * STACKS + 1)
            for j in range(2):
                pool.memset(C.oblk[:, j, HD * j:HD * j + HD], 1.0).then_inc(rest_zero, 1)

        @block.vector
        def _(dve):
            for q in range(STACKS):
                for j in range(2):
                    dve.memset(C.kst[q][j][:, :, :].bitcast(F32), 0.0).then_inc(k_zero, 1)

        @block.sync
        def _(sp):
            for q in range(STACKS):
                sp.wait_ge(k_zero, 2 * q + 2)
                for j in range(2):
                    sp.dma_start(C.kst[q][j][GUARD + j:GUARD + j + 1, :, :].bitcast(F32),
                                 C.ones[0:1, :].rearrange("o (g t) -> o g t", g=PAIRS)).then_inc(ones_in, 16)
            sp.wait_ge(ones_in, 32 * STACKS)
            sp.wait_ge(rest_zero, 2 * STACKS + 3)
    ph.close()


def build_attention(nc, C, A, hv, bounce, layer):
    ph = Phase(nc, "att")
    w_qkv = ph.sb("w_qkv", [D, 3 * D])
    w_turned = ph.sb("w_turned", [D, 2, 2, HD, PAIRS])
    w_proj = ph.sb("w_proj", [D, D])
    ln = ph.sb("ln", [D, 2])
    b_qk = ph.sb("b_qk", [D, 2])
    b_v = ph.sb("b_v", [128, D])
    b_proj = ph.sb("b_proj", [128, D])
    ha = [ph.sb(f"ha{p}", [CP, 2, D]) for p in range(2)]
    hr = [ph.sb(f"hr{p}", [CP, 2, D]) for p in range(3)]
    xn = [ph.sb(f"xn{p}", [CP, 2, D]) for p in range(2)]
    st = ph.sb("st", [CP, 2, 6])
    mv = [ph.sb(f"mv{p}", [CP, 2, 2]) for p in range(2)]
    ve = ph.sb("ve", [CP, 2])
    rs = [ph.sb(f"rs{p}", [CP, 2]) for p in range(2)]
    yT = [ph.sb(f"yT{p}", [D, NTP]) for p in range(2)]
    Q_LO, Q_HI, K_LO, K_HI = range(4)
    parts = [ph.sb(f"parts{p}", [D, 4, NTP], F32R) for p in range(2)]
    vblk, oblk, qst, kst = C.vblk, C.oblk, C.qst, C.kst
    negm = [ph.sb(f"negm{p}", [CP, 2, HEADS]) for p in range(2)]
    gmax = ph.sb("gmax", [HEADS, NTP], F32R)
    E = [ph.sb(f"E{c}", [CP, PAIRS, 2, NTP]) for c in range(2)]
    rden = ph.sb("rden", [D, NTP])
    oT = [ph.sb(f"oT{p}", [D, NTP]) for p in range(2)]

    weights, turned = ph.sem("weights"), ph.sem("turned")
    ha_in = [ph.sem(f"ha_in{p}") for p in range(2)]
    hr_in = [ph.sem(f"hr_in{p}") for p in range(2)]
    bounced = [ph.sem(f"bounced{p}") for p in range(2)]
    stacked = [ph.sem(f"stacked{p}") for p in range(2)]
    guarded = [ph.sem(f"guarded{p}") for p in range(2)]
    stored = [ph.sem(f"stored{p}") for p in range(2)]
    (stats, var, eps_added, rstd, normed, xT, y_ready, qk, v_sum, hi, lo, v_ready, max_sum, maxed, gT, g_ready,
     s_sum, exped, pv, rden_ready, o_ready, projected, biased, summed) = (ph.sem(n) for n in (
        "stats", "var", "eps_added", "rstd", "normed", "xT", "y_ready", "qk", "v_sum", "hi", "lo", "v_ready",
        "max_sum", "maxed", "gT", "g_ready", "s_sum", "exped", "pv", "rden_ready", "o_ready", "projected",
        "biased", "summed"))

    FIRST, LAST = 3, 20

    def steps(eng, step):
        def peeled(i):
            def at(d):
                return (i + d) // 2, (i + d) % 2, i + d, (i + d) % STACKS
            step(at, lambda d: 0 <= i + d < NB, lambda d, n: i + d >= n)

        def looped(m, r):
            def at(d):
                c = FIRST + r + d
                return STACKS // 2 * m + c // 2, c % 2, STACKS * m + c, c % STACKS
            step(at, lambda d: True, lambda d, n: True)
        for i in range(-5, FIRST):
            peeled(i)
        with eng.Fori(0, (LAST - FIRST + 1) // STACKS) as m:
            for r in range(STACKS):
                looped(m, r)
        for i in range(LAST + 1, NB + 2):
            peeled(i)

    with nc.Block() as block:
        @block.sync
        def _(sp):
            def of(nm):
                return A["L0_tok_" + nm][bass.ds(layer, 1)]
            sp.dma_start(ha[0][:, :, :], image(hv, 0)).then_inc(ha_in[0], 16)
            sp.dma_start(w_qkv[:, :], of("qkv_w").rearrange("o p n -> (o p) n")).then_inc(weights, 16)
            sp.dma_start(w_proj[:, :], of("proj_w").rearrange("o p n -> (o p) n")).then_inc(weights, 16)
            for k, nm in enumerate(("ln1_w", "ln1_b")):
                sp.dma_start(ln[:, k:k + 1], of(nm).rearrange("o p -> p o"), allow_slow_non_contiguous=True)\
                  .then_inc(weights, 16)
            for k in range(2):
                by_side = of("qkv_b")[:, k * D:(k + 1) * D].rearrange("o (g j d) -> j d g o", j=2, d=HD)
                for j in range(2):
                    sp.dma_start(b_qk[64 * j:64 * j + 64, k:k + 1], by_side[j], allow_slow_non_contiguous=True)\
                      .then_inc(weights, 16)
            sp.dma_start(b_v[:, :], of("qkv_b")[:, 2 * D:3 * D].broadcast_to([128, D])).then_inc(weights, 16)
            sp.dma_start(b_proj[:, :], of("proj_b").broadcast_to([128, D])).then_inc(weights, 16)
            def step(at, live, old):
                if live(-2):
                    k, p, n, q4 = at(-2)
                    sp.wait_ge(summed, 2 * k + p + 1)
                    sp.dma_start(hv[bass.ds(n * NT, NT - 1), :].rearrange("(p c) d -> p c d", c=2),
                                 hr[q4 % 3][0:CP - 1, :, :]).then_inc(stored[p], 16)
                    sp.dma_start(hv[bass.ds(n * NT + NT - 1, 1), :], hr[q4 % 3][CP - 1:CP, 0, :]).then_inc(stored[p], 16)
                if live(0):
                    k, p, n, q4 = at(0)
                    if old(0, 3):
                        sp.wait_ge(stored[1 - p], 32 * (k - 1 + p))
                    sp.dma_start(hr[q4 % 3][:, :, :], image(hv, n)).then_inc(hr_in[p], 16)
                if live(6):
                    k, p, n, q4 = at(6)
                    if old(6, 2):
                        sp.wait_ge(normed, 2 * (2 * k + p) - 2)
                    sp.dma_start(ha[p][:, :, :], image(hv, n)).then_inc(ha_in[p], 16)
                if live(1):
                    k, p, n, q4 = at(1)
                    sp.wait_ge(g_ready, 2 * k + p + 1)
                    sp.dma_start(qst[q4][GUARD:GUARD + 2, :, :].bitcast(F32), gmax[:, :].bitcast(F32))\
                      .then_inc(guarded[p], 16)
                if live(3):
                    k, p, n, q4 = at(3)
                    sp.wait_ge(bounced[p], 32 * k + 32)
                    if old(3, STACKS):
                        sp.wait_ge(s_sum, 8 * (2 * k + p) - 8 * STACKS + 8)
                    sp.dma_start(qst[q4][0:PARTS, :, :].bitcast(F32), bounce[p][0:3].rearrange("s j d g t -> (s j d) g t"))\
                      .then_inc(stacked[p], 16)
                    for j in range(2):
                        for s in range(3):
                            r = 32 * s + HD * j
                            sp.dma_start(kst[q4][j][r:r + HD, :, :].bitcast(F32), bounce[p][3 + s, j])\
                              .then_inc(stacked[p], 16)
            steps(sp, step)
            for p in range(2):
                sp.wait_ge(stored[p], 32 * NB // 2)

        @block.gpsimd
        def _(pool):
            pool.wait_ge(weights, 160)

            def step(at, live, old):
                if live(5):
                    k, p, n, q4 = at(5)
                    pool.wait_ge(var, 2 * (2 * k + p) + 2)
                    pool.tensor_tensor(ve[:, :], mv[p][:, :, 1], C.eps[0:CP, 0:2], ALU.add).then_inc(eps_added, 1)
                    pool.wait_ge(eps_added, 2 * k + p + 1)
                    if old(5, 2):
                        pool.wait_ge(normed, 2 * (2 * k + p) - 2)
                    pool.tensor_tensor(rs[p][:, :], ve[:, :], C.half[0:CP, 0:2], ALU.pow).then_inc(rstd, 1)
                if live(-1):
                    k, p, n, q4 = at(-1)
                    pool.wait_ge(hr_in[p], 16 * k + 16)
                    pool.tensor_tensor(hr[q4 % 3][:, :, :], hr[q4 % 3][:, :, :],
                                       b_proj[0:CP, :].unsqueeze(1).broadcast_to([CP, 2, D]), ALU.add)\
                        .then_inc(biased, 1)
            steps(pool, step)

        @block.vector
        def _(dve):
            dve.wait_ge(weights, 160)
            for q in range(2):
                for j in range(2):
                    dve.tensor_copy(w_turned[:, q, j, :, :],
                                    w_qkv[:, q * D:(q + 1) * D].rearrange("p (g j d) -> p j d g", j=2, d=HD)[:, j, :, :])\
                       .then_inc(turned, 1)

            def step(at, live, old):
                def maximum(u):
                    k, p, n, q4 = at(2)
                    b = 2 * k + p
                    dve.wait_ge(max_sum, 8 * b + u + 1)
                    if u == 0 and old(2, 2):
                        dve.wait_ge(gT, b - 1)
                    c, g = u // PAIRS, u % PAIRS
                    src = C.bank[2 + u % 2][0:CP, 0:2 * NTP].rearrange("p (j t) -> p j t", j=2)[:, :, 0:NT]
                    dve.tensor_reduce(negm[p][:, c, g::PAIRS], src, AX.X, ALU.max, negate=True).then_inc(maxed, 1)
                if live(2):
                    maximum(0)
                if live(5):
                    k, p, n, q4 = at(5)
                    b = 2 * k + p
                    dve.wait_ge(ha_in[p], 16 * k + 16)
                    for c in range(2):
                        dve.bn_stats(st[:, c, :], ha[p][:, c, :]).then_inc(stats, 1)
                if live(2):
                    maximum(1)
                if live(5):
                    k, p, n, q4 = at(5)
                    b = 2 * k + p
                    dve.wait_ge(stats, 3 * b + 2)
                    dve.memset(C.mark[:, :], 0.0).then_inc(stats, 1)
                    for c in range(2):
                        dve.bn_aggr(mv[p][:, c, :], st[:, c, :]).then_inc(var, 1)
                if live(2):
                    maximum(2)
                if live(-1):
                    k, p, n, q4 = at(-1)
                    b = 2 * k + p
                    dve.wait_ge(pv, 2 * b + 2)
                    dve.reciprocal(rden[:, :], C.bank[4][:, NTP:2 * NTP]).then_inc(rden_ready, 1)
                if live(2):
                    maximum(3)
                if live(-1):
                    k, p, n, q4 = at(-1)
                    b = 2 * k + p
                    dve.wait_ge(rden_ready, b + 1)
                    if old(-1, 2):
                        dve.wait_ge(projected, b - 1)
                    dve.tensor_tensor(oT[p][:, :], C.bank[4][:, 0:NTP], rden[:, :], ALU.mult).then_inc(o_ready, 1)
                if live(2):
                    for u in range(4, 6):
                        maximum(u)
                if live(5):
                    k, p, n, q4 = at(5)
                    b = 2 * k + p
                    dve.wait_ge(rstd, b + 1)
                    if old(5, 2):
                        dve.wait_ge(xT, b - 1)
                    for c in range(2):
                        dve.tensor_scalar(xn[p][:, c, :], ha[p][:, c, :], mv[p][:, c, 0:1], rs[p][:, c:c + 1],
                                          ALU.subtract, ALU.mult).then_inc(normed, 1)
                if live(4):
                    k, p, n, q4 = at(4)
                    b = 2 * k + p
                    dve.wait_ge(v_sum, b + 1)
                    if old(4, STACKS):
                        dve.wait_ge(pv, 2 * b - 2 * STACKS + 2)
                    for j in range(2):
                        out = vblk[q4][:, :, j::2, HD * j:HD * j + HD]
                        src = C.bank[5][0:CP, 2 * D:4 * D].rearrange("p (c g j d) -> p c g j d", c=2, j=2, d=HD)
                        bias = b_v[0:CP, :].rearrange("p (g j d) -> p g j d", j=2, d=HD)[:, :, j, :]
                        dve.tensor_tensor(out, src[:, :, :, j, :], bias.unsqueeze(1).broadcast_to([CP, 2, PAIRS, HD]),
                                          ALU.add).then_inc(v_ready, 1)
                if live(2):
                    maximum(6)
                if live(4):
                    k, p, n, q4 = at(4)
                    b = 2 * k + p
                    dve.wait_ge(hi, 2 * b + 2)
                    for q, (dl, dh) in enumerate(((Q_LO, Q_HI), (K_LO, K_HI))):
                        dve.scalar_tensor_tensor(out=parts[p][:, dl, :], in0=C.bank[6][:, q * NTP:(q + 1) * NTP],
                                                 scalar=b_qk[:, q:q + 1], in1=parts[p][:, dh, :].bitcast(F32),
                                                 op0=ALU.add, op1=ALU.subtract).then_inc(lo, 1)
                if live(2):
                    maximum(7)
                if live(-1):
                    k, p, n, q4 = at(-1)
                    b = 2 * k + p
                    dve.wait_ge(projected, b + 1)
                    dve.wait_ge(biased, b + 1)
                    dve.tensor_tensor(hr[q4 % 3][:, :, :], C.bank[7][0:CP, 0:2 * D].rearrange("p (c d) -> p c d", c=2),
                                      hr[q4 % 3][:, :, :], ALU.add).then_inc(summed, 1)
            steps(dve, step)

        @block.scalar
        def _(act):
            act.wait_ge(weights, 160)

            def step(at, live, old):
                def exponential(u):
                    k, p, n, q4 = at(0)
                    b = 2 * k + p
                    c, g = u // PAIRS, u % PAIRS
                    act.wait_ge(s_sum, 8 * b + u + 1)
                    if g == 0 and old(0, 1):
                        act.wait_ge(pv, 2 * b - 1 + c)
                    nk = KROWS[c]
                    act.activation(E[c][0:nk, g, :, :], C.bank[u % 2][0:nk, 0:2 * NTP].rearrange("p (j t) -> p j t", j=2),
                                   ACT.Exp, scale=HD ** -0.5).then_inc(exped, 1)
                if live(3):
                    k, p, n, q4 = at(3)
                    b = 2 * k + p
                    act.wait_ge(lo, 2 * b + 2)
                    if old(3, 2):
                        act.wait_ge(stacked[p], STACK_DMAS * k)
                    places = bounce[p].rearrange("s j d g t -> (j d g) s t")
                    act.dma_start(places[:, 1:5, :], parts[p][:, :, :].bitcast(F32)).then_inc(bounced[p], 16)
                    act.dma_start(places[:, 0:6:5, :], parts[p][:, Q_HI:K_HI + 1:K_HI - Q_HI, :].bitcast(F32))\
                       .then_inc(bounced[p], 16)
                if live(0):
                    for u in range(2):
                        exponential(u)
                if live(4):
                    k, p, n, q4 = at(4)
                    b = 2 * k + p
                    act.wait_ge(xT, b + 1)
                    if old(4, 2):
                        act.wait_ge(v_sum, b - 1)
                    act.activation(yT[p][:, :], C.bank[5][:, 0:NTP], ACT.Identity, scale=ln[:, 0:1], bias=ln[:, 1:2])\
                       .then_inc(y_ready, 1)
                if live(0):
                    exponential(2)
                if live(1):
                    k, p, n, q4 = at(1)
                    b = 2 * k + p
                    act.wait_ge(gT, b + 1)
                    if old(1, 1):
                        ko = k - 1 + p
                        act.wait_ge(guarded[1 - p], 16 * ko + 16)
                    act.activation(gmax[:, :], C.bank[7][0:HEADS, 2 * D:2 * D + NTP], ACT.Copy).then_inc(g_ready, 1)
                if live(0):
                    for u in range(3, 5):
                        exponential(u)
                if live(4):
                    k, p, n, q4 = at(4)
                    b = 2 * k + p
                    act.wait_ge(qk, b + 1)
                    if old(4, 2):
                        act.wait_ge(bounced[p], 32 * k)
                    for q, dh in enumerate((Q_HI, K_HI)):
                        act.activation(parts[p][:, dh, :], C.bank[6][:, q * NTP:(q + 1) * NTP], ACT.Identity,
                                       bias=b_qk[:, q:q + 1]).then_inc(hi, 1)
                if live(0):
                    for u in range(5, 8):
                        exponential(u)
            steps(act, step)

        @block.tensor
        def _(pe):
            pe.wait_ge(weights, 160)
            pe.wait_ge(turned, 4)

            def step(at, live, old):
                def scores(u):
                    k, p, n, q4 = at(0)
                    b = 2 * k + p
                    c, g = u // PAIRS, u % PAIRS
                    nk = KROWS[c]
                    if u == 0:
                        pe.wait_ge(guarded[p], 16 * k + 16)
                    if u >= 2 or old(0, 1):
                        pe.wait_ge(exped, 8 * b + u - 1)
                    for j in range(2):
                        mm = pe.matmul(C.bank[u % 2][0:nk, j * NTP:(j + 1) * NTP],
                                       kst[q4][j][0:GUARD + 2, g, c * CP:c * CP + nk], qst[q4][0:GUARD + 2, g, :],
                                       start=True, stop=True)
                    mm.then_inc(s_sum, 1)

                def scores_for_max(u):
                    k, p, n, q4 = at(2)
                    b = 2 * k + p
                    c, g = u // PAIRS, u % PAIRS
                    if u == 0:
                        pe.wait_ge(stacked[p], STACK_DMAS * k + STACK_DMAS)
                    if u >= 2 or old(2, 1):
                        pe.wait_ge(maxed, 8 * b + u - 1)
                    for j in range(2):
                        mm = pe.matmul(C.bank[2 + u % 2][0:CP, j * NTP:(j + 1) * NTP],
                                       qst[q4][0:GUARD, g, c * CP:(c + 1) * CP], kst[q4][j][0:GUARD, g, :],
                                       start=True, stop=True)
                    mm.then_inc(max_sum, 1)

                def values(d, c, what):
                    k, p, n, q4 = at(d)
                    b = 2 * k + p
                    if what == 0:
                        pe.wait_ge(exped, 8 * b + 4 * c + 4)
                    if c == 0 and what == 0:
                        pe.wait_ge(v_ready, 2 * b + 2)
                        if old(0, 1):
                            pe.wait_ge(o_ready, b)
                    nk = KROWS[c]
                    for j in range(2):
                        for g in range(PAIRS):
                            lhs = vblk[q4][0:nk, c, 2 * g + j, :] if what == 0 else oblk[0:nk, j, :]
                            mm = pe.matmul(C.bank[4][32 * g:32 * g + 32, what * NTP:(what + 1) * NTP], lhs,
                                           E[c][0:nk, g, j, :], start=(c == 0 and what == 0 and j == 0),
                                           stop=(c == 1 and j == 1), skip_group_check=True)
                    if what == 1:
                        mm.then_inc(pv, 1)

                for u in range(8):
                    if live(0):
                        scores(u)
                    if live(2):
                        scores_for_max(u)
                    if u == 0 and live(4):
                        k, p, n, q4 = at(4)
                        b = 2 * k + p
                        pe.wait_ge(normed, 2 * b + 2)
                        if old(4, 1):
                            pe.wait_ge(v_ready, 2 * b)
                        for c in range(2):
                            mm = pe.transpose(C.bank[5][:, c * CP:(c + 1) * CP], xn[p][:, c, :], C.ident[0:CP, 0:CP])
                        mm.then_inc(xT, 1)
                    if u == 1 and live(1):
                        k, p, n, q4 = at(1)
                        b = 2 * k + p
                        pe.wait_ge(maxed, 8 * b + 8)
                        if old(1, 1):
                            pe.wait_ge(g_ready, b)
                        if live(-2):
                            pe.wait_ge(summed, b - 2)
                        for c in range(2):
                            mm = pe.transpose(C.bank[7][0:HEADS, 2 * D + c * CP:2 * D + (c + 1) * CP], negm[p][:, c, :],
                                              C.ident[0:CP, 0:CP])
                        mm.then_inc(gT, 1)
                    if u in (1, 2) and live(-1):
                        values(-1, 1, u - 1)
                    if u == 3 and live(4):
                        k, p, n, q4 = at(4)
                        b = 2 * k + p
                        pe.wait_ge(y_ready, b + 1)
                        if old(4, 1):
                            pe.wait_ge(lo, 2 * b)
                        for q in range(2):
                            mm = pe.matmul(C.bank[6][:, q * NTP:(q + 1) * NTP],
                                           w_turned[:, q, :, :, :].rearrange("p j d g -> p (j d g)"),
                                           yT[p][:, :], start=True, stop=True)
                        mm.then_inc(qk, 1)
                    if u == 4 and live(4):
                        k, p, n, q4 = at(4)
                        for c in range(2):
                            mm = pe.matmul(C.bank[5][0:CP, (2 + c) * D:(3 + c) * D], yT[p][:, c * CP:(c + 1) * CP],
                                           w_qkv[:, 2 * D:3 * D], start=True, stop=True)
                        mm.then_inc(v_sum, 1)
                    if u in (6, 7) and live(0):
                        values(0, 0, u - 6)
                    if u == 6 and live(-1):
                        k, p, n, q4 = at(-1)
                        b = 2 * k + p
                        pe.wait_ge(o_ready, b + 1)
                        if live(1):
                            pe.wait_ge(g_ready, b + 3)
                        for c in range(2):
                            mm = pe.matmul(C.bank[7][0:CP, c * D:(c + 1) * D], oT[p][:, c * CP:(c + 1) * CP],
                                           w_proj[:, :], start=True, stop=True)
                        mm.then_inc(projected, 1)
            steps(pe, step)
    ph.close()


def build_mlp(nc, C, A, hv, layer):
    ph = Phase(nc, "mlp")
    NG = VG + 1
    fc1 = ph.sb("fc1", [D, HID])
    fc2 = ph.sb("fc2", [128, 2, D])
    ln = ph.sb("ln", [D, 2])
    b_fc1 = ph.sb("b_fc1", [128, 2])
    b_fc2 = ph.sb("b_fc2", [128, D])
    ha = [ph.sb(f"ha{p}", [128, 4, D]) for p in range(2)]
    hr = [ph.sb(f"hr{p}", [128, 4, D]) for p in range(2)]
    ho = [ph.sb(f"ho{p}", [128, 4, D]) for p in range(2)]
    xn = [ph.sb(f"xn{p}", [128, 4, D]) for p in range(2)]
    st = ph.sb("st", [128, 4, 6])
    mv = [ph.sb(f"mv{p}", [128, 4, 2]) for p in range(2)]
    ve = ph.sb("ve", [128, 4])
    rs = [ph.sb(f"rs{p}", [128, 4]) for p in range(2)]
    yT = [ph.sb(f"yT{p}", [D, 512]) for p in range(2)]
    mid = [ph.sb(f"mid{p}", [128, 2, 512]) for p in range(2)]
    ha_in = [ph.sem(f"ha_in{p}") for p in range(2)]
    hr_in = [ph.sem(f"hr_in{p}") for p in range(2)]
    stored = [ph.sem(f"stored{p}") for p in range(2)]
    weights, stats, var, eps_added, rstd, normed, xT, y_ready, up, gelued, down, biased, summed = (ph.sem(n) for n in (
        "weights", "stats", "var", "eps_added", "rstd", "normed", "xT", "y_ready", "up", "gelued", "down", "biased",
        "summed"))
    LOOP = (4, 9)

    def steps(eng, step):
        def peeled(i):
            step(lambda d: ((i + d) // 2, (i + d) % 2, i + d), lambda d: 0 <= i + d < NG, lambda d, n: i + d >= n,
                 lambda d: VREM if i + d == NG - 1 else 128)
        for i in range(-2, LOOP[0]):
            peeled(i)
        with eng.Fori(0, (LOOP[1] - LOOP[0] + 1) // 2) as m:
            for r in range(2):
                c0 = LOOP[0] + r
                step(lambda d, c0=c0: (m + (c0 + d) // 2, (c0 + d) % 2, 2 * m + c0 + d), lambda d: True,
                     lambda d, n: True, lambda d: 128)
        for i in range(LOOP[1] + 1, NG + 2):
            peeled(i)

    def group(n, P):
        return hv[bass.ds(n * 512, 4 * P), :].rearrange("(p t) d -> p t d", t=4)

    with nc.Block() as block:
        @block.sync
        def _(sp):
            def of(nm):
                return A["L0_tok_" + nm][bass.ds(layer, 1)]
            sp.dma_start(ha[0][:, :, :], group(0, 128)).then_inc(ha_in[0], 16)
            sp.dma_start(fc1[:, :], of("fc1_w").rearrange("o p n -> (o p) n")).then_inc(weights, 16)
            sp.dma_start(fc2[:, :, :], of("fc2_w").rearrange("o (c p) n -> p (o c) n", c=2)).then_inc(weights, 16)
            for k, nm in enumerate(("ln2_w", "ln2_b")):
                sp.dma_start(ln[:, k:k + 1], of(nm).rearrange("o p -> p o"), allow_slow_non_contiguous=True)\
                  .then_inc(weights, 16)
            sp.dma_start(b_fc1[:, :], of("fc1_b").rearrange("o (c p) -> p (o c)", c=2), allow_slow_non_contiguous=True)\
              .then_inc(weights, 16)
            sp.dma_start(b_fc2[:, :], of("fc2_b").broadcast_to([128, D])).then_inc(weights, 16)

            def step(at, live, old, parts):
                if live(2) and old(2, 1):
                    k, p, n = at(2)
                    if old(2, 2):
                        sp.wait_ge(normed, 4 * (2 * k + p) - 4)
                    sp.dma_start(ha[p][0:parts(2), :, :], group(n, parts(2))).then_inc(ha_in[p], 16)
                if live(0):
                    k, p, n = at(0)
                    if old(0, 2):
                        sp.wait_ge(summed, 2 * k + p - 1)
                    sp.dma_start(hr[p][0:parts(0), :, :], group(n, parts(0))).then_inc(hr_in[p], 16)
                if live(-2):
                    k, p, n = at(-2)
                    sp.wait_ge(summed, 2 * k + p + 1)
                    sp.dma_start(group(n, parts(-2)), ho[p][0:parts(-2), :, :]).then_inc(stored[p], 16)
            steps(sp, step)
            for p in range(2):
                sp.wait_ge(stored[p], 16 * ((NG + 1 - p) // 2))

        @block.gpsimd
        def _(pool):
            pool.wait_ge(weights, 96)

            def step(at, live, old, parts):
                if live(1):
                    k, p, n = at(1)
                    b, P = 2 * k + p, parts(1)
                    pool.wait_ge(var, 4 * b + 4)
                    pool.tensor_tensor(ve[0:P, :], mv[p][0:P, :, 1], C.eps[0:P, 0:4], ALU.add).then_inc(eps_added, 1)
                    pool.wait_ge(eps_added, b + 1)
                    if old(1, 2):
                        pool.wait_ge(normed, 4 * b - 4)
                    pool.tensor_tensor(rs[p][0:P, :], ve[0:P, :], C.half[0:P, 0:4], ALU.pow).then_inc(rstd, 1)
                if live(-1):
                    k, p, n = at(-1)
                    b, P = 2 * k + p, parts(-1)
                    pool.wait_ge(hr_in[p], 16 * k + 16)
                    pool.tensor_tensor(hr[p][0:P, :, :], hr[p][0:P, :, :],
                                       b_fc2[0:P, :].unsqueeze(1).broadcast_to([P, 4, D]), ALU.add).then_inc(biased, 1)
            steps(pool, step)

        @block.vector
        def _(dve):
            def step(at, live, old, parts):
                if live(1):
                    k, p, n = at(1)
                    b, P = 2 * k + p, parts(1)
                    dve.wait_ge(ha_in[p], 16 * k + 16)
                    for t in range(4):
                        dve.bn_stats(st[0:P, t, :], ha[p][0:P, t, :]).then_inc(stats, 1)
                    dve.wait_ge(stats, 5 * b + 4)
                    dve.memset(C.mark[:, :], 0.0).then_inc(stats, 1)
                    for t in range(4):
                        dve.bn_aggr(mv[p][0:P, t, :], st[0:P, t, :]).then_inc(var, 1)
                if live(-2):
                    k, p, n = at(-2)
                    b, P = 2 * k + p, parts(-2)
                    dve.wait_ge(down, b + 1)
                    dve.wait_ge(biased, b + 1)
                    if old(-2, 2):
                        dve.wait_ge(stored[p], 16 * k)
                    dve.tensor_tensor(ho[p][0:P, :, :], C.bank[5 + p][0:P, :].rearrange("p (t d) -> p t d", t=4),
                                      hr[p][0:P, :, :], ALU.add).then_inc(summed, 1)
                if live(1):
                    k, p, n = at(1)
                    b, P = 2 * k + p, parts(1)
                    dve.wait_ge(rstd, b + 1)
                    if old(1, 2):
                        dve.wait_ge(xT, b - 1)
                    for t in range(4):
                        dve.tensor_scalar(xn[p][0:P, t, :], ha[p][0:P, t, :], mv[p][0:P, t, 0:1], rs[p][0:P, t:t + 1],
                                          ALU.subtract, ALU.mult).then_inc(normed, 1)
            steps(dve, step)

        @block.scalar
        def _(act):
            act.wait_ge(weights, 96)

            def step(at, live, old, parts):
                if live(0):
                    k, p, n = at(0)
                    b, P = 2 * k + p, parts(0)
                    for f in range(2):
                        act.wait_ge(up, 2 * b + f + 1)
                        if f == 0 and old(0, 2):
                            act.wait_ge(down, b - 1)
                        act.activation(mid[p][:, f, 0:4 * P], C.bank[1 + 2 * p + f][:, 0:4 * P], ACT.Gelu,
                                       bias=b_fc1[:, f:f + 1]).then_inc(gelued, 1)
                if live(1):
                    k, p, n = at(1)
                    b, P = 2 * k + p, parts(1)
                    act.wait_ge(xT, b + 1)
                    if old(1, 2):
                        act.wait_ge(up, 2 * b - 2)
                    act.activation(yT[p][:, 0:4 * P], C.bank[0][:, 0:4 * P], ACT.Identity, scale=ln[:, 0:1],
                                   bias=ln[:, 1:2]).then_inc(y_ready, 1)
            steps(act, step)

        @block.tensor
        def _(pe):
            pe.wait_ge(weights, 96)

            def step(at, live, old, parts):
                def second_layer(tiles):
                    k, p, n = at(-1)
                    b, P = 2 * k + p, parts(-1)
                    for t in tiles:
                        for f in range(2):
                            mm = pe.matmul(C.bank[5 + p][0:P, t * D:(t + 1) * D], mid[p][:, f, t * P:(t + 1) * P],
                                           fc2[:, f, :], start=(f == 0), stop=(f == 1))
                    return mm
                if live(0):
                    k, p, n = at(0)
                    b, P = 2 * k + p, parts(0)
                    pe.wait_ge(y_ready, b + 1)
                    if old(0, 2):
                        pe.wait_ge(gelued, 2 * b - 2)
                    for f in range(2):
                        pe.matmul(C.bank[1 + 2 * p + f][:, 0:4 * P], fc1[:, f * 128:(f + 1) * 128], yT[p][:, 0:4 * P],
                                  start=True, stop=True).then_inc(up, 1)
                if live(-1):
                    k, p, n = at(-1)
                    b, P = 2 * k + p, parts(-1)
                    pe.wait_ge(gelued, 2 * b + 2)
                    if old(-1, 2):
                        pe.wait_ge(summed, b - 1)
                    second_layer(range(3))
                if live(1):
                    k, p, n = at(1)
                    b, P = 2 * k + p, parts(1)
                    pe.wait_ge(normed, 4 * b + 4)
                    if old(1, 1):
                        pe.wait_ge(y_ready, b)
                    for t in range(4):
                        mm = pe.transpose(C.bank[0][:, t * P:(t + 1) * P], xn[p][0:P, t, :], C.ident[0:P, 0:P])
                    mm.then_inc(xT, 1)
                if live(-1):
                    second_layer([3]).then_inc(down, 1)
            steps(pe, step)
    ph.close()


def build_joint(nc, C, A, hv, txt_dram, hj):
    ph = Phase(nc, "joint")
    WAVES = NB // 2
    LS = 8
    SS = 4
    NC = 3
    ROWS = (*KROWS, T)
    COL = (0, KROWS[0], NT, S)
    wq, wk, wv, w1 = (ph.sb(n, [D, DI]) for n in ("wq", "wk", "wv", "w1"))
    wo, w2 = (ph.sb(n, [128, 4, D]) for n in ("wo", "w2"))
    b1 = ph.sb("b1", [128, 4])
    b2, nw, nb = (ph.sb(n, [128, D]) for n in ("b2", "nw", "nb"))
    wT = ph.sb("wT", [128, 2, 4, D])
    gram = ph.sb("gram", [D, 2, D])
    h, z, a = ([ph.sb(f"{n}{s}", [CP, NC, D]) for s in range(LS)] for n in ("h", "z", "a"))
    st = ph.sb("st", [CP, LS, NC, 6])
    mv = ph.sb("mv", [CP, LS, NC, 2])
    ve = ph.sb("ve", [CP, LS, NC])
    rs = ph.sb("rs", [CP, LS, NC])
    nsq = ph.sb("nsq", [CP, LS, 2 * NC])
    rn = ph.sb("rn", [CP, LS, 2 * NC])
    junk = ph.sb("junk", [CP, 2 * NC, D])
    zT = [ph.sb(f"zT{s}", [D, S]) for s in range(LS)]
    M = ph.sb("M", [D, SS, D])
    prod = ph.sb("prod", [D, SS, DI])
    kv = ph.sb("kv", [128, SS, 4])
    wos = ph.sb("wos", [128, SS, 4, D])
    W = ph.sb("W", [D, SS, D])
    hid = ph.sb("hid", [128, SS, 4, S])
    loaded = [ph.sem(f"loaded{s}") for s in range(LS)]
    stored = [ph.sem(f"stored{s}") for s in range(LS)]
    names = ("weights turnedT turned grammed gram_ready zeroed stats var eps rstd finaled scaled shifted stats2 var2 "
             "eps2 rstd2 z_ready z_turned zT_ready products norms clipped unit zk_ready m_sum m_ready mv_sum prod_ready "
             "kv_sum kv_ready wo_scaled w_sum w_ready a_sum a_ready a_turned aT_ready up relued down biased summed").split()
    sm = {n: ph.sem(n) for n in names}
    FIRST, LAST = 4, 11

    def steps(eng, step):
        def images(k, c, w):
            return [(e, 2 * (c % 4) + e, 2 * (c % 2) + e, 2 * w + e, k) for e in range(2)]

        def peeled(i):
            step(lambda d: images((i + d) // 4, i + d, i + d), lambda d: 0 <= i + d < WAVES, lambda d, n: i + d >= n)
        for i in range(-3, FIRST):
            peeled(i)
        with eng.Fori(0, (LAST - FIRST + 1) // 4) as m:
            for r in range(4):
                c0 = FIRST + r
                step(lambda d, c0=c0: images(m + (c0 + d) // 4, c0 + d, 4 * m + c0 + d), lambda d: True,
                     lambda d, n: True)
        for i in range(LAST + 1, WAVES):
            peeled(i)

    def front(e):
        return C.bank[2 * e], C.bank[2 * e + 1]

    def back(e):
        return C.bank[4 + 2 * e], C.bank[5 + 2 * e]

    with nc.Block() as block:
        @block.sync
        def _(sp):
            for dst, nm in ((wq, "wq"), (wk, "wk"), (wv, "wv"), (w1, "w1")):
                sp.dma_start(dst[:, :], A["L0_attn_" + nm]).then_inc(sm["weights"], 16)
            for dst, nm in ((wo, "wo"), (w2, "w2")):
                sp.dma_start(dst[:, :, :], A["L0_attn_" + nm].rearrange("(c p) d -> p c d", c=4)).then_inc(sm["weights"], 16)
            sp.dma_start(b1[:, :], A["L0_attn_b1"].rearrange("(c p) -> p c", c=4), allow_slow_non_contiguous=True)\
              .then_inc(sm["weights"], 16)
            for dst, nm in ((b2, "L0_attn_b2"), (nw, "L0_tok_norm_w"), (nb, "L0_tok_norm_b")):
                sp.dma_start(dst[:, :], row(A[nm], 128)).then_inc(sm["weights"], 16)
            sp.wait_ge(sm["zeroed"], LS + 1)

            def step(wave, live, old):
                if live(3):
                    for e, s, s2, n, k in wave(3):
                        if old(3, 4):
                            sp.wait_ge(stored[s], 48 * k)
                        sp.dma_start(h[s][:, 0:2, :], image(hv, n)).then_inc(loaded[s], 16)
                        sp.dma_start(h[s][0:T, 2, :], txt_dram[bass.ds(n, 1)].rearrange("o t d -> (o t) d"))\
                          .then_inc(loaded[s], 16)
                if live(0):
                    for e, s, s2, n, k in wave(0):
                        sp.wait_ge(sm["summed"], n * NC + NC)
                        sp.dma_start(hj[bass.ds(n * S, NT - 1), :].rearrange("(p c) d -> p c d", c=2),
                                     h[s][0:CP - 1, 0:2, :]).then_inc(stored[s], 16)
                        sp.dma_start(hj[bass.ds(n * S + NT - 1, 1), :], h[s][CP - 1:CP, 0, :]).then_inc(stored[s], 16)
                        sp.dma_start(hj[bass.ds(n * S + NT, T), :], h[s][0:T, 2, :]).then_inc(stored[s], 16)
            steps(sp, step)
            for s in range(LS):
                sp.wait_ge(stored[s], 48 * NB // LS)

        @block.gpsimd
        def _(pool):
            for s in range(LS):
                pool.memset(h[s][:, :, :], 0.0).then_inc(sm["zeroed"], 1)
            pool.memset(nsq[:, :, :], 1.0).then_inc(sm["zeroed"], 1)
            pool.wait_ge(sm["weights"], 160)

            def step(wave, live, old):
                if live(2):
                    for e, s, s2, n, k in wave(2):
                        pool.wait_ge(sm["var"], 2 * n + 2)
                        pool.tensor_tensor(ve[:, s, 0:2], mv[:, s, 0:2, 1], C.eps[0:CP, 0:2], ALU.add).then_inc(sm["eps"], 1)
                        pool.wait_ge(sm["eps"], n + 1)
                        pool.tensor_tensor(rs[:, s, 0:2], ve[:, s, 0:2], C.half[0:CP, 0:2], ALU.pow).then_inc(sm["rstd"], 1)
                if live(1):
                    for e, s, s2, n, k in wave(1):
                        pool.wait_ge(sm["clipped"], n + 1)
                        pool.tensor_tensor(rn[:, s, :], nsq[:, s, :], C.half[0:CP, 0:2 * NC], ALU.pow).then_inc(sm["unit"], 1)
                if live(2):
                    for e, s, s2, n, k in wave(2):
                        pool.wait_ge(sm["finaled"], 2 * n + 2)
                        pool.tensor_tensor(h[s][:, 0:2, :], h[s][:, 0:2, :],
                                           nw[0:CP, :].unsqueeze(1).broadcast_to([CP, 2, D]), ALU.mult).then_inc(sm["scaled"], 1)
                        pool.wait_ge(sm["scaled"], n + 1)
                        pool.tensor_tensor(h[s][:, 0:2, :], h[s][:, 0:2, :],
                                           nb[0:CP, :].unsqueeze(1).broadcast_to([CP, 2, D]), ALU.add).then_inc(sm["shifted"], 1)
                    for e, s, s2, n, k in wave(2):
                        pool.wait_ge(sm["var2"], NC * n + NC)
                        pool.tensor_tensor(ve[:, s, :], mv[:, s, :, 1], C.eps[0:CP, 0:NC], ALU.add).then_inc(sm["eps2"], 1)
                        pool.wait_ge(sm["eps2"], n + 1)
                        pool.tensor_tensor(rs[:, s, :], ve[:, s, :], C.half[0:CP, 0:NC], ALU.pow).then_inc(sm["rstd2"], 1)
                if live(0):
                    for e, s, s2, n, k in wave(0):
                        pool.wait_ge(sm["a_ready"], NC * n + NC)
                        pool.tensor_tensor(h[s][:, :, :], h[s][:, :, :], a[s][:, :, :], ALU.add).then_inc(sm["biased"], 1)
                        pool.wait_ge(sm["biased"], 2 * n + 1)
                        pool.tensor_tensor(h[s][:, :, :], h[s][:, :, :], b2[0:CP, :].unsqueeze(1).broadcast_to([CP, NC, D]),
                                           ALU.add).then_inc(sm["biased"], 1)
            steps(pool, step)

        @block.vector
        def _(dve):
            dve.wait_ge(sm["weights"], 160)
            for q in range(2):
                dve.wait_ge(sm["turnedT"], q + 1)
                dve.tensor_copy(wT[:, q, :, :], C.bank[q][:, :].rearrange("p (c i) -> p c i", c=4)).then_inc(sm["turned"], 1)
            dve.wait_ge(sm["grammed"], 1)
            dve.tensor_copy(gram[:, :, :], C.bank[2][:, 0:2 * D].rearrange("p (q i) -> p q i", q=2)).then_inc(sm["gram_ready"], 1)

            def step(wave, live, old):
                def norms(e, s, s2, n, k):
                    dve.wait_ge(sm["products"], n + 1)
                    for c in range(NC):
                        r = ROWS[c]
                        for q in range(2):
                            src = front(e)[c // 2][0:r, (c % 2) * 2 * D + q * D:(c % 2) * 2 * D + (q + 1) * D]
                            dve.tensor_tensor_reduce(junk[0:r, 2 * c + q, :], src, z[s][0:r, c, :], 1.0, 0.0, ALU.mult, ALU.add,
                                                     nsq[0:r, s, 2 * c + q:2 * c + q + 1]).then_inc(sm["norms"], 1)
                    dve.wait_ge(sm["norms"], 2 * NC * n + 2 * NC)
                    dve.tensor_scalar(nsq[:, s, :], nsq[:, s, :], 1e-24, None, ALU.max).then_inc(sm["clipped"], 1)
                if live(2):
                    for e, s, s2, n, k in wave(2):
                        dve.wait_ge(loaded[s], 32 * k + 32)
                        for c in range(2):
                            dve.bn_stats(st[:, s, c, :], h[s][:, c, :]).then_inc(sm["stats"], 1)
                        dve.wait_ge(sm["stats"], 3 * n + 2)
                        dve.memset(C.mark[:, :], 0.0).then_inc(sm["stats"], 1)
                        for c in range(2):
                            dve.bn_aggr(mv[:, s, c, :], st[:, s, c, :]).then_inc(sm["var"], 1)
                if live(1):
                    norms(*wave(1)[0])
                if live(0):
                    for e, s, s2, n, k in wave(0):
                        dve.wait_ge(sm["a_sum"], n + 1)
                        for c in range(NC):
                            r = ROWS[c]
                            dve.scalar_tensor_tensor(out=a[s][0:r, c, :], in0=back(e)[0][0:r, c * D:(c + 1) * D],
                                                     scalar=rn[0:r, s, 2 * c:2 * c + 1], in1=z[s][0:r, c, :],
                                                     op0=ALU.mult, op1=ALU.add).then_inc(sm["a_ready"], 1)
                if live(1):
                    norms(*wave(1)[1])
                if live(2):
                    for e, s, s2, n, k in wave(2):
                        dve.wait_ge(sm["rstd"], n + 1)
                        for c in range(2):
                            dve.tensor_scalar(h[s][:, c, :], h[s][:, c, :], mv[:, s, c, 0:1], rs[:, s, c:c + 1],
                                              ALU.subtract, ALU.mult).then_inc(sm["finaled"], 1)
                if live(1):
                    for e, s, s2, n, k in wave(1):
                        dve.wait_ge(sm["unit"], n + 1)
                        for c in range(NC):
                            dve.tensor_scalar(a[s][:, c, :], z[s][:, c, :], rn[:, s, 2 * c + 1:2 * c + 2], None, ALU.mult)\
                               .then_inc(sm["zk_ready"], 1)
                if live(2):
                    for e, s, s2, n, k in wave(2):
                        dve.wait_ge(sm["shifted"], n + 1)
                        for c in range(NC):
                            dve.bn_stats(st[:, s, c, :], h[s][:, c, :]).then_inc(sm["stats2"], 1)
                        dve.wait_ge(sm["stats2"], (NC + 1) * n + NC)
                        dve.memset(C.mark2[:, :], 0.0).then_inc(sm["stats2"], 1)
                        for c in range(NC):
                            dve.bn_aggr(mv[:, s, c, :], st[:, s, c, :]).then_inc(sm["var2"], 1)
                if live(1):
                    for e, s, s2, n, k in wave(1):
                        dve.wait_ge(sm["mv_sum"], n + 1)
                        dve.tensor_tensor(prod[:, s2, :], front(e)[0][:, :], wk[:, :], ALU.mult).then_inc(sm["prod_ready"], 1)
                if live(2):
                    for e, s, s2, n, k in wave(2):
                        dve.wait_ge(sm["rstd2"], n + 1)
                        for c in range(NC):
                            dve.tensor_scalar(z[s][:, c, :], h[s][:, c, :], mv[:, s, c, 0:1], rs[:, s, c:c + 1],
                                              ALU.subtract, ALU.mult).then_inc(sm["z_ready"], 1)
                if live(0):
                    for e, s, s2, n, k in wave(0):
                        dve.wait_ge(sm["down"], n + 1)
                        dve.wait_ge(sm["biased"], 2 * n + 2)
                        for c in range(NC):
                            r = ROWS[c]
                            dve.tensor_tensor(h[s][0:r, c, :], back(e)[0][0:r, c * D:(c + 1) * D], h[s][0:r, c, :],
                                              ALU.add).then_inc(sm["summed"], 1)
            steps(dve, step)

        @block.scalar
        def _(act):
            act.wait_ge(sm["weights"], 160)

            def step(wave, live, old):
                if live(1):
                    for e, s, s2, n, k in wave(1):
                        act.wait_ge(sm["z_turned"], n + 1)
                        act.activation(zT[s][:, :], front(e)[0][:, 0:S], ACT.Copy).then_inc(sm["zT_ready"], 1)
                if live(0):
                    for e, s, s2, n, k in wave(0):
                        act.wait_ge(sm["w_sum"], n + 1)
                        act.activation(W[:, s2, :], back(e)[1][:, 256:256 + D], ACT.Copy).then_inc(sm["w_ready"], 1)
                    for e, s, s2, n, k in wave(0):
                        act.wait_ge(sm["a_turned"], n + 1)
                        act.activation(zT[s][:, :], back(e)[1][:, 0:S], ACT.Copy).then_inc(sm["aT_ready"], 1)
                    for f2 in range(2):
                        for e, s, s2, n, k in wave(0):
                            for f in (2 * f2, 2 * f2 + 1):
                                act.wait_ge(sm["up"], 4 * (n - e) + 4 * f2 + 2 * e + f % 2 + 1)
                                act.activation(hid[:, s2, f, :], back(e)[f % 2][:, 0:S], ACT.Relu, bias=b1[:, f:f + 1])\
                                   .then_inc(sm["relued"], 1)
                if live(1):
                    for e, s, s2, n, k in wave(1):
                        act.wait_ge(sm["m_sum"], n + 1)
                        act.activation(M[:, s2, :], front(e)[1][:, 256:256 + D], ACT.Copy).then_inc(sm["m_ready"], 1)
                    for e, s, s2, n, k in wave(1):
                        act.wait_ge(sm["kv_sum"], n + 1)
                        act.activation(kv[:, s2, :], front(e)[1][:, 0:4], ACT.Copy).then_inc(sm["kv_ready"], 1)
                    for e, s, s2, n, k in wave(1):
                        act.wait_ge(sm["kv_ready"], n + 1)
                        for c in range(4):
                            act.activation(wos[:, s2, c, :], wo[:, c, :], ACT.Copy, scale=kv[:, s2, c:c + 1])\
                               .then_inc(sm["wo_scaled"], 1)
            steps(act, step)

        @block.tensor
        def _(pe):
            pe.wait_ge(sm["weights"], 160)
            for q, w in enumerate((wq, wk)):
                for c in range(4):
                    mm = pe.transpose(C.bank[q][:, c * D:(c + 1) * D], w[:, c * D:(c + 1) * D], C.ident[:, :])
                mm.then_inc(sm["turnedT"], 1)
            pe.wait_ge(sm["turned"], 2)
            for q in range(2):
                for c in range(4):
                    mm = pe.matmul(C.bank[2][:, q * D:(q + 1) * D], wT[:, q, c, :], wT[:, q, c, :],
                                   start=(c == 0), stop=(c == 3))
            mm.then_inc(sm["grammed"], 1)
            pe.wait_ge(sm["gram_ready"], 1)

            def step(wave, live, old):
                def turn(s, src, dst):
                    for c in range(NC):
                        mm = pe.transpose(dst[:, COL[c]:COL[c + 1]], src[0:ROWS[c], c, :], C.ident[0:ROWS[c], 0:ROWS[c]])
                    return mm

                def second_layer(e, s, s2, n, k):
                    pe.wait_ge(sm["relued"], 4 * (n - e) + 4 + 2 * e + 2)
                    for c in range(NC):
                        for f in range(4):
                            mm = pe.matmul(back(e)[0][0:ROWS[c], c * D:(c + 1) * D], hid[:, s2, f, COL[c]:COL[c + 1]],
                                           w2[:, f, :], start=(f == 0), stop=(f == 3))
                    mm.then_inc(sm["down"], 1)
                if live(1):
                    for e, s, s2, n, k in wave(1):
                        pe.wait_ge(sm["z_ready"], NC * n + NC)
                        turn(s, z[s], front(e)[0]).then_inc(sm["z_turned"], 1)
                if live(0):
                    for e, s, s2, n, k in wave(0):
                        pe.wait_ge(sm["wo_scaled"], 4 * n + 4)
                        for c in range(4):
                            mm = pe.matmul(back(e)[1][:, 256:256 + D], wT[:, 0, c, :], wos[:, s2, c, :],
                                           start=(c == 0), stop=(c == 3))
                        mm.then_inc(sm["w_sum"], 1)
                if live(1):
                    for e, s, s2, n, k in wave(1):
                        pe.wait_ge(sm["zT_ready"], n + 1)
                        if old(1, 1):
                            pe.wait_ge(sm["kv_ready"], n - 1)
                        for c in range(NC):
                            mm = pe.matmul(front(e)[c // 2][0:ROWS[c], (c % 2) * 256:(c % 2) * 256 + 256],
                                           zT[s][:, COL[c]:COL[c + 1]], gram[:, :, :].rearrange("p q i -> p (q i)"),
                                           start=True, stop=True)
                        mm.then_inc(sm["products"], 1)
                if live(0):
                    for e, s, s2, n, k in wave(0):
                        pe.wait_ge(sm["w_ready"], n + 1)
                        if old(0, 1):
                            pe.wait_ge(sm["summed"], NC * n - NC)
                        for c in range(NC):
                            mm = pe.matmul(back(e)[0][0:ROWS[c], c * D:(c + 1) * D], zT[s][:, COL[c]:COL[c + 1]],
                                           W[:, s2, :], start=True, stop=True)
                        mm.then_inc(sm["a_sum"], 1)
                    for e, s, s2, n, k in wave(0):
                        pe.wait_ge(sm["a_ready"], NC * n + NC)
                        turn(s, a[s], back(e)[1]).then_inc(sm["a_turned"], 1)
                    for f2 in range(2):
                        for e, s, s2, n, k in wave(0):
                            if f2 == 0:
                                pe.wait_ge(sm["aT_ready"], n + 1)
                            else:
                                pe.wait_ge(sm["relued"], 4 * (n - e) + 2 * e + 2)
                            for f in (2 * f2, 2 * f2 + 1):
                                pe.matmul(back(e)[f % 2][:, 0:S], w1[:, f * 128:(f + 1) * 128], zT[s][:, :],
                                          start=True, stop=True).then_inc(sm["up"], 1)
                if live(1):
                    for e, s, s2, n, k in wave(1):
                        pe.wait_ge(sm["zk_ready"], NC * n + NC)
                        for c in range(NC):
                            mm = pe.matmul(front(e)[1][:, 256:256 + D], a[s][0:ROWS[c], c, :], z[s][0:ROWS[c], c, :],
                                           start=(c == 0), stop=(c == NC - 1))
                        mm.then_inc(sm["m_sum"], 1)
                if live(0):
                    second_layer(*wave(0)[0])
                if live(1):
                    for e, s, s2, n, k in wave(1):
                        pe.wait_ge(sm["m_ready"], n + 1)
                        pe.matmul(front(e)[0][:, :], M[:, s2, :], wv[:, :], start=True, stop=True).then_inc(sm["mv_sum"], 1)
                if live(0):
                    second_layer(*wave(0)[1])
                if live(1):
                    for e, s, s2, n, k in wave(1):
                        pe.wait_ge(sm["prod_ready"], n + 1)
                        for c in range(4):
                            mm = pe.matmul(front(e)[1][:, c:c + 1], prod[:, s2, c * 128:(c + 1) * 128], C.ones[:, 0:1],
                                           start=True, stop=True)
                        mm.then_inc(sm["kv_sum"], 1)
            steps(pe, step)
    ph.close()


def build_experts(nc, C, A, hj, out):
    ph = Phase(nc, "moe")
    NG = JG + 1
    LOOP = (2, 13)
    K2 = 2
    w1 = ph.sb("w1", [D, NE, EF])
    w1s = [ph.sb(f"w1_{part}", [D, NE, EF], F32R) for part in ("hi", "lo")]
    w2 = ph.sb("w2", [128, NE, 2, D])
    b1 = ph.sb("b1", [128, NE, 2])
    b2 = ph.sb("b2", [NE, D])
    wg = ph.sb("wg", [D, NE])
    bg = ph.sb("bg", [128, NE])
    number = ph.sb("number", [128, NE])
    h, xn, acc = ([ph.sb(f"{n}{p}", [128, 4, D]) for p in range(2)] for n in ("h", "xn", "acc"))
    st = ph.sb("st", [128, 4, 6])
    mv = [ph.sb(f"mv{p}", [128, 4, 2]) for p in range(2)]
    ve = ph.sb("ve", [128, 4])
    rs = [ph.sb(f"rs{p}", [128, 4]) for p in range(2)]
    uT = [ph.sb(f"uT{p}", [D, 512]) for p in range(2)]
    us = [[ph.sb(f"u_{part}{p}", [D, 512], F32R) for part in ("hi", "lo")] for p in range(2)]
    logits = ph.sb("logits", [128, 4, NE])
    top = ph.sb("top", [128, 4, 8])
    where = ph.sb("where", [128, 4, 8], U32)
    wheref = ph.sb("wheref", [128, 4, K2])
    diff = ph.sb("diff", [128, 4])
    share = ph.sb("share", [128, 3, 4])
    first = ph.sb("first", [128, 4])
    sel = ph.sb("sel", [128, K2, 4, NE])
    wt = [ph.sb(f"wt{p}", [128, 4, NE]) for p in range(2)]
    wtT = [ph.sb(f"wtT{p}", [NE, 512]) for p in range(2)]
    mid = [ph.sb(f"mid{q}", [128, 2, 512]) for q in range(2)]
    loaded = [ph.sem(f"loaded{p}") for p in range(2)]
    stored = [ph.sem(f"stored{p}") for p in range(2)]
    (weights, numbered, stats, var, eps_added, rstd, normed, xT, u_ready, gated, logits_ready, topped, placed, converted,
     differed, exped, chain, wt_ready, wtT_sum, wtT_ready, up, relued, down, added) = (ph.sem(n) for n in (
        "weights", "numbered", "stats", "var", "eps_added", "rstd", "normed", "xT", "u_ready", "gated", "logits_ready",
        "topped", "placed", "converted", "differed", "exped", "chain", "wt_ready", "wtT_sum", "wtT_ready", "up",
        "relued", "down", "added"))
    CHAIN = 8
    UNITS = NE + 1

    def steps(eng, step):
        def peeled(i):
            step(lambda d: ((i + d) // 2, (i + d) % 2, i + d), lambda d: 0 <= i + d < NG, lambda d, n: i + d >= n,
                 lambda d: JREM if i + d == NG - 1 else 128)
        for i in range(-1, LOOP[0]):
            peeled(i)
        with eng.Fori(0, (LOOP[1] - LOOP[0] + 1) // 2) as m:
            for r in range(2):
                c0 = LOOP[0] + r
                step(lambda d, c0=c0: (m + (c0 + d) // 2, (c0 + d) % 2, 2 * m + c0 + d), lambda d: True,
                     lambda d, n: True, lambda d: 128)
        for i in range(LOOP[1] + 1, NG):
            peeled(i)

    def group(t, n, P):
        return t[bass.ds(n * 512, 4 * P), :].rearrange("(p t) d -> p t d", t=4)
    out_rows = out.rearrange("b s d -> (b s) d")

    w_hi, w_lo, u_hi, u_lo = (ph.sem(n) for n in ("w_hi", "w_lo", "u_hi", "u_lo"))

    with nc.Block() as block:
        @block.sync
        def _(sp):
            sp.dma_start(h[0][:, :, :], group(hj, 0, 128)).then_inc(loaded[0], 16)
            sp.dma_start(wg[:, :], A["L0_ffn_gate_w"]).then_inc(weights, 16)
            sp.dma_start(bg[:, :], row(A["L0_ffn_gate_b"], 128)).then_inc(weights, 16)
            sp.dma_start(w1[:, :, :], A["L0_ffn_w1"].rearrange("e p f -> p e f")).then_inc(weights, 16)
            for c in range(2):
                sp.dma_start(w2[:, :, c, :], A["L0_ffn_w2"][:, c * 128:(c + 1) * 128, :].rearrange("e p d -> p e d"))\
                  .then_inc(weights, 16)
                sp.dma_start(b1[:, :, c], A["L0_ffn_b1"][:, c * 128:(c + 1) * 128].rearrange("e p -> p e"),
                             allow_slow_non_contiguous=True).then_inc(weights, 16)
            sp.dma_start(b2[:, :], A["L0_ffn_b2"]).then_inc(weights, 16)

            def step(at, live, old, parts):
                if live(2):
                    k, p, n = at(2)
                    if old(2, 2):
                        sp.wait_ge(added, UNITS * (2 * k + p) - 2 * UNITS + 1)
                    sp.dma_start(h[p][0:parts(2), :, :], group(hj, n, parts(2))).then_inc(loaded[p], 16)
                if live(0):
                    k, p, n = at(0)
                    sp.wait_ge(added, UNITS * (2 * k + p) + UNITS)
                    sp.dma_start(group(out_rows, n, parts(0)), acc[p][0:parts(0), :, :]).then_inc(stored[p], 16)
            steps(sp, step)
            for p in range(2):
                sp.wait_ge(stored[p], 16 * ((NG + 1 - p) // 2))

        @block.gpsimd
        def _(pool):
            pool.iota(number[:, :], pattern=[[1, NE]], base=0, channel_multiplier=0,
                      allow_small_or_imprecise_dtypes=True).then_inc(numbered, 1)

            def step(at, live, old, parts):
                if live(1):
                    k, p, n = at(1)
                    b, P = 2 * k + p, parts(1)
                    pool.wait_ge(var, 4 * b + 4)
                    pool.tensor_tensor(ve[0:P, :], mv[p][0:P, :, 1], C.eps[0:P, 0:4], ALU.add).then_inc(eps_added, 1)
                    pool.wait_ge(eps_added, b + 1)
                    if old(1, 2):
                        pool.wait_ge(normed, 4 * b - 4)
                    pool.tensor_tensor(rs[p][0:P, :], ve[0:P, :], C.half[0:P, 0:4], ALU.pow).then_inc(rstd, 1)
            steps(pool, step)

        @block.vector
        def _(dve):
            dve.wait_ge(weights, 128)
            dve.wait_ge(numbered, 1)
            dve.wait_ge(w_hi, 1)
            dve.tensor_tensor(w1s[1][:, :, :], w1[:, :, :], w1s[0][:, :, :].bitcast(F32), ALU.subtract).then_inc(w_lo, 1)

            def step(at, live, old, parts):
                def add(u):
                    k, p, n = at(0)
                    b, P = 2 * k + p, parts(0)
                    dve.wait_ge(down, UNITS * b + u + 1)
                    bank = C.bank[6 + u % 2]
                    if u == 0:
                        dve.wait_ge(normed, 4 * b + 4)
                        if old(0, 2):
                            dve.wait_ge(stored[p], 16 * k)
                        dve.tensor_tensor(acc[p][0:P, :, :], bank[0:P, :].rearrange("p (t d) -> p t d", t=4), h[p][0:P, :, :],
                                          ALU.add).then_inc(added, 1)
                        return
                    dve.wait_ge(added, UNITS * b + u)
                    for t in range(4):
                        ins = dve.scalar_tensor_tensor(out=acc[p][0:P, t, :], in0=bank[0:P, t * D:(t + 1) * D],
                                                       scalar=wt[p][0:P, t, u - 1:u], in1=acc[p][0:P, t, :],
                                                       op0=ALU.mult, op1=ALU.add)
                    ins.then_inc(added, 1)
                if live(1):
                    k, p, n = at(1)
                    b, P = 2 * k + p, parts(1)
                    dve.wait_ge(loaded[p], 16 * k + 16)
                    for t in range(4):
                        dve.bn_stats(st[0:P, t, :], h[p][0:P, t, :]).then_inc(stats, 1)
                    dve.wait_ge(stats, 5 * b + 4)
                    dve.memset(C.mark[:, :], 0.0).then_inc(stats, 1)
                    for t in range(4):
                        dve.bn_aggr(mv[p][0:P, t, :], st[0:P, t, :]).then_inc(var, 1)
                if live(0):
                    for u in range(2):
                        add(u)
                if live(1):
                    dve.wait_ge(rstd, b + 1)
                    if old(1, 2):
                        dve.wait_ge(xT, b - 1)
                    for t in range(4):
                        dve.tensor_scalar(xn[p][0:P, t, :], h[p][0:P, t, :], mv[p][0:P, t, 0:1], rs[p][0:P, t:t + 1],
                                          ALU.subtract, ALU.mult).then_inc(normed, 1)
                if live(0):
                    for u in range(2, 5):
                        add(u)
                if live(1):
                    dve.wait_ge(u_hi, b + 1)
                    dve.tensor_tensor(us[p][1][:, 0:4 * P], uT[p][:, 0:4 * P], us[p][0][:, 0:4 * P].bitcast(F32),
                                      ALU.subtract).then_inc(u_lo, 1)
                    dve.wait_ge(gated, b + 1)
                    dve.tensor_tensor(logits[0:P, :, :], C.bank[1][0:P, 0:4 * NE].rearrange("p (t e) -> p t e", t=4),
                                      bg[0:P, :].unsqueeze(1).broadcast_to([P, 4, NE]), ALU.add).then_inc(logits_ready, 1)
                    dve.wait_ge(logits_ready, 2 * b + 1)
                    dve.memset(C.mark3[:, :], 0.0).then_inc(logits_ready, 1)
                    for t in range(4):
                        dve.max(top[0:P, t, :], logits[0:P, t, :]).then_inc(topped, 1)
                    dve.wait_ge(topped, 5 * b + 4)
                    dve.memset(C.mark2[:, :], 0.0).then_inc(topped, 1)
                    for t in range(4):
                        dve.max_index(where[0:P, t, :], top[0:P, t, :], logits[0:P, t, :]).then_inc(placed, 1)
                    if old(1, 1):
                        dve.wait_ge(exped, b)
                    dve.tensor_tensor(diff[0:P, :], top[0:P, :, 1], top[0:P, :, 0], ALU.subtract).then_inc(differed, 1)
                    dve.wait_ge(placed, 4 * b + 4)
                    dve.tensor_copy(wheref[0:P, :, :], where[0:P, :, 0:K2]).then_inc(converted, 1)
                if live(0):
                    add(5)
                if live(1):
                    if old(1, 2):
                        dve.wait_ge(wtT_sum, b - 1)
                    dve.wait_ge(converted, b + 1)
                    for q in range(K2):
                        dve.tensor_tensor(sel[0:P, q, :, :], number[0:P, :].unsqueeze(1).broadcast_to([P, 4, NE]),
                                          wheref[0:P, :, q:q + 1].broadcast_to([P, 4, NE]), ALU.is_equal).then_inc(chain, 1)
                    dve.wait_ge(exped, b + 1)
                    dve.tensor_scalar(share[0:P, 1, :], share[0:P, 0, :], 1.0, None, ALU.add).then_inc(chain, 1)
                    dve.wait_ge(chain, CHAIN * b + 3)
                    dve.reciprocal(first[0:P, :], share[0:P, 1, :]).then_inc(chain, 1)
                    dve.wait_ge(chain, CHAIN * b + 4)
                    dve.tensor_tensor(share[0:P, 2, :], share[0:P, 0, :], first[0:P, :], ALU.mult).then_inc(chain, 1)
                    dve.wait_ge(chain, CHAIN * b + 5)
                    for q, weight in enumerate((first[0:P, :], share[0:P, 2, :])):
                        dve.tensor_tensor(sel[0:P, q, :, :], sel[0:P, q, :, :],
                                          weight.unsqueeze(2).broadcast_to([P, 4, NE]), ALU.mult).then_inc(chain, 1)
                    dve.wait_ge(chain, CHAIN * b + 7)
                    dve.tensor_tensor(wt[p][0:P, :, :], sel[0:P, 0, :, :], sel[0:P, 1, :, :], ALU.add).then_inc(chain, 1)
                if live(0):
                    for u in range(6, UNITS):
                        add(u)
            steps(dve, step)

        @block.scalar
        def _(act):
            act.wait_ge(weights, 128)
            act.activation(w1s[0][:, :, :], w1[:, :, :], ACT.Copy).then_inc(w_hi, 1)

            def step(at, live, old, parts):
                def relu(e):
                    k, p, n = at(0)
                    b, P = 2 * k + p, parts(0)
                    for f in range(2):
                        act.wait_ge(up, 2 * (NE * b + e) + f + 1)
                        if f == 0 and (e >= 2 or old(0, 1)):
                            act.wait_ge(down, UNITS * b + e)
                        act.activation(mid[e % 2][:, f, 0:4 * P], C.bank[2 + 2 * (e % 2) + f][:, 0:4 * P], ACT.Relu,
                                       bias=b1[:, e, f:f + 1]).then_inc(relued, 1)
                if live(0):
                    for e in range(3):
                        relu(e)
                if live(1):
                    k, p, n = at(1)
                    b, P = 2 * k + p, parts(1)
                    act.wait_ge(xT, b + 1)
                    act.activation(uT[p][:, 0:4 * P], C.bank[0][:, 0:4 * P], ACT.Copy).then_inc(u_ready, 1)
                    act.activation(us[p][0][:, 0:4 * P], C.bank[0][:, 0:4 * P], ACT.Copy).then_inc(u_hi, 1)
                if live(0):
                    for e in range(3, 6):
                        relu(e)
                if live(1):
                    act.wait_ge(differed, b + 1)
                    if old(1, 1):
                        act.wait_ge(chain, CHAIN * b)
                    act.activation(share[0:P, 0, :], diff[0:P, :], ACT.Exp).then_inc(exped, 1)
                if live(0):
                    for e in range(6, 8):
                        relu(e)
                if live(1):
                    act.wait_ge(wtT_sum, b + 1)
                    act.activation(wtT[p][:, 0:4 * P], C.bank[0][0:NE, 0:4 * P], ACT.Copy).then_inc(wtT_ready, 1)
            steps(act, step)

        @block.tensor
        def _(pe):
            pe.wait_ge(weights, 128)
            pe.wait_ge(w_lo, 1)

            def step(at, live, old, parts):
                def first_layer(e):
                    k, p, n = at(0)
                    b, P = 2 * k + p, parts(0)
                    if e >= 2 or old(0, 1):
                        pe.wait_ge(relued, 2 * (NE * b + e) - 2)
                    for f in range(2):
                        for m, (wp, xp) in enumerate(((0, 0), (0, 1), (1, 0))):
                            mm = pe.matmul(C.bank[2 + 2 * (e % 2) + f][:, 0:4 * P], w1s[wp][:, e, f * 128:(f + 1) * 128],
                                           us[p][xp][:, 0:4 * P], start=(m == 0), stop=(m == 2))
                        mm.then_inc(up, 1)

                def second_layer(e):
                    k, p, n = at(0)
                    b, P = 2 * k + p, parts(0)
                    u = e + 1
                    pe.wait_ge(relued, 2 * (NE * b + e) + 2)
                    if u >= 2 or old(0, 1):
                        pe.wait_ge(added, UNITS * b + u - 1)
                    for t in range(4):
                        for f in range(2):
                            mm = pe.matmul(C.bank[6 + u % 2][0:P, t * D:(t + 1) * D], mid[e % 2][:, f, t * P:(t + 1) * P],
                                           w2[:, e, f, :], start=(f == 0), stop=(f == 1))
                    mm.then_inc(down, 1)
                if live(0):
                    k, p, n = at(0)
                    b, P = 2 * k + p, parts(0)
                    pe.wait_ge(u_lo, b + 1)
                    first_layer(0)
                    first_layer(1)
                    pe.wait_ge(wtT_ready, b + 1)
                    if old(0, 1):
                        pe.wait_ge(added, UNITS * b)
                    for t in range(4):
                        mm = pe.matmul(C.bank[6][0:P, t * D:(t + 1) * D], wtT[p][:, t * P:(t + 1) * P], b2[:, :],
                                       start=True, stop=True)
                    mm.then_inc(down, 1)
                    second_layer(0)
                    for e in range(1, 3):
                        first_layer(e + 1)
                        second_layer(e)
                if live(1):
                    k, p, n = at(1)
                    b, P = 2 * k + p, parts(1)
                    pe.wait_ge(normed, 4 * b + 4)
                    if old(1, 1):
                        pe.wait_ge(wtT_ready, b)
                    for t in range(4):
                        mm = pe.transpose(C.bank[0][:, t * P:(t + 1) * P], xn[p][0:P, t, :], C.ident[0:P, 0:P])
                    mm.then_inc(xT, 1)
                if live(0):
                    first_layer(4)
                    second_layer(3)
                if live(1):
                    pe.wait_ge(u_ready, b + 1)
                    if old(1, 1):
                        pe.wait_ge(logits_ready, 2 * b)
                    for t in range(4):
                        mm = pe.matmul(C.bank[1][0:P, t * NE:(t + 1) * NE], uT[p][:, t * P:(t + 1) * P], wg[:, :],
                                       start=True, stop=True)
                    mm.then_inc(gated, 1)
                if live(0):
                    for e in range(4, 7):
                        first_layer(e + 1)
                        second_layer(e)
                if live(1):
                    pe.wait_ge(chain, CHAIN * b + 8)
                    for t in range(4):
                        mm = pe.transpose(C.bank[0][0:NE, t * P:(t + 1) * P], wt[p][0:P, t, :], C.ident[0:P, 0:P])
                    mm.then_inc(wtT_sum, 1)
                if live(0):
                    second_layer(7)
            steps(pe, step)
    ph.close()


class Consts:
    pass


def make_consts(nc, ctx):
    C = Consts()
    C.bank = [ctx.enter_context(nc.psum_tensor(f"bank{i}", [128, 512], F32)) for i in range(8)]
    C.ident = ctx.enter_context(nc.sbuf_tensor("ident", [128, 128], F32))
    C.ones = ctx.enter_context(nc.sbuf_tensor("ones", [128, NTP * PAIRS], F32))
    C.zeros = ctx.enter_context(nc.sbuf_tensor("zeros", [1, D], F32))
    C.eps = ctx.enter_context(nc.sbuf_tensor("eps", [128, 8], F32))
    C.mark = ctx.enter_context(nc.sbuf_tensor("mark", [1, 1], F32))
    C.mark2 = ctx.enter_context(nc.sbuf_tensor("mark2", [1, 1], F32))
    C.mark3 = ctx.enter_context(nc.sbuf_tensor("mark3", [1, 1], F32))
    C.half = ctx.enter_context(nc.sbuf_tensor("half", [128, 8], F32))
    return C


def build_program(nc, A, out):
    hv = nc.dram_tensor("hv", (VROWS + 2, D), F32, kind="Internal").ap()
    txt_dram = nc.dram_tensor("txt_dram", (NB, T, D), F32, kind="Internal").ap()
    hj = nc.dram_tensor("hj", (JROWS, D), F32, kind="Internal").ap()
    rows_dram = nc.dram_tensor("rows_dram", (3, NB, T), F32, kind="Internal").ap()
    bounce = [nc.dram_tensor(f"bounce{p}", (6, 2, HD, PAIRS, NTP), F32, kind="Internal").ap() for p in range(2)]
    with ExitStack() as ctx:
        C = make_consts(nc, ctx)
        build_constants(nc, C, hv)
        build_texts(nc, C, A, rows_dram, txt_dram)
        build_patches(nc, C, A, hv)
        with ExitStack() as stacks:
            build_stacks(nc, C, stacks)
            with nc.Fori(0, DEPTH) as layer:
                build_attention(nc, C, A, hv, bounce, layer)
                build_mlp(nc, C, A, hv, layer)
        build_joint(nc, C, A, hv, txt_dram, hj)
        build_experts(nc, C, A, hj, out)


_INS = ["x", "x_txt", "L0_tok_conv_w", "L0_tok_conv_b", "L0_tok_cls_token", "L0_tok_pos_embed", "L0_tok_ln1_w",
        "L0_tok_ln1_b", "L0_tok_qkv_w", "L0_tok_qkv_b", "L0_tok_proj_w", "L0_tok_proj_b", "L0_tok_ln2_w",
        "L0_tok_ln2_b", "L0_tok_fc1_w", "L0_tok_fc1_b", "L0_tok_fc2_w", "L0_tok_fc2_b", "L0_tok_norm_w",
        "L0_tok_norm_b", "L0_txt_p", "L0_attn_wq", "L0_attn_wk", "L0_attn_wv", "L0_attn_wo", "L0_attn_w1",
        "L0_attn_b1", "L0_attn_w2", "L0_attn_b2", "L0_ffn_gate_w", "L0_ffn_gate_b", "L0_ffn_w1", "L0_ffn_b1",
        "L0_ffn_w2", "L0_ffn_b2"]


def kernel(**inputs):
    import numpy as _np
    import concourse.bacc as _bacc
    from concourse import mybir as _mybir
    from concourse.bass_utils import run_bass_kernel_spmd as _run

    nc = _bacc.Bacc("TRN2", target_bir_lowering=False, num_devices=1)
    arrays, A = {}, {}
    for name in _INS:
        a = _np.ascontiguousarray(inputs[name])
        arrays[f"in_{name}_dram"] = a
        A[name] = nc.dram_tensor(f"in_{name}_dram", a.shape, _mybir.dt.from_np(a.dtype), kind="ExternalInput").ap()
    out = nc.dram_tensor("out_0_dram", (NB, S, D), _mybir.dt.float32, kind="ExternalOutput").ap()
    build_program(nc, A, out)
    r = _run(nc, [arrays], core_ids=[0])
    return r.results[0]["out_0_dram"]
```
